# Optimizing a Trainium2 kernel written in Bass

```python
import numpy as np
import jax
import jax.numpy as jnp

def _softmax(x, axis=-1):
    return jax.nn.softmax(x, axis=axis)

def _gelu(x):
    return jax.nn.gelu(x, approximate=True)

def _silu(x):
    return jax.nn.silu(x)

def _sigmoid(x):
    return jax.nn.sigmoid(x)

def _layernorm(x, axis=-1, eps=1e-05):
    m = jnp.mean(x, axis=axis, keepdims=True)
    v = jnp.var(x, axis=axis, keepdims=True)
    return (x - m) / jnp.sqrt(v + eps)

def _scatter_add(tgt, idx, src, axis=0):
    return tgt.at[idx].add(src)

def _segment_sum(src, seg, n):
    return jax.ops.segment_sum(src, seg, n)
kernel_name = 'mk_flamingo_gated_d2_seqx_r8_c54c53'

def setup_inputs(seed: int=0):
    np.random.seed(seed)
    _w = jnp.asarray

    def _rec_inputs():
        import jax
        import jax.numpy as jnp
        _rk = jax.random.key(seed)
        x = -0.0002928 + 1 * jax.random.normal(jax.random.fold_in(_rk, 1), (16, 56, 128), jnp.float32)
        _lenS = 56 - jax.random.randint(jax.random.fold_in(_rk, 7), (16,), 0, max(1, 56 // 4) + 1, jnp.int32)
        _lenS2 = 1500 - jax.random.randint(jax.random.fold_in(_rk, 8), (16,), 0, max(1, 1500 // 4) + 1, jnp.int32)
        _ctx_1024P = jax.random.normal(jax.random.fold_in(_rk, 11), (16, 16, 128), jnp.float32)
        _ctx_1024c = jax.random.dirichlet(jax.random.fold_in(_rk, 511), 0.3 * jnp.ones((16,), jnp.float32), (16, 1500))
        _ctx_1024t = jnp.einsum('bsk,bkd->bsd', _ctx_1024c, _ctx_1024P)
        _ctx_1024t = _ctx_1024t * jax.lax.rsqrt(jnp.mean(jnp.square(_ctx_1024t)) + 1e-12) * 0.953939
        ctx_1024 = -1.39393e-06 + 0.999914 * (_ctx_1024t + 0.3 * jax.random.normal(jax.random.fold_in(_rk, 611), (16, 1500, 128), jnp.float32))
        _validS = jnp.arange(56)[None, :] < _lenS[:, None]
        _validS2 = jnp.arange(1500)[None, :] < _lenS2[:, None]
        _causal = jnp.tril(jnp.ones((56, 56), dtype=bool))
        mask_BxSxS2_ff0 = jnp.where(jnp.ones((16, 56, 1500), dtype=bool), 0.0, -1000000000.0).astype(jnp.float32)
        mask_SxS2_fk0 = jnp.where(jnp.broadcast_to(_validS2[0:1, :], (56, 1500)), -1000000000.0, 0.0).astype(jnp.float32)
        _g = jax.random.normal(jax.random.fold_in(_rk, 9001), (2, 2), jnp.float32)
        _g = jnp.sign(_g) * jnp.maximum(jnp.abs(_g), 1.0) + (_g == 0) * 1.0
        g_xattn = _g[0]
        g_ffn = _g[1]
        return (x, ctx_1024, mask_BxSxS2_ff0, mask_SxS2_fk0, g_xattn, g_ffn)
    x, ctx_1024, mask_BxSxS2_ff0, mask_SxS2_fk0, g_xattn, g_ffn = _rec_inputs()

    def _L0_xattn_setup():
        import jax, jax.numpy as jnp
        import numpy as np
        NUM_HEADS = 16
        DIM_MODEL = 128
        DIM_HEAD = DIM_MODEL // NUM_HEADS
        B, S = (2, 256)

        def _split_heads(x):
            b, s, _ = x.shape
            return x.reshape(b, s, NUM_HEADS, DIM_HEAD).transpose(0, 2, 1, 3)
        key = jax.random.key(seed)
        ks = jax.random.split(key, 6)
        scale = 1.0 / np.sqrt(DIM_MODEL)
        return {'input_Q': jax.random.normal(ks[0], (B, S, DIM_MODEL), jnp.float32), 'input_K': jax.random.normal(ks[1], (B, S, DIM_MODEL), jnp.float32), 'input_V': jax.random.normal(ks[2], (B, S, DIM_MODEL), jnp.float32), 'mask': jnp.zeros((B, S, S), jnp.float32), 'Wq': jax.random.normal(ks[3], (DIM_MODEL, DIM_MODEL), jnp.float32) * scale, 'bq': jnp.zeros((DIM_MODEL,), jnp.float32), 'Wk': jax.random.normal(ks[4], (DIM_MODEL, DIM_MODEL), jnp.float32) * scale, 'bk': jnp.zeros((DIM_MODEL,), jnp.float32), 'Wv': jax.random.normal(ks[5], (DIM_MODEL, DIM_MODEL), jnp.float32) * scale, 'bv': jnp.zeros((DIM_MODEL,), jnp.float32)}
    _L0_xattn_all = _L0_xattn_setup()
    _L0_xattn_in = {k: v for k, v in _L0_xattn_all.items() if k in ('Wq', 'bq', 'Wk', 'bk', 'Wv', 'bv')}
    del _L0_xattn_all

    def _L0_ffn_setup():
        import jax, jax.numpy as jnp
        import numpy as np
        B, S, D, F, E = (4, 256, 128, 512, 8)
        key = jax.random.key(seed)
        ks = jax.random.split(key, 7)
        s1 = 1.0 / np.sqrt(D)
        s2 = 1.0 / np.sqrt(F)
        x = jax.random.normal(ks[0], (B, S, D), dtype=jnp.float32)
        W1 = jax.random.uniform(ks[1], (E, D, F), jnp.float32, -s1, s1)
        b1 = jax.random.uniform(ks[2], (E, F), jnp.float32, -s1, s1)
        W2 = jax.random.uniform(ks[3], (E, F, D), jnp.float32, -s2, s2)
        b2 = jax.random.uniform(ks[4], (E, D), jnp.float32, -s2, s2)
        Wr = jax.random.uniform(ks[5], (D, E), jnp.float32, -s1, s1)
        br = jax.random.uniform(ks[6], (E,), jnp.float32, -s1, s1)
        return {'x': x, 'W1': W1, 'b1': b1, 'W2': W2, 'b2': b2, 'Wr': Wr, 'br': br}
    _L0_ffn_all = _L0_ffn_setup()
    _L0_ffn_in = {k: v for k, v in _L0_ffn_all.items() if k in ('W1', 'b1', 'W2', 'b2', 'Wr', 'br')}
    del _L0_ffn_all

    def _L1_xattn_setup():
        import jax, jax.numpy as jnp
        import numpy as np
        B, S, D, H = (2, 256, 128, 16)
        A = D // H
        NEG = -1000000000.0
        key = jax.random.key(seed)
        ks = jax.random.split(key, 5)
        std = 1.0 / np.sqrt(D)
        query = jax.random.normal(ks[0], (B, S, D), dtype=jnp.float32)
        context = jax.random.normal(ks[1], (B, S, D), dtype=jnp.float32)
        Wq = jax.random.normal(ks[2], (D, D), dtype=jnp.float32) * std
        Wkv = jax.random.normal(ks[3], (2 * D, D), dtype=jnp.float32) * std
        Wout = jax.random.normal(ks[4], (D, D), dtype=jnp.float32) * std
        mask = jnp.where(jnp.tril(jnp.ones((S, S), dtype=bool)), 0.0, NEG).astype(jnp.float32)
        return {'query': query, 'context': context, 'Wq': Wq, 'Wkv': Wkv, 'Wout': Wout, 'mask': mask}
    _L1_xattn_all = _L1_xattn_setup()
    _L1_xattn_in = {k: v for k, v in _L1_xattn_all.items() if k in ('Wq', 'Wkv', 'Wout')}
    del _L1_xattn_all

    def _L1_ffn_setup():
        import jax, jax.numpy as jnp
        import numpy as np
        B, N, D, E, MULT = (4, 256, 128, 8, 4)
        F = D * MULT

        def _top2_gate(xn, Wg):
            logits = jnp.einsum('bnd,ed->bne', xn, Wg)
            probs = jax.nn.softmax(logits, axis=-1)
            top1 = jnp.argmax(probs, axis=-1)
            t1v = jnp.take_along_axis(probs, top1[..., None], axis=-1)[..., 0]
            masked = jnp.where(jax.nn.one_hot(top1, probs.shape[-1], dtype=bool), -jnp.inf, probs)
            top2 = jnp.argmax(masked, axis=-1)
            t2v = jnp.take_along_axis(masked, top2[..., None], axis=-1)[..., 0]
            denom = t1v + t2v + 1e-09
            combine = jnp.stack([t1v / denom, t2v / denom], axis=-1)
            idx = jnp.stack([top1, top2], axis=-1)
            return (combine, idx)
        key = jax.random.key(seed)
        ks = jax.random.split(key, 8)
        s_in = 1.0 / np.sqrt(D)
        s_hid = 1.0 / np.sqrt(F)
        return {'x': jax.random.normal(ks[0], (B, N, D), dtype=jnp.float32), 'gamma': jnp.ones((D,), dtype=jnp.float32), 'beta': jnp.zeros((D,), dtype=jnp.float32), 'Wg': jax.random.normal(ks[1], (E, D), dtype=jnp.float32) * s_in, 'W1': jax.random.normal(ks[2], (E, D, F), dtype=jnp.float32) * s_in, 'b1': jax.random.normal(ks[3], (E, F), dtype=jnp.float32) * 0.01, 'W2': jax.random.normal(ks[4], (E, F, D), dtype=jnp.float32) * s_hid, 'b2': jax.random.normal(ks[5], (E, D), dtype=jnp.float32) * 0.01}
    _L1_ffn_all = _L1_ffn_setup()
    _L1_ffn_in = {k: v for k, v in _L1_ffn_all.items() if k in ('gamma', 'beta', 'Wg', 'W1', 'b1', 'W2', 'b2')}
    del _L1_ffn_all
    return {'x': x, 'ctx_1024': ctx_1024, 'mask_BxSxS2_ff0': mask_BxSxS2_ff0, 'mask_SxS2_fk0': mask_SxS2_fk0, 'g_xattn': g_xattn, 'g_ffn': g_ffn, 'L0_xattn_Wq': _L0_xattn_in['Wq'], 'L0_xattn_bq': _L0_xattn_in['bq'], 'L0_xattn_Wk': _L0_xattn_in['Wk'], 'L0_xattn_bk': _L0_xattn_in['bk'], 'L0_xattn_Wv': _L0_xattn_in['Wv'], 'L0_xattn_bv': _L0_xattn_in['bv'], 'L0_ffn_W1': _L0_ffn_in['W1'], 'L0_ffn_b1': _L0_ffn_in['b1'], 'L0_ffn_W2': _L0_ffn_in['W2'], 'L0_ffn_b2': _L0_ffn_in['b2'], 'L0_ffn_Wr': _L0_ffn_in['Wr'], 'L0_ffn_br': _L0_ffn_in['br'], 'L1_xattn_Wq': _L1_xattn_in['Wq'], 'L1_xattn_Wkv': _L1_xattn_in['Wkv'], 'L1_xattn_Wout': _L1_xattn_in['Wout'], 'L1_ffn_gamma': _L1_ffn_in['gamma'], 'L1_ffn_beta': _L1_ffn_in['beta'], 'L1_ffn_Wg': _L1_ffn_in['Wg'], 'L1_ffn_W1': _L1_ffn_in['W1'], 'L1_ffn_b1': _L1_ffn_in['b1'], 'L1_ffn_W2': _L1_ffn_in['W2'], 'L1_ffn_b2': _L1_ffn_in['b2']}

def reference(x, ctx_1024, mask_BxSxS2_ff0, mask_SxS2_fk0, g_xattn, g_ffn, L0_xattn_Wq, L0_xattn_bq, L0_xattn_Wk, L0_xattn_bk, L0_xattn_Wv, L0_xattn_bv, L0_ffn_W1, L0_ffn_b1, L0_ffn_W2, L0_ffn_b2, L0_ffn_Wr, L0_ffn_br, L1_xattn_Wq, L1_xattn_Wkv, L1_xattn_Wout, L1_ffn_gamma, L1_ffn_beta, L1_ffn_Wg, L1_ffn_W1, L1_ffn_b1, L1_ffn_W2, L1_ffn_b2):
    import jax
    import jax.numpy as jnp

    def _L0_xattn_ref(input_Q, input_K, input_V, mask, Wq, bq, Wk, bk, Wv, bv):
        import jax, jax.numpy as jnp
        import numpy as np
        NUM_HEADS = 16
        DIM_MODEL = 128
        DIM_HEAD = DIM_MODEL // NUM_HEADS
        B, S = (2, 256)

        def _split_heads(x):
            b, s, _ = x.shape
            return x.reshape(b, s, NUM_HEADS, DIM_HEAD).transpose(0, 2, 1, 3)
        Q = _split_heads(input_Q @ Wq.T + bq)
        K = _split_heads(input_K @ Wk.T + bk)
        V = _split_heads(input_V @ Wv.T + bv)
        scores = -jnp.einsum('bhqd,bhkd->bhqk', Q, K) / np.sqrt(DIM_HEAD)
        scores = scores + mask[:, None, :, :]
        attn = jax.nn.softmax(scores, axis=-1)
        ctx = jnp.einsum('bhqk,bhkd->bhqd', attn, V)
        b = input_V.shape[0]
        return ctx.transpose(0, 2, 1, 3).reshape(b, -1, NUM_HEADS * DIM_HEAD)

    def _L0_ffn_ref(x, W1, b1, W2, b2, Wr, br):
        import jax, jax.numpy as jnp
        import numpy as np
        B, S, D, F, E = (4, 256, 128, 512, 8)
        b, s, d = x.shape
        e = Wr.shape[1]
        logits = x @ Wr + br
        idx = jnp.argmax(logits, axis=-1)
        probs = jax.nn.softmax(logits, axis=-1)
        gates = jnp.take_along_axis(probs, idx[..., None], axis=-1)[..., 0]
        xf = x.reshape(-1, d)
        idxf = idx.reshape(-1)
        gf = gates.reshape(-1)
        out = jnp.zeros_like(xf)
        for ei in range(e):
            h = jax.nn.gelu(xf @ W1[ei] + b1[ei], approximate=False)
            y = h @ W2[ei] + b2[ei]
            mask = (idxf == ei).astype(xf.dtype)
            out = out + y * (gf * mask)[:, None]
        return out.reshape(b, s, d)

    def _L1_xattn_ref(query, context, Wq, Wkv, Wout, mask):
        import jax, jax.numpy as jnp
        import numpy as np
        B, S, D, H = (2, 256, 128, 16)
        A = D // H
        NEG = -1000000000.0
        b, q_len, d = query.shape
        c_len = context.shape[1]
        h, a = (H, A)
        scale = 1.0 / np.sqrt(d)
        q = query @ Wq.T
        kv = context @ Wkv.T
        k, v = jnp.split(kv, 2, axis=-1)
        q = q.reshape(b, q_len, h, a)
        k = k.reshape(b, c_len, h, a)
        v = v.reshape(b, c_len, h, a)
        scores = jnp.einsum('bqha,bkha->bqkh', q, k)
        scores = scores + mask[None, :, :, None]
        attn = jax.nn.softmax(scores * scale, axis=2)
        out = jnp.einsum('bqkh,bkha->bqha', attn, v).reshape(b, q_len, d)
        return out @ Wout.T

    def _L1_ffn_ref(x, gamma, beta, Wg, W1, b1, W2, b2):
        import jax, jax.numpy as jnp
        import numpy as np
        B, N, D, E, MULT = (4, 256, 128, 8, 4)
        F = D * MULT

        def _top2_gate(xn, Wg):
            logits = jnp.einsum('bnd,ed->bne', xn, Wg)
            probs = jax.nn.softmax(logits, axis=-1)
            top1 = jnp.argmax(probs, axis=-1)
            t1v = jnp.take_along_axis(probs, top1[..., None], axis=-1)[..., 0]
            masked = jnp.where(jax.nn.one_hot(top1, probs.shape[-1], dtype=bool), -jnp.inf, probs)
            top2 = jnp.argmax(masked, axis=-1)
            t2v = jnp.take_along_axis(masked, top2[..., None], axis=-1)[..., 0]
            denom = t1v + t2v + 1e-09
            combine = jnp.stack([t1v / denom, t2v / denom], axis=-1)
            idx = jnp.stack([top1, top2], axis=-1)
            return (combine, idx)
        residual = x
        mu = jnp.mean(x, axis=-1, keepdims=True)
        var = jnp.mean(jnp.square(x - mu), axis=-1, keepdims=True)
        xn = (x - mu) / jnp.sqrt(var + 1e-05) * gamma + beta
        combine, idx = _top2_gate(xn, Wg)
        n_expert = Wg.shape[0]
        onehot = jax.nn.one_hot(idx, n_expert, dtype=x.dtype)
        gates = jnp.einsum('bns,bnse->ebn', combine, onehot)

        def body(acc, params):
            w1, b1e, w2, b2e, g = params
            h = jax.nn.gelu(jnp.einsum('bnd,df->bnf', xn, w1) + b1e, approximate=True)
            y = jnp.einsum('bnf,fd->bnd', h, w2) + b2e
            return (acc + g[..., None] * y, None)
        out, _ = jax.lax.scan(body, jnp.zeros_like(x), (W1, b1, W2, b2, gates))
        return residual + out
    x = x + jnp.tanh(g_xattn[0]) * _L0_xattn_ref(_layernorm(x, axis=-1), ctx_1024, ctx_1024, mask_BxSxS2_ff0, L0_xattn_Wq, L0_xattn_bq, L0_xattn_Wk, L0_xattn_bk, L0_xattn_Wv, L0_xattn_bv)
    x = x + jnp.tanh(g_ffn[0]) * _L0_ffn_ref(_layernorm(x, axis=-1), L0_ffn_W1, L0_ffn_b1, L0_ffn_W2, L0_ffn_b2, L0_ffn_Wr, L0_ffn_br)
    x = x + jnp.tanh(g_xattn[1]) * _L1_xattn_ref(_layernorm(x, axis=-1), ctx_1024, L1_xattn_Wq, L1_xattn_Wkv, L1_xattn_Wout, mask_SxS2_fk0)
    x = x + jnp.tanh(g_ffn[1]) * _L1_ffn_ref(_layernorm(x, axis=-1), L1_ffn_gamma, L1_ffn_beta, L1_ffn_Wg, L1_ffn_W1, L1_ffn_b1, L1_ffn_W2, L1_ffn_b2)
    return x

_drawn_inputs = setup_inputs


def setup_inputs(seed=0):
    import zlib

    import numpy as np

    out = dict(_drawn_inputs(seed))
    spreads = {'g_ffn': (-1.0, 0.2),
     'L0_xattn_bq': (0.0, 0.1),
     'L0_xattn_bk': (0.0, 0.8),
     'L0_xattn_bv': (0.0, 0.1),
     'L1_ffn_gamma': (1.0, 0.2),
     'L1_ffn_beta': (0.0, 0.1)}
    factors = {'L0_ffn_br': 2.68, 'L1_ffn_b1': 7.444, 'L1_ffn_b2': 4.99}
    for name, (base, spread) in spreads.items():
        noise = np.random.default_rng([zlib.crc32(name.encode()), seed]).standard_normal(out[name].shape)
        drawn = base * np.exp(spread * noise) if base else spread * noise
        out[name] = jnp.asarray(drawn.astype(out[name].dtype))
    for name, factor in factors.items():
        out[name] = (out[name] * factor).astype(out[name].dtype)
    return out
```

```python
from contextlib import ExitStack

import concourse.bass as bass
from concourse import mybir

ALU = mybir.AluOpType
ACT = mybir.ActivationFunctionType
AX = mybir.AxisListType.X
RMAX = bass.bass_isa.ReduceOp.max
F32 = mybir.dt.float32
BF16 = mybir.dt.bfloat16
I32 = mybir.dt.int32

P = 128
B, S, D = 16, 56, 128
S2 = 1500
H, A = 16, 8
PAIRS = H // 2
CH, CK = 12, 125
TH, TK = 3, 500
HQ = H * S
T, TR = 8, 112
NTOK = B * S
HALF = NTOK // 2
E, F = 8, 512
FC = F // P
EPS = 1e-5
TERMS = 6
K_PART = (0, 0, 0, 1, 1, 2)
Q_PART = (0, 1, 2, 0, 1, 0)
SHIFT_ROW = TERMS * 2 * A
MASK_ROW = SHIFT_ROW + 3
ROWS = MASK_ROW + 3


def build(nc, x, ctx_t, mask0, mask1, gates_in, ident_in, tie_in,
          wq0, bq0, wk0, bk0, wv0, bv0, wq1, wk1, wv1, wo1,
          fw1_0, fb1_0, fw2_0, fb2_0, wr0, br0,
          gamma, beta, fw1_1, fb1_1, fw2_1, fb2_1, wr1, out):
    es = ExitStack()
    with es:
        def sb(name, shape, dt=F32):
            return es.enter_context(nc.sbuf_tensor(name, shape, dt))

        made = []

        def sem(name):
            made.append(nc.alloc_semaphore(name=name))
            return made[-1]

        mask_scratch = nc.dram_tensor("mask_scratch", (B + 1, 3, S2), BF16, kind="Internal").ap()
        gate_scratch = nc.dram_tensor("gate_scratch", (2, E, NTOK), F32, kind="Internal").ap()

        shared = sb("shared", [P, 2 * PAIRS * S2 // 2])
        k_stack = shared[:, :].bitcast(BF16).rearrange("p (b h k) -> p b h k", b=2, h=PAIRS)
        k_part = [sb(n, [P, S2], BF16) for n in ("k_hi", "k_mid", "k_lo")]
        k_rest = sb("k_rest", [P, TH, TK])
        ctx_sb = sb("ctx_sb", [P, 2, S2])
        v_sb = sb("v_sb", [P, 2, CH, 4, 34])
        e_sb = sb("e_sb", [P, 3, HQ])
        q_all = sb("q_all", [SHIFT_ROW, PAIRS, B, 2 * S], BF16)
        q_cur = sb("q_cur", [ROWS, 2, PAIRS, 2 * S], BF16)
        q_part = [sb(n, [P, NTOK], BF16) for n in ("q_hi", "q_mid", "q_lo")]
        u_all = sb("u_all", [P, 4, B, S])
        q_f = u_all[:, 0, :, :].rearrange("p b q -> p (b q)")
        q_rest = u_all[:, 1, :, :].rearrange("p b q -> p (b q)")
        mask_sb = sb("mask_sb", [S, 2, S2])
        mask_cmp = sb("mask_cmp", [2 * S, S2])
        mask_row = sb("mask_row", [2 * S, S2])
        differ = sb("differ", [2 * S, 4])
        flag = sb("flag", [1, 1], I32)
        ident_q = sb("ident_q", [S, PAIRS, S])
        mx = sb("mx", [TR, TH, PAIRS])
        m_fold = sb("m_fold", [TR, PAIRS])
        m_rest = sb("m_rest", [TR, PAIRS])
        m_part = sb("m_part", [TR, PAIRS, 3], BF16)
        x_sb = sb("x_sb", [TR, T, D])
        xn = sb("xn", [TR, T, D])
        xt = sb("xt", [P, NTOK])
        stats = sb("stats", [TR, T, 6])
        mv = sb("mv", [TR, T, 2])
        rstd = sb("rstd", [TR, T])
        minus_half = sb("minus_half", [TR, T])
        rec = sb("rec", [TR, T, 4, 4])
        ident = sb("ident", [P, P])
        ident_b = sb("ident_b", [P, P], BF16)
        tie = sb("tie", [TR, E])
        tg = sb("tg", [P, 4])
        w_q = [sb(f"w_q{i}", [P, D]) for i in range(2)]
        w_k = [sb(f"w_k{i}", [P, D]) for i in range(2)]
        w_v = [sb(f"w_v{i}", [P, D]) for i in range(2)]
        w_o = sb("w_o", [P, D])
        w_r = [sb(f"w_r{i}", [P, E]) for i in range(2)]
        b_q = sb("b_q", [P, 1])
        b_k = sb("b_k", [P, 2])
        b_v = sb("b_v", [TR, D])
        b_r = sb("b_r", [TR, E])
        gam = sb("gam", [TR, D])
        bet = sb("bet", [TR, D])
        lg = sb("lg", [TR, 8, T, E])
        ls = sb("ls", [TR, 8, T])
        g_t = sb("g_t", [E, NTOK])
        b1_sb = sb("b1_sb", [P, 2, FC])
        fb2 = [sb(f"fb2{i}", [E, D]) for i in range(2)]

        ff = shared[:, :]
        w1_sb = ff[:, 0:1024].rearrange("p (b f) -> p b f", b=2)
        w2_sb = ff[:, 1024:2048].rearrange("p (b c d) -> p b c d", b=2, c=FC)
        gate_b = ff[:, 2048:2048 + 2 * NTOK].rearrange("p (b n) -> p b n", b=2)
        h_sb = ff[:, 4096:4096 + 4 * HALF].rearrange("p (b n) -> p b n", b=4)
        hg_sb = ff[:, 6144:6144 + 4 * HALF].rearrange("p (b n) -> p b n", b=4)
        resid = ff[0:TR, 10752:10752 + T * D].rearrange("r (t d) -> r t d", t=T)
        y_t = ff[:, 8192:8192 + NTOK]
        m_row = ff[0:B + 1, 9216:9216 + S2]
        mr_part = [k_part[i][0:B + 1, :] for i in range(3)]

        bank = [es.enter_context(nc.psum_tensor(f"bank{i}", [P, 512], F32)) for i in range(4)]
        wide = [es.enter_context(nc.psum_tensor(f"wide{i}", [P, 2, 512], F32)) for i in range(2)]
        acc, aux = bank[2], bank[3]
        post = bank

        state = {}

        w_in = sem("w_in")
        n_w = [0]
        mr_in = sem("mr_in")
        mask_out = sem("mask_out")
        x_in = sem("x_in")
        const = sem("const")
        tg_in = sem("tg_in")
        with nc.Block() as block:
            @block.sync
            def _(sp):
                sp.dma_start(x_sb[:, :, :], x.rearrange("(t r) d -> r t d", r=TR)).then_inc(x_in, 16)
                sp.dma_start(ident[:, :], ident_in).then_inc(x_in, 16)
                sp.dma_start(m_row[0:B, :], mask0[:, 0, :]).then_inc(mr_in, 16)
                sp.dma_start(m_row[B:B + 1, :], mask1[0:1, :]).then_inc(mr_in, 16)
                for dst, src in ((w_q[0], wq0), (w_k[0], wk0), (w_v[0], wv0), (b_q, bq0), (b_k, bk0),
                                 (w_q[1], wq1), (w_k[1], wk1), (w_v[1], wv1), (w_o, wo1),
                                 (w_r[0], wr0), (w_r[1], wr1),
                                 (fb2[0], fb2_0), (fb2[1], fb2_1)):
                    sp.dma_start(dst[:, :], src).then_inc(w_in, 16)
                    n_w[0] += 16
            @block.scalar
            def _(act):
                act.dma_start(tg[:, :], gates_in.broadcast_to([P, 4])).then_inc(tg_in, 16)
                for dst, src, w in ((b_v, bv0, D), (b_r, br0, E), (gam, gamma, D), (bet, beta, D),
                                    (tie, tie_in, E)):
                    act.dma_start(dst[:, :], src.broadcast_to([TR, w])).then_inc(w_in, 16)
                    n_w[0] += 16
                act.wait_ge(tg_in, 16)
                nc.scalar.activation(tg[:, :], tg[:, :], ACT.Tanh).then_inc(const, 1)
            @block.vector
            def _(dve):
                dve.wait_ge(x_in, 32)
                nc.vector.tensor_copy(ident_b[:, :], ident[:, :]).then_inc(const, 1)
                nc.vector.tensor_copy(ident_q[:, :, :], ident[0:S, None, 0:S].broadcast_to([S, PAIRS, S]))\
                    .then_inc(const, 1)
                nc.vector.memset(q_all[:, :, :, :].rearrange("r p b n -> r (p b n)").bitcast(F32), 0.0)\
                    .then_inc(const, 1)
                nc.vector.memset(q_cur[SHIFT_ROW:ROWS, :, :, :], 1.0).then_inc(const, 1)
                nc.vector.memset(differ[:, :], 0.0).then_inc(const, 1)
                nc.vector.memset(v_sb[:, :, :, :, 0:1], 1.0).then_inc(const, 1)
                nc.vector.memset(v_sb[:, :, :, :, 33:34], 1.0).then_inc(const, 1)
                nc.vector.memset(minus_half[:, :], -0.5).then_inc(const, 1)
                split = sem("split")
                rest = ctx_sb[0:B + 1, 0, :]
                dve.wait_ge(mr_in, 32)
                nc.vector.tensor_copy(mr_part[0], m_row).then_inc(split, 1)
                dve.wait_ge(split, 1)
                nc.vector.tensor_tensor(rest, m_row, mr_part[0], ALU.subtract).then_inc(split, 1)
                dve.wait_ge(split, 2)
                nc.vector.tensor_copy(mr_part[1], rest).then_inc(split, 1)
                dve.wait_ge(split, 3)
                nc.vector.tensor_tensor(mr_part[2], rest, mr_part[1], ALU.subtract).then_inc(split, 1)
                state["split"] = split
            @block.gpsimd
            def _(pool):
                pool.wait_ge(state["split"], 4)
                for i in range(3):
                    pool.dma_start(mask_scratch[:, i, :], mr_part[i]).then_inc(mask_out, 16)
                pool.wait_ge(mask_out, 48)
        CONST = 9
        n_w = n_w[0]

        def norm(tag, block, src, dst, first, affine=False):
            st, ag, rs, nm, tp, ev, af = (sem(f"{tag}_{n}") for n in ("stat", "aggr", "rstd", "norm", "tp", "ev", "aff"))
            return st, ag, rs, nm, tp, ev, af

        def norm_vector(dve, q, src, dst, affine):
            st, ag, rs, nm, tp, ev, af = q
            for t in range(T):
                nc.vector.bn_stats(stats[:, t, :], src[:, t, :]).then_inc(st, 1)
            for t in range(T):
                dve.wait_ge(st, t + 1)
                nc.vector.bn_aggr(mv[:, t, :], stats[:, t, :]).then_inc(ag, 1)
            dve.wait_ge(rs, 2)
            for t in range(T):
                nc.vector.tensor_scalar(dst[:, t, :], src[:, t, :], mv[:, t, 0:1], rstd[:, t:t + 1],
                                        ALU.subtract, ALU.mult).then_inc(nm, 1)
            if affine:
                dve.wait_ge(nm, T)
                nc.vector.tensor_tensor(dst[:, :, :], dst[:, :, :], gam[:, None, :].broadcast_to([TR, T, D]),
                                        ALU.mult).then_inc(af, 1)
                dve.wait_ge(af, 1)
                nc.vector.tensor_tensor(dst[:, :, :], dst[:, :, :], bet[:, None, :].broadcast_to([TR, T, D]),
                                        ALU.add).then_inc(af, 1)

        def norm_pool(pool, q):
            st, ag, rs, nm, tp, ev, af = q
            pool.wait_ge(ag, T)
            nc.gpsimd.tensor_scalar(rstd[:, :], mv[:, :, 1], EPS, None, ALU.add).then_inc(rs, 1)
            pool.wait_ge(rs, 1)
            nc.gpsimd.tensor_tensor(rstd[:, :], rstd[:, :], minus_half[:, :], ALU.pow).then_inc(rs, 1)

        def transpose_tensor(pe, q, src, affine):
            st, ag, rs, nm, tp, ev, af = q
            if affine:
                pe.wait_ge(af, 2)
            for t in range(T):
                if not affine:
                    pe.wait_ge(nm, t + 1)
                dst = wide[0][:, t // 4, TR * (t % 4):TR * (t % 4) + TR]
                nc.tensor.transpose(dst, src[:, t, :], ident[0:TR, 0:TR]).then_inc(tp, 1)

        def transpose_copy(act, q):
            st, ag, rs, nm, tp, ev, af = q
            for i in range(2):
                act.wait_ge(tp, 4 * i + 4)
                nc.scalar.copy(xt[:, HALF * i:HALF * i + HALF], wide[0][:, i, 0:HALF]).then_inc(ev, 1)

        def attention(L):
            s = {n: sem(f"a{L}_{n}") for n in (
                "qp", "qs", "qr", "qm", "ql", "qd", "qd0", "kp", "khi", "kres", "kmid", "klo",
                "ctx0", "ctx1", "st0", "st1", "st2", "mk", "mk0", "mk1", "ci", "cs", "cr", "ca", "cf", "fl", "vp", "vc", "qc", "p1", "mxd", "fold", "shi", "srs", "smid", "slo",
                "ones", "mt", "mrow", "sc", "ex", "pv", "uc", "ut", "rc", "o", "xo", "ot", "otc", "wo", "xd")}
            q = norm(f"n{L}", None, x_sb, xn, True)
            scale_q = -1.0 / A ** 0.5 if L == 0 else 1.0
            scale_e = 1.0 if L == 0 else 1.0 / D ** 0.5

            NST = TERMS + (1 if L == 0 else 0)

            def wait_mask(pe, b, r, par):
                pe.wait_ge(s[f"mk{par}"], 16 * r + 16 if L == 0 else 16)

            def k_proj(pe, b, r, par, th, free):
                if th == 0:
                    pe.wait_ge(s[f"ctx{par}"], 16 * r + 16)
                if free is not None:
                    pe.wait_ge(*free)
                nc.tensor.matmul(aux[:, 0:TK], w_k[L][:, :], ctx_sb[:, par, TK * th:TK * th + TK],
                                 start=True, stop=True).then_inc(s["kp"], 1)

            def v_proj(pe, b, par, f, free):
                if free is not None:
                    pe.wait_ge(*free)
                for c in range(4):
                    k0 = CK * (4 * f + c)
                    i = nc.tensor.matmul(aux[0:CK, P * c:P * c + P], ctx_sb[:, par, k0:k0 + CK], w_v[L][:, :],
                                         start=True, stop=True)
                i.then_inc(s["vp"], 1)

            def max_scores(pe, b, r, par, n, masked):
                th, p = n // PAIRS, n % PAIRS
                if n == 0:
                    pe.wait_ge(s["qc"], 2 * b + 2)
                if p == 0:
                    pe.wait_ge(s[f"st{th}"], 16 * NST * (b + 1))
                if not (isinstance(b, int) and b == 0 and n < 2):
                    pe.wait_ge(s["mxd"], 24 * b + n - 1)
                cols = slice(TK * th, TK * th + TK)
                rows = MASK_ROW if masked else ROWS
                i = nc.tensor.matmul(bank[n % 2][0:TR, 0:TK], q_cur[0:rows, par, p, :],
                                     k_stack[0:rows, par, p, cols], start=True, stop=not masked)
                if masked:
                    if n == 0:
                        wait_mask(pe, b, r, par)
                    i = nc.tensor.matmul(bank[n % 2][0:TR, 0:TK],
                                         ident_q[:, 0:2, :].rearrange("k h q -> k (h q)"),
                                         mask_sb[:, par, cols], start=False, stop=True)
                i.then_inc(s["p1"], 1)

            def max_rows(pe, b, free):
                pe.wait_ge(s["slo"], b + 1)
                pe.wait_ge(*free)
                rows = aux[SHIFT_ROW:SHIFT_ROW + 3, 0:448].bitcast(BF16)
                for p in range(PAIRS):
                    i = nc.tensor.transpose(rows[:, TR * p:TR * p + TR], m_part[:, p, :], ident_b[0:TR, 0:TR])
                i.then_inc(s["mt"], 1)

            def scores(pe, b, r, par, c, half, masked):
                if c == 0 and half == 0:
                    pe.wait_ge(s["mrow"], b + 1)
                if half == 0 and not (isinstance(b, int) and b == 0 and c < 2):
                    pe.wait_ge(s["ex"], CH * b + c - 1)
                if masked and c == 0 and half == 0:
                    wait_mask(pe, b, r, par)
                rows = MASK_ROW if masked else ROWS
                for n in range(4):
                    p = 4 * half + n
                    i = nc.tensor.matmul(wide[c % 2][0:CK, half, TR * n:TR * n + TR],
                                         k_stack[0:rows, par, p, CK * c:CK * c + CK], q_cur[0:rows, par, p, :],
                                         start=(n == 0), stop=(n == 3 and not masked), skip_group_check=True)
                if masked:
                    i = nc.tensor.matmul(wide[c % 2][0:CK, half, 0:4 * TR], mask_sb[:, par, CK * c:CK * c + CK],
                                         ident_q[:, :, :].rearrange("k h q -> k (h q)"),
                                         start=False, stop=True, skip_group_check=True)
                if half:
                    i.then_inc(s["sc"], 1)

            def weigh(pe, b, par, c, part):
                if part == 0:
                    pe.wait_ge(s["ex"], CH * b + c + 1)
                    if c == 0:
                        pe.wait_ge(s["vc"], 3 * b + 3)
                        if not (isinstance(b, int) and b == 0):
                            pe.wait_ge(s["uc"], b)
                    for j in range(4):
                        nc.tensor.matmul(acc[32 * j:32 * j + 32, 0:3 * S], v_sb[0:CK, par, c, j, 0:32],
                                         e_sb[0:CK, c % 3, 4 * S * j:4 * S * j + 3 * S],
                                         start=(c == 0), stop=(c == CH - 1), skip_group_check=True)
                else:
                    for j in range(4):
                        i = nc.tensor.matmul(acc[32 * j:32 * j + 32, 3 * S:4 * S], v_sb[0:CK, par, c, j, 2:34],
                                             e_sb[0:CK, c % 3, 4 * S * j + 3 * S:4 * S * j + 4 * S],
                                             start=False, stop=(c == CH - 1), skip_group_check=True)
                    i.then_inc(s["pv"], 1)

            SPREAD = (2, 2, 2, 2, 2, 2, 2, 3, 3, 3, 1, 0)
            K_AT, V_AT = (1, 5, 9), (2, 3, 4)

            def pe_batch(pe, b, r, par, first, nxt, nxt2, masked):
                r1 = r + par
                for c in range(CH):
                    n0 = sum(SPREAD[:c])
                    todo = list(range(n0, n0 + SPREAD[c])) if nxt else []

                    def spread():
                        if todo:
                            max_scores(pe, b + 1, r1, 1 - par, todo.pop(0), masked)

                    scores(pe, b, r, par, c, 0, masked)
                    spread()
                    scores(pe, b, r, par, c, 1, masked)
                    if nxt and c in V_AT:
                        f = c - V_AT[0]
                        v_proj(pe, b + 1, 1 - par, f,
                               ((s["kres"], 3 * b + 7) if nxt2 else (s["mrow"], b + 1)) if f == 0
                               else (s["vc"], 3 * b + 3 + f))
                    if nxt2 and c in K_AT:
                        th = K_AT.index(c)
                        k_proj(pe, b + 2, r + 1, par, th, (
                            (s["mrow"], b + 1), (s["vc"], 3 * b + 6), (s["kres"], 3 * b + 8))[th])
                    spread()
                    wb, wp, wc = (b, par, c - 1) if c > 0 else (b - 1, 1 - par, CH - 1)
                    if not (first and c == 0):
                        weigh(pe, wb, wp, wc, 0)
                    spread()
                    if not (first and c == 0):
                        weigh(pe, wb, wp, wc, 1)
                    if nxt and c == 11:
                        if L == 0 and par == 1 and not (isinstance(r, int) and r == B // 2 - 2):
                            pe.wait_ge(s["fl"], r + 2)
                        max_rows(pe, b + 1, (s["kres"], 3 * b + 9) if nxt2 else (s["vc"], 3 * b + 6))

            def over_rounds(e, emit, peeled=1):
                last = B // 2 - peeled
                for b in range(2):
                    emit(e, b, 0, b, b == 0, True, True, True)
                with e.Fori(1, last) as i:
                    for par in range(2):
                        emit(e, 2 * i + par, i, par, False, True, True, True)
                for b in range(2 * last, B):
                    emit(e, b, b // 2, b % 2, False, b < B - 1, b < B - 2, b < B - 3)

            def by_mask(pe, emit, count=None):
                if count is not None:
                    pe.wait_ge(s["fl"], count)
                seen = pe.value_load(flag[0:1, 0:1], min_val=0, max_val=1)
                with pe.If(seen > 0):
                    emit(True)
                with pe.Else():
                    emit(False)

            def pe_rounds(pe):
                def emit(masked, r, b, first=False, last=False):
                    for par in range(2):
                        pe_batch(pe, b + par, r, par, first and par == 0, not (last and par == 1), not last, masked)

                def start(masked):
                    for n in range(24):
                        max_scores(pe, 0, 0, 0, n, masked)
                    max_rows(pe, 0, (s["vc"], 3))
                    emit(masked, 0, 0, first=True)

                by_mask(pe, start, 1)
                with pe.Fori(1, B // 2 - 1) as i:
                    by_mask(pe, lambda masked: emit(masked, i, 2 * i))
                by_mask(pe, lambda masked: emit(masked, B // 2 - 1, B - 2, last=True))

            def act_k(act, b, th):
                act.wait_ge(s["kp"], 3 * b + th + 1)
                if not (isinstance(b, int) and b == 0):
                    act.wait_ge(s[f"st{th}"], 16 * NST * b)
                nc.scalar.activation(k_part[0][:, TK * th:TK * th + TK], aux[:, 0:TK], ACT.Identity,
                                     bias=b_k[:, L:L + 1]).then_inc(s["khi"], 1)

            def act_v(act, b, par, f):
                act.wait_ge(s["vp"], 3 * b + f + 1)
                if f == 0 and not (isinstance(b, int) and b < 2):
                    act.wait_ge(s["pv"], CH * (b - 1))
                nc.scalar.copy(v_sb[0:CK, par, 4 * f:4 * f + 4, :, 1:33],
                               aux[0:CK, :].rearrange("p (c j d) -> p c j d", c=4, j=4)).then_inc(s["vc"], 1)

            def act_u(act, b):
                act.wait_ge(s["pv"], CH * b + CH)
                nc.scalar.copy(u_all[:, :, b, :], acc[:, 0:4 * S].rearrange("p (s q) -> p s q", s=4))\
                    .then_inc(s["uc"], 1)

            def act_batch(act, b, r, par, first, nxt, nxt2, nxt3):
                for c in range(CH):
                    act.wait_ge(s["sc"], CH * b + c + 1)
                    if not (isinstance(b, int) and b == 0 and c < 3):
                        act.wait_ge(s["pv"], CH * b + c - 2)
                    nc.scalar.activation(e_sb[0:CK, c % 3, :].rearrange("p (h n) -> p h n", h=2),
                                         wide[c % 2][0:CK, :, 0:448], ACT.Exp, scale=scale_e).then_inc(s["ex"], 1)
                    if c == 0 and not first:
                        act_u(act, b - 1)
                    if nxt and c in V_AT:
                        act_v(act, b + 1, 1 - par, c - V_AT[0])
                    if nxt2 and c in K_AT:
                        act_k(act, b + 2, K_AT.index(c))

            def dve_k(dve, b, th):
                cols = slice(TK * th, TK * th + TK)
                dve.wait_ge(s["khi"], 3 * b + th + 1)
                if not (isinstance(b, int) and b == 0):
                    dve.wait_ge(s["klo"], 3 * b + th - 2)
                nc.vector.scalar_tensor_tensor(k_rest[:, th, :], aux[:, 0:TK], b_k[:, L:L + 1], k_part[0][:, cols],
                                               ALU.add, ALU.subtract).then_inc(s["kres"], 1)
                dve.wait_ge(s["kres"], 3 * b + th + 1)
                nc.vector.tensor_copy(k_part[1][:, cols], k_rest[:, th, :]).then_inc(s["kmid"], 1)

            def dve_q(dve, b, par):
                if not (isinstance(b, int) and b < 2):
                    dve.wait_ge(s["sc"], CH * (b - 1))
                nc.vector.memset(q_cur[SHIFT_ROW:MASK_ROW, par, :, :].bitcast(F32), 0.0).then_inc(s["qc"], 1)
                nc.vector.tensor_copy(q_cur[0:SHIFT_ROW, par, :, :], q_all[:, :, b, :]).then_inc(s["qc"], 1)

            def dve_max(dve, b, n):
                dve.wait_ge(s["p1"], 24 * b + n + 1)
                nc.vector.tensor_reduce(out=mx[:, n // PAIRS, n % PAIRS:n % PAIRS + 1], in_=bank[n % 2][0:TR, 0:TK],
                                        axis=AX, op=ALU.max).then_inc(s["mxd"], 1)

            def dve_shift(dve, b, par):
                dve.wait_ge(s["mxd"], 24 * b + 24)
                nc.vector.tensor_reduce(out=m_fold[:, :], in_=mx[:, :, :].rearrange("q t p -> q p t"),
                                        axis=AX, op=ALU.max).then_inc(s["fold"], 1)
                dve.wait_ge(s["fold"], b + 1)
                nc.vector.tensor_scalar(m_part[:, :, 0], m_fold[:, :], -1.0, None, ALU.mult).then_inc(s["shi"], 1)
                dve.wait_ge(s["shi"], b + 1)
                nc.vector.scalar_tensor_tensor(m_rest[:, :], m_fold[:, :], -1.0, m_part[:, :, 0],
                                               ALU.mult, ALU.subtract).then_inc(s["srs"], 1)
                dve.wait_ge(s["srs"], b + 1)
                nc.vector.tensor_copy(m_part[:, :, 1], m_rest[:, :]).then_inc(s["smid"], 1)
                dve.wait_ge(s["smid"], b + 1)
                nc.vector.tensor_tensor(m_part[:, :, 2], m_rest[:, :], m_part[:, :, 1], ALU.subtract)\
                    .then_inc(s["slo"], 1)
                dve.wait_ge(s["mt"], b + 1)
                nc.vector.tensor_copy(q_cur[SHIFT_ROW:SHIFT_ROW + 3, par, :, :].rearrange("r p n -> r (p n)"),
                                      aux[SHIFT_ROW:SHIFT_ROW + 3, 0:448].bitcast(BF16)).then_inc(s["mrow"], 1)

            def dve_compare(dve, r):
                dve.wait_ge(s["cs"], r + 1)
                if not (isinstance(r, int) and r == 0):
                    dve.wait_ge(s["ca"], r)
                nc.vector.tensor_reduce(out=differ[:, 0:1], in_=mask_cmp[:, :], axis=AX, op=ALU.max,
                                        apply_absolute_value=True).then_inc(s["cr"], 1)
                dve.wait_ge(s["cr"], r + 1)
                nc.vector.tensor_tensor(differ[:, 1:2], differ[:, 1:2], differ[:, 0:1], ALU.max).then_inc(s["ca"], 1)

            def dve_flag(dve, r):
                dve.wait_ge(s["cf"], r + 2)
                nc.vector.tensor_scalar(flag[:, :], differ[0:1, 2:3], 0.0, None, ALU.is_gt).then_inc(s["fl"], 1)

            def dve_batch(dve, b, r, par, first, nxt, nxt2, nxt3):
                if nxt:
                    dve_q(dve, b + 1, 1 - par)
                compare = L == 0 and par == 1 and not (isinstance(r, int) and r + 2 >= B // 2)
                for c in range(CH):
                    n0 = sum(SPREAD[:c])
                    if nxt:
                        for n in range(n0, n0 + SPREAD[c]):
                            dve_max(dve, b + 1, n)
                    if nxt2 and c in K_AT:
                        dve_k(dve, b + 2, K_AT.index(c))
                    if compare and c == 2:
                        dve_compare(dve, r + 2)
                    if compare and c == 6:
                        dve_flag(dve, r)
                    if L == 0 and isinstance(b, int) and b == B - 3 and c == 6:
                        dve_flag(dve, r - 1)
                if nxt:
                    dve_shift(dve, b + 1, 1 - par)

            def load_ctx(sp, b, par):
                if not (isinstance(b, int) and b < 2):
                    sp.wait_ge(s["vp"], 3 * (b - 1))
                sp.dma_start(ctx_sb[:, par, :], ctx_t[b]).then_inc(s[f"ctx{par}"], 16)

            def load_mask(sp, b, par):
                if not (isinstance(b, int) and b < 2):
                    sp.wait_ge(s["sc"], CH * (b - 1))
                sp.dma_start(mask_sb[:, par, :], mask0[b] if L == 0 else mask1).then_inc(s[f"mk{par}"], 16)

            def load_compare(sp, r):
                if L == 0:
                    if not (isinstance(r, int) and r == 0):
                        sp.wait_ge(s["cr"], r)
                    sp.dma_start(mask_cmp[:, :], mask0.rearrange("(r h) q k -> r (h q) k", h=2)[r])\
                        .then_inc(s["ci"], 16)
                    for h in range(2):
                        sp.dma_start(mask_row[S * h:S * h + S, :], mask0[2 * r + h, 0:1, :].broadcast_to([S, S2]))\
                            .then_inc(s["ci"], 16)
                else:
                    for h in range(2):
                        sp.dma_start(mask_cmp[S * h:S * h + S, :], mask1).then_inc(s["ci"], 16)
                    sp.dma_start(mask_row[:, :], mask1[0:1, :].broadcast_to([2 * S, S2])).then_inc(s["ci"], 16)

            def stack(sp, b, par, th):
                sp.wait_ge(s["klo"], 3 * b + th + 1)
                cols = slice(TK * th, TK * th + TK)
                for t in range(TERMS):
                    sp.dma_start(k_stack[16 * t:16 * t + 16, par, :, cols],
                                 k_part[K_PART[t]][:, cols]).then_inc(s[f"st{th}"], 16)
                if L == 0:
                    sp.dma_start(k_stack[MASK_ROW:ROWS, par, :, cols],
                                 mask_scratch[b][:, None, cols].broadcast_to([3, PAIRS, TK])).then_inc(s[f"st{th}"], 16)

            def sp_batch(sp, b, r, par, first, nxt, nxt2, nxt3):
                if L == 0 and nxt:
                    load_mask(sp, b + 1, 1 - par)
                if nxt2:
                    stack(sp, b + 2, par, 0)
                if nxt3:
                    load_ctx(sp, b + 3, 1 - par)
                if L == 0 and par == 0 and not (isinstance(r, int) and r + 2 >= B // 2):
                    load_compare(sp, r + 2)
                if nxt2:
                    stack(sp, b + 2, par, 1)
                if nxt2:
                    stack(sp, b + 2, par, 2)

            with nc.Block() as block:
                @block.sync
                def _(sp):
                    load_ctx(sp, 0, 0)
                    load_ctx(sp, 1, 1)
                    load_compare(sp, 0)
                    load_mask(sp, 0, 0)
                    if L == 1:
                        load_mask(sp, 1, 1)
                    else:
                        load_compare(sp, 1)
                    sp.wait_ge(s["ql"], 1)
                    for t in range(TERMS):
                        for h2 in range(2):
                            r = 16 * t + A * h2
                            sp.dma_start(
                                q_all[r:r + A, :, :, S * h2:S * h2 + S].rearrange("a p b q -> a (p b) q"),
                                q_part[Q_PART[t]][64 * h2:64 * h2 + 64, :].rearrange("n (b q) -> n b q", b=B),
                            ).then_inc(s["qd"], 16)
                    sp.wait_ge(s["ones"], 1)
                    if L == 1:
                        for par in range(2):
                            sp.dma_start(k_stack[MASK_ROW:ROWS, par, :, :],
                                         mask_scratch[B][:, None, :].broadcast_to([3, PAIRS, S2]))\
                                .then_inc(s["mk"], 16)
                    for b in range(2):
                        for th in range(TH):
                            stack(sp, b, b, th)
                    load_ctx(sp, 2, 0)
                    over_rounds(sp, sp_batch, 2)
                    for par in range(2):
                        sp.wait_ge(s[f"mk{par}"], 16 * (B // 2 if L == 0 else 1))

                @block.gpsimd
                def _(pool):
                    norm_pool(pool, q)

                    def lo(b, th):
                        cols = slice(TK * th, TK * th + TK)
                        if not (isinstance(b, int) and b < 2):
                            pool.wait_ge(s["sc"], CH * (b - 2) + 4 * th + 4)
                        pool.wait_ge(s["kmid"], 3 * b + th + 1)
                        nc.gpsimd.tensor_tensor(k_part[2][:, cols], k_rest[:, th, :], k_part[1][:, cols],
                                                ALU.subtract).then_inc(s["klo"], 1)

                    def against_row(r):
                        pool.wait_ge(s["ci"], 48 * r + 48)
                        nc.gpsimd.tensor_tensor(mask_cmp[:, :], mask_cmp[:, :], mask_row[:, :], ALU.subtract)\
                            .then_inc(s["cs"], 1)

                    def over_partitions():
                        nc.gpsimd.partition_all_reduce(differ[:, 2:3], differ[:, 1:2], 2 * S, RMAX)\
                            .then_inc(s["cf"], 1)

                    def pool_batch(pool, b, r, par, first, nxt, nxt2, nxt3):
                        compare = L == 0 and not (isinstance(r, int) and r + 2 >= B // 2)
                        for th in range(TH):
                            if compare and par == 1 and th == 1:
                                pool.wait_ge(s["ca"], r + 3)
                            if nxt2:
                                lo(b + 2, th)
                            if compare and par == 1 and th == 1:
                                over_partitions()
                        if compare and par == 0:
                            against_row(r + 2)

                    against_row(0)
                    if L == 0:
                        against_row(1)
                    pool.wait_ge(s["ca"], 2 if L == 0 else 1)
                    over_partitions()
                    for b in range(2):
                        for th in range(TH):
                            lo(b, th)
                    over_rounds(pool, pool_batch, 2)

                @block.scalar
                def _(act):
                    if L == 0:
                        act.wait_ge(w_in, n_w)
                        act.wait_ge(const, CONST)
                    transpose_copy(act, q)
                    for i in range(2):
                        act.wait_ge(s["qp"], i + 1)
                        if L == 0:
                            act.wait_ge(s["qs"], 1)
                            nc.scalar.activation(q_f[:, HALF * i:HALF * i + HALF], wide[1][:, i, 0:HALF],
                                                 ACT.Identity, bias=b_q[:, 0:1], scale=scale_q).then_inc(s["qs"], 1)
                        else:
                            nc.scalar.copy(q_f[:, HALF * i:HALF * i + HALF], wide[1][:, i, 0:HALF])\
                                .then_inc(s["qs"], 1)
                    for b in range(2):
                        for th in range(TH):
                            act_k(act, b, th)
                    for f in range(3):
                        act_v(act, 0, 0, f)
                    over_rounds(act, act_batch)
                    act_u(act, B - 1)
                    if L == 1:
                        for i in range(2):
                            act.wait_ge(s["ot"], 4 * i + 4)
                            nc.scalar.copy(xt[:, HALF * i:HALF * i + HALF], wide[1][:, i, 0:HALF])\
                                .then_inc(s["otc"], 1)

                @block.vector
                def _(dve):
                    if L == 0:
                        dve.wait_ge(w_in, n_w)
                        dve.wait_ge(const, CONST)
                        nc.vector.tensor_scalar(b_q[:, :], b_q[:, :], scale_q, None, ALU.mult).then_inc(s["qs"], 1)
                    else:
                        nc.vector.memset(differ[:, :], 0.0).then_inc(s["xo"], 1)
                    nc.vector.memset(k_stack[SHIFT_ROW:ROWS, :, :, :], 1.0).then_inc(s["ones"], 1)
                    norm_vector(dve, q, x_sb, xn, False)
                    for r in range(2 if L == 0 else 1):
                        if L == 1:
                            dve.wait_ge(s["xo"], 1)
                        dve_compare(dve, r)
                    dve_flag(dve, -1)
                    dve.wait_ge(s["qs"], 3 if L == 0 else 2)
                    nc.vector.tensor_copy(q_part[0][:, :], q_f[:, :]).then_inc(s["qr"], 1)
                    dve.wait_ge(s["qr"], 1)
                    nc.vector.tensor_tensor(q_rest[:, :], q_f[:, :], q_part[0][:, :], ALU.subtract)\
                        .then_inc(s["qr"], 1)
                    dve.wait_ge(s["qr"], 2)
                    nc.vector.tensor_copy(q_part[1][:, :], q_rest[:, :]).then_inc(s["qm"], 1)
                    dve.wait_ge(s["qm"], 1)
                    nc.vector.tensor_tensor(q_part[2][:, :], q_rest[:, :], q_part[1][:, :], ALU.subtract)\
                        .then_inc(s["ql"], 1)
                    for b in range(2):
                        for th in range(TH):
                            dve_k(dve, b, th)
                    dve.wait_ge(s["qd"], 16 * 12)
                    dve_q(dve, 0, 0)
                    for n in range(24):
                        dve_max(dve, 0, n)
                    dve_shift(dve, 0, 0)
                    over_rounds(dve, dve_batch, 2)
                    for g in range(2):
                        dve.wait_ge(s["ut"], 16 * g + 16)
                        for t4 in range(4):
                            t = 4 * g + t4
                            src = post[t4][0:TR, :].rearrange("r (s j n) -> r s j n", s=4, j=4)
                            nc.vector.reciprocal(rec[:, t, 0:3, :], src[:, 0:3, :, 0]).then_inc(s["rc"], 1)
                            nc.vector.reciprocal(rec[:, t, 3, :], src[:, 3, :, 31]).then_inc(s["rc"], 1)
                        for t4 in range(4):
                            t = 4 * g + t4
                            src = post[t4][0:TR, :].rearrange("r (s j n) -> r s j n", s=4, j=4)
                            dve.wait_ge(s["rc"], 2 * t + 2)
                            for k in range(4):
                                r0 = 1 + A * k if k < 3 else 23
                                o = xn[:, t, :].rearrange("r (j k a) -> r j k a", j=4, k=4)[:, :, k, :]
                                nc.vector.tensor_tensor(o, src[:, k, :, r0:r0 + A],
                                                        rec[:, t, k, :, None].broadcast_to([TR, 4, A]), ALU.mult)\
                                    .then_inc(s["o"], 1)
                    if L == 0:
                        dve.wait_ge(s["o"], 32)
                        nc.vector.tensor_tensor(xn[:, :, :], xn[:, :, :], b_v[:, None, :].broadcast_to([TR, T, D]),
                                                ALU.add).then_inc(s["xo"], 1)
                        dve.wait_ge(s["xo"], 1)
                        nc.vector.scalar_tensor_tensor(
                            x_sb[:, :, :].rearrange("r t d -> r (t d)"), xn[:, :, :].rearrange("r t d -> r (t d)"),
                            tg[0:TR, 0:1], x_sb[:, :, :].rearrange("r t d -> r (t d)"), ALU.mult, ALU.add)\
                            .then_inc(s["xd"], 1)
                        dve.wait_ge(s["xd"], 1)
                    else:
                        for i in range(2):
                            dve.wait_ge(s["wo"], 4 * i + 4)
                            v = x_sb[:, 4 * i:4 * i + 4, :].rearrange("r t d -> r (t d)")
                            nc.vector.scalar_tensor_tensor(v, wide[0][0:TR, i, :], tg[0:TR, 1:2], v,
                                                           ALU.mult, ALU.add).then_inc(s["xd"], 1)
                        dve.wait_ge(s["xd"], 2)

                @block.tensor
                def _(pe):
                    if L == 0:
                        pe.wait_ge(w_in, n_w)
                        pe.wait_ge(const, CONST)
                    transpose_tensor(pe, q, xn, False)
                    for i in range(2):
                        pe.wait_ge(q[5], i + 1)
                        nc.tensor.matmul(wide[1][:, i, 0:HALF], w_q[L][:, :], xt[:, HALF * i:HALF * i + HALF],
                                         start=True, stop=True).then_inc(s["qp"], 1)
                    for th in range(TH):
                        k_proj(pe, 0, 0, 0, th, None if th == 0 else (s["kres"], th))
                    for th in range(TH):
                        k_proj(pe, 1, 0, 1, th, (s["kres"], 3 + th))
                    for f in range(3):
                        v_proj(pe, 0, 0, f, (s["kres"], 6) if f == 0 else (s["vc"], f))
                    if L == 1:
                        pe.wait_ge(s["mk"], 32)
                    pe_rounds(pe)
                    for part in range(2):
                        weigh(pe, B - 1, 1, CH - 1, part)
                    pe.wait_ge(s["ex"], CH * B)
                    pe.wait_ge(s["uc"], B)
                    for t in range(T):
                        if t >= 4:
                            pe.wait_ge(s["o"], 4 * (t - 4) + 4)
                        for k in range(4):
                            nc.tensor.transpose(post[t % 4][0:TR, P * k:P * k + P],
                                                u_all[:, k, 2 * t:2 * t + 2, :].rearrange("p b q -> p (b q)"),
                                                ident[:, :]).then_inc(s["ut"], 1)
                    if L == 1:
                        for t in range(T):
                            pe.wait_ge(s["o"], 4 * t + 4)
                            nc.tensor.transpose(wide[1][:, t // 4, TR * (t % 4):TR * (t % 4) + TR], xn[:, t, :],
                                                ident[0:TR, 0:TR]).then_inc(s["ot"], 1)
                        for t in range(T):
                            pe.wait_ge(s["otc"], t // 4 + 1)
                            nc.tensor.matmul(wide[0][0:TR, t // 4, P * (t % 4):P * (t % 4) + P],
                                             xt[:, TR * t:TR * t + TR], w_o[:, :], start=True, stop=True)\
                                .then_inc(s["wo"], 1)


        def experts(L):
            s = {n: sem(f"f{L}_{n}") for n in (
                "ch", "lg", "ex", "g", "gt", "gtc", "gs", "w10", "w11", "w20", "w21", "gb0", "gb1", "hp", "gelu", "hg", "yp",
                "yc", "yt", "xd", "out")}
            fw1, fb1, fw2 = (fw1_0, fb1_0, fw2_0) if L == 0 else (fw1_1, fb1_1, fw2_1)
            q0 = norm(f"m{L}", None, None, None, False)
            q1 = norm("mm", None, None, None, True) if L == 1 else q0
            U = 2 * FC
            LAG = 2
            chain = [0]

            def over_experts(e, emit):
                for n in range(2):
                    emit(e, n, 0, n, n == 0, False)
                with e.Fori(1, E // 2 - 1) as i:
                    for par in range(2):
                        emit(e, 2 * i + par, i, par, False, False)
                for n in range(E - 2, E):
                    emit(e, n, n // 2, n % 2, False, n == E - 1)

            def early(n, k):
                return isinstance(n, int) and n < k

            def load(sp, e, par):
                if not early(e, 2):
                    sp.wait_ge(s["hp"], U * (e - 1))
                sp.dma_start(w1_sb[:, par, :], fw1[e]).then_inc(s[f"w1{par}"], 16)
                if not early(e, 2):
                    sp.wait_ge(s["gelu"], U * (e - 1))
                sp.dma_start(b1_sb[:, par, :], fb1[e]).then_inc(s[f"w1{par}"], 16)
                if not early(e, 2):
                    sp.wait_ge(s["yp"], U * (e - 1))
                sp.dma_start(w2_sb[:, par, :, :], fw2[e]).then_inc(s[f"w2{par}"], 16)

            def load_gates(sp, e, par):
                if not early(e, 2):
                    sp.wait_ge(s["hg"], U * (e - 1))
                sp.dma_start(gate_b[:, par, :], gate_scratch[L, e][None, :].broadcast_to([P, NTOK]))\
                    .then_inc(s[f"gb{par}"], 16)

            def hidden(pe, e, r, par, u):
                n = U * e + u
                if u == 0:
                    pe.wait_ge(s[f"w1{par}"], 32 * r + 32)
                if not early(n, 4):
                    pe.wait_ge(s["gelu"], n - 3)
                fc, half = u // 2, u % 2
                nc.tensor.matmul(bank[u % 4][:, 0:HALF], w1_sb[:, par, P * fc:P * fc + P],
                                 xt[:, HALF * half:HALF * half + HALF], start=True, stop=True).then_inc(s["hp"], 1)

            def back(pe, e, r, par, u, last):
                n = U * e + u
                if u == 0:
                    pe.wait_ge(s[f"w2{par}"], 16 * r + 16)
                pe.wait_ge(s["hg"], n + 1)
                fc, half = u // 2, u % 2
                nc.tensor.matmul(wide[1][:, half, 0:HALF], w2_sb[:, par, fc, :], hg_sb[:, u % 4, :],
                                 start=False, stop=last and fc == FC - 1, skip_group_check=True)\
                    .then_inc(s["yp"], 1)

            def pe_expert(pe, e, r, par, first, last):
                for u in range(U):
                    if u + LAG < U:
                        hidden(pe, e, r, par, u + LAG)
                    elif not last:
                        hidden(pe, e + 1, r + par, 1 - par, u + LAG - U)
                    back(pe, e, r, par, u, last)

            def act_expert(act, e, r, par, first, last):
                for u in range(U):
                    n = U * e + u
                    act.wait_ge(s["hp"], n + 1)
                    if not early(n, 4):
                        act.wait_ge(s["hg"], n - 3)
                    nc.scalar.activation(h_sb[:, u % 4, :], bank[u % 4][:, 0:HALF],
                                         ACT.Gelu if L == 0 else ACT.Gelu_apprx_tanh,
                                         bias=b1_sb[:, par, u // 2:u // 2 + 1]).then_inc(s["gelu"], 1)

            def dve_expert(dve, e, r, par, first, last):
                dve.wait_ge(s[f"gb{par}"], 16 * r + 16)
                for u in range(U):
                    n = U * e + u
                    dve.wait_ge(s["gelu"], n + 1)
                    if not early(n, 4):
                        dve.wait_ge(s["yp"], n - 3)
                    half = u % 2
                    nc.vector.tensor_tensor(hg_sb[:, u % 4, :], h_sb[:, u % 4, :],
                                            gate_b[:, par, HALF * half:HALF * half + HALF], ALU.mult)\
                        .then_inc(s["hg"], 1)

            def sp_expert(sp, e, r, par, first, last):
                load(sp, e, par)
                load_gates(sp, e, par)

            def over_tokens(v):
                return v[:, :, None].broadcast_to([TR, T, E])

            with nc.Block() as block:
                @block.sync
                def _(sp):
                    sp.wait_ge(s["gtc"], 2)
                    sp.dma_start(gate_scratch[L], g_t[:, :]).then_inc(s["gs"], 16)
                    sp.wait_ge(s["gs"], 16)
                    over_experts(sp, sp_expert)
                    if L == 1:
                        for i in range(2):
                            sp.wait_ge(s["xd"], i + 1)
                            sp.dma_start(out[HALF * i:HALF * i + HALF, :].rearrange("(t r) d -> r t d", r=TR),
                                         x_sb[:, 4 * i:4 * i + 4, :]).then_inc(s["out"], 16)
                        sp.wait_ge(s["out"], 32)

                @block.gpsimd
                def _(pool):
                    norm_pool(pool, q0)
                    if L == 1:
                        pool.wait_ge(q0[2], 2)
                        pool.wait_ge(q0[3], T)
                        norm_pool(pool, q1)

                @block.tensor
                def _(pe):
                    transpose_tensor(pe, q1, xn, L == 1)
                    for t in range(T):
                        pe.wait_ge(q1[5], t // 4 + 1)
                        i = nc.tensor.matmul(aux[0:TR, E * t:E * t + E], xt[:, TR * t:TR * t + TR], w_r[L][:, :],
                                             start=True, stop=True)
                    i.then_inc(s["lg"], 1)
                    pe.wait_ge(s["g"], 1)
                    for t in range(T):
                        nc.tensor.transpose(wide[0][0:E, t // 4, TR * (t % 4):TR * (t % 4) + TR],
                                            lg[:, 7, t, :], ident[0:TR, 0:TR]).then_inc(s["gt"], 1)
                    pe.wait_ge(s["gtc"], 2)
                    for i in range(2):
                        nc.tensor.matmul(wide[1][:, i, 0:HALF], fb2[L][:, :], g_t[:, HALF * i:HALF * i + HALF],
                                         start=True, stop=False, skip_group_check=True)
                    for u in range(LAG):
                        hidden(pe, 0, 0, 0, u)
                    over_experts(pe, pe_expert)
                    for t in range(T):
                        pe.wait_ge(s["yc"], t // 4 + 1)
                        nc.tensor.transpose(wide[0][0:TR, t // 4, P * (t % 4):P * (t % 4) + P],
                                            y_t[:, TR * t:TR * t + TR], ident[:, :]).then_inc(s["yt"], 1)

                @block.scalar
                def _(act):
                    transpose_copy(act, q1)
                    act.wait_ge(s["ch"], 3)
                    nc.scalar.activation(lg[:, 2, :, :], lg[:, 1, :, :], ACT.Exp).then_inc(s["ex"], 1)
                    for i in range(2):
                        act.wait_ge(s["gt"], 4 * i + 4)
                        nc.scalar.copy(g_t[:, HALF * i:HALF * i + HALF], wide[0][0:E, i, 0:HALF])\
                            .then_inc(s["gtc"], 1)
                    over_experts(act, act_expert)
                    act.wait_ge(s["yp"], U * E)
                    for i in range(2):
                        nc.scalar.copy(y_t[:, HALF * i:HALF * i + HALF], wide[1][:, i, 0:HALF])\
                            .then_inc(s["yc"], 1)

                @block.vector
                def _(dve):
                    def link(ins):
                        chain[0] += 1
                        ins.then_inc(s["ch"], 1)
                        dve.wait_ge(s["ch"], chain[0])

                    def first_of(eq, best, tie_of, to):
                        link(nc.vector.tensor_tensor(lg[:, eq, :, :], lg[:, eq, :, :],
                                                     tie[:, None, :].broadcast_to([TR, T, E]), ALU.mult))
                        link(nc.vector.tensor_reduce(out=ls[:, best, :], in_=lg[:, eq, :, :], axis=AX, op=ALU.max))
                        link(nc.vector.tensor_tensor(lg[:, to, :, :], lg[:, eq, :, :], over_tokens(ls[:, best, :]),
                                                     ALU.is_equal))

                    if L == 0:
                        norm_vector(dve, q0, x_sb, xn, False)
                    else:
                        norm_vector(dve, q0, x_sb, resid, False)
                        dve.wait_ge(q0[3], T)
                        norm_vector(dve, q1, resid, xn, True)
                    dve.wait_ge(s["lg"], 1)
                    logits = aux[0:TR, 0:T * E].rearrange("r (t e) -> r t e", t=T)
                    if L == 0:
                        link(nc.vector.tensor_tensor(lg[:, 0, :, :], logits,
                                                     b_r[:, None, :].broadcast_to([TR, T, E]), ALU.add))
                    else:
                        link(nc.vector.tensor_copy(lg[:, 0, :, :], logits))
                    link(nc.vector.tensor_reduce(out=ls[:, 0, :], in_=lg[:, 0, :, :], axis=AX, op=ALU.max))
                    link(nc.vector.tensor_tensor(lg[:, 1, :, :], lg[:, 0, :, :], over_tokens(ls[:, 0, :]),
                                                 ALU.subtract))
                    dve.wait_ge(s["ex"], 1)
                    link(nc.vector.tensor_reduce(out=ls[:, 1, :], in_=lg[:, 2, :, :], axis=AX, op=ALU.add))
                    link(nc.vector.reciprocal(ls[:, 2, :], ls[:, 1, :]))
                    if L == 0:
                        link(nc.vector.tensor_tensor(lg[:, 3, :, :], lg[:, 0, :, :], over_tokens(ls[:, 0, :]),
                                                     ALU.is_equal))
                        first_of(3, 3, tie, 4)
                        nc.vector.tensor_tensor(lg[:, 7, :, :], lg[:, 4, :, :], over_tokens(ls[:, 2, :]),
                                                ALU.mult).then_inc(s["g"], 1)
                    else:
                        link(nc.vector.tensor_tensor(lg[:, 3, :, :], lg[:, 2, :, :], over_tokens(ls[:, 2, :]),
                                                     ALU.mult))
                        link(nc.vector.tensor_reduce(out=ls[:, 3, :], in_=lg[:, 3, :, :], axis=AX, op=ALU.max))
                        link(nc.vector.tensor_tensor(lg[:, 4, :, :], lg[:, 3, :, :], over_tokens(ls[:, 3, :]),
                                                     ALU.is_equal))
                        first_of(4, 4, tie, 5)
                        link(nc.vector.tensor_scalar(lg[:, 6, :, :], lg[:, 5, :, :], -4.0, None, ALU.mult))
                        link(nc.vector.tensor_tensor(lg[:, 3, :, :], lg[:, 3, :, :], lg[:, 6, :, :], ALU.add))
                        link(nc.vector.tensor_reduce(out=ls[:, 5, :], in_=lg[:, 3, :, :], axis=AX, op=ALU.max))
                        link(nc.vector.tensor_tensor(lg[:, 4, :, :], lg[:, 3, :, :], over_tokens(ls[:, 5, :]),
                                                     ALU.is_equal))
                        first_of(4, 4, tie, 6)
                        link(nc.vector.tensor_tensor(ls[:, 6, :], ls[:, 3, :], ls[:, 5, :], ALU.add))
                        link(nc.vector.tensor_scalar(ls[:, 6, :], ls[:, 6, :], 1e-9, None, ALU.add))
                        link(nc.vector.reciprocal(ls[:, 7, :], ls[:, 6, :]))
                        link(nc.vector.tensor_tensor(ls[:, 3, :], ls[:, 3, :], ls[:, 7, :], ALU.mult))
                        link(nc.vector.tensor_tensor(ls[:, 5, :], ls[:, 5, :], ls[:, 7, :], ALU.mult))
                        link(nc.vector.tensor_tensor(lg[:, 5, :, :], lg[:, 5, :, :], over_tokens(ls[:, 3, :]),
                                                     ALU.mult))
                        link(nc.vector.tensor_tensor(lg[:, 6, :, :], lg[:, 6, :, :], over_tokens(ls[:, 5, :]),
                                                     ALU.mult))
                        nc.vector.tensor_tensor(lg[:, 7, :, :], lg[:, 5, :, :], lg[:, 6, :, :], ALU.add)\
                            .then_inc(s["g"], 1)
                    over_experts(dve, dve_expert)
                    for i in range(2):
                        dve.wait_ge(s["yt"], 4 * i + 4)
                        y = wide[0][0:TR, i, :]
                        v = x_sb[:, 4 * i:4 * i + 4, :].rearrange("r t d -> r (t d)")
                        if L == 1:
                            r = resid[:, 4 * i:4 * i + 4, :].rearrange("r t d -> r (t d)")
                            link(nc.vector.tensor_tensor(r, y, r, ALU.add))
                            y = r
                        nc.vector.scalar_tensor_tensor(v, y, tg[0:TR, 2 + L:3 + L], v, ALU.mult, ALU.add)\
                            .then_inc(s["xd"], 1)
                    dve.wait_ge(s["xd"], 2)

        attention(0)
        experts(0)
        nc.all_engine_barrier()
        nc.clear_and_free_semaphores(made)
        nc.all_engine_barrier()
        attention(1)
        experts(1)


def kernel(x, ctx_1024, mask_BxSxS2_ff0, mask_SxS2_fk0, g_xattn, g_ffn, L0_xattn_Wq, L0_xattn_bq, L0_xattn_Wk,
           L0_xattn_bk, L0_xattn_Wv, L0_xattn_bv, L0_ffn_W1, L0_ffn_b1, L0_ffn_W2, L0_ffn_b2, L0_ffn_Wr, L0_ffn_br,
           L1_xattn_Wq, L1_xattn_Wkv, L1_xattn_Wout, L1_ffn_gamma, L1_ffn_beta, L1_ffn_Wg, L1_ffn_W1, L1_ffn_b1,
           L1_ffn_W2, L1_ffn_b2):
    import numpy as np
    import concourse.bacc as bacc
    from concourse.bass_utils import run_bass_kernel_spmd

    def by_pair(w):
        return np.asarray(w).reshape(PAIRS, 2, A, -1).transpose(1, 2, 0, 3).reshape(D, -1)

    def turned(w):
        return np.ascontiguousarray(np.asarray(w).T)

    def row(v):
        return np.asarray(v).reshape(1, -1)

    def chunks(v):
        return np.asarray(v).reshape(E, FC, P).transpose(0, 2, 1)

    def chunked_rows(w):
        return np.asarray(w).reshape(E, FC, P, D).transpose(0, 2, 1, 3)

    wkv = np.asarray(L1_xattn_Wkv)
    arrays = {
        "x": np.asarray(x).reshape(NTOK, D),
        "ctx_t": np.asarray(ctx_1024).transpose(0, 2, 1),
        "mask0": mask_BxSxS2_ff0, "mask1": mask_SxS2_fk0,
        "gates_in": row(np.concatenate([np.asarray(g_xattn), np.asarray(g_ffn)])),
        "ident_in": np.eye(P, dtype=np.float32),
        "tie_in": row(np.arange(E, 0, -1, dtype=np.float32)),
        "wq0": turned(by_pair(L0_xattn_Wq)), "bq0": by_pair(L0_xattn_bq),
        "wk0": turned(by_pair(L0_xattn_Wk)),
        "bk0": np.concatenate([by_pair(L0_xattn_bk), np.zeros((D, 1), np.float32)], axis=1),
        "wv0": turned(L0_xattn_Wv), "bv0": row(L0_xattn_bv),
        "wq1": turned(by_pair(L1_xattn_Wq)), "wk1": turned(by_pair(wkv[:D])), "wv1": turned(wkv[D:]),
        "wo1": turned(L1_xattn_Wout),
        "fw1_0": L0_ffn_W1, "fb1_0": chunks(L0_ffn_b1), "fw2_0": chunked_rows(L0_ffn_W2), "fb2_0": L0_ffn_b2,
        "wr0": L0_ffn_Wr, "br0": row(L0_ffn_br),
        "gamma": row(L1_ffn_gamma), "beta": row(L1_ffn_beta),
        "fw1_1": L1_ffn_W1, "fb1_1": chunks(L1_ffn_b1), "fw2_1": chunked_rows(L1_ffn_W2), "fb2_1": L1_ffn_b2,
        "wr1": turned(L1_ffn_Wg),
    }
    nc = bacc.Bacc("TRN2", target_bir_lowering=False, num_devices=1)
    feeds, args = {}, {}
    for name, a in arrays.items():
        a = np.ascontiguousarray(a)
        feeds[f"in_{name}"] = a
        args[name] = nc.dram_tensor(f"in_{name}", a.shape, mybir.dt.from_np(a.dtype), kind="ExternalInput").ap()
    args["out"] = nc.dram_tensor("out_x", (NTOK, D), F32, kind="ExternalOutput").ap()
    build(nc, **args)
    got = run_bass_kernel_spmd(nc, [feeds], core_ids=[0])
    return got.results[0]["out_x"].reshape(B, S, D)
```

```python
from contextlib import ExitStack

import concourse.bass as bass
from concourse import mybir

ALU = mybir.AluOpType
ACT = mybir.ActivationFunctionType
AX = mybir.AxisListType.X
RMAX = bass.bass_isa.ReduceOp.max
F32 = mybir.dt.float32
BF16 = mybir.dt.bfloat16
I32 = mybir.dt.int32

P = 128
B, S, D = 16, 56, 128
S2 = 1500
H, A = 16, 8
PAIRS = H // 2
CH, CK = 12, 125
TH, TK = 3, 500
HQ = H * S
MJ, MK = 6, 250
T, TR = 8, 112
NTOK = B * S
HALF = NTOK // 2
E, F = 8, 512
FC = F // P
EPS = 1e-5
TERMS = 6
K_PART = (0, 0, 0, 1, 1, 2)
Q_PART = (0, 1, 2, 0, 1, 0)
SHIFT_ROW = TERMS * 2 * A
MASK_ROW = SHIFT_ROW + 3
ROWS = MASK_ROW + 3


def build(nc, x, ctx_t, mask0, mask1, gates_in, ident_in, tie_in,
          wq0, bq0, wk0, bk0, wv0, bv0, wq1, wk1, wv1, wo1,
          fw1_0, fb1_0, fw2_0, fb2_0, wr0, br0,
          gamma, beta, fw1_1, fb1_1, fw2_1, fb2_1, wr1, out):
    es = ExitStack()
    with es:
        def sb(name, shape, dt=F32):
            return es.enter_context(nc.sbuf_tensor(name, shape, dt))

        made = []

        def sem(name):
            made.append(nc.alloc_semaphore(name=name))
            return made[-1]

        mask_scratch = nc.dram_tensor("mask_scratch", (B + 1, 3, S2), BF16, kind="Internal").ap()
        gate_scratch = nc.dram_tensor("gate_scratch", (2, E, NTOK), F32, kind="Internal").ap()

        shared = sb("shared", [P, 2 * PAIRS * S2 // 2])
        k_stack = shared[:, :].bitcast(BF16).rearrange("p (b h k) -> p b h k", b=2, h=PAIRS)
        k_part = [sb(n, [P, S2], BF16) for n in ("k_hi", "k_mid", "k_lo")]
        k_rest = sb("k_rest", [P, TH, TK])
        ctx_sb = sb("ctx_sb", [P, 2, S2])
        v_sb = sb("v_sb", [P, 2, CH, 4, 34])
        e_sb = sb("e_sb", [P, 3, HQ])
        q_all = sb("q_all", [SHIFT_ROW, PAIRS, B, 2 * S], BF16)
        q_cur = sb("q_cur", [ROWS, 2, PAIRS, 2 * S], BF16)
        q_part = [sb(n, [P, NTOK], BF16) for n in ("q_hi", "q_mid", "q_lo")]
        u_all = sb("u_all", [P, 4, B, S])
        q_f = u_all[:, 0, :, :].rearrange("p b q -> p (b q)")
        q_rest = u_all[:, 1, :, :].rearrange("p b q -> p (b q)")
        mask_sb = sb("mask_sb", [S, 2, S2])
        mask_cmp = sb("mask_cmp", [2 * S, S2])
        mask_row = sb("mask_row", [2 * S, S2])
        differ = sb("differ", [2 * S, 5])
        flag = sb("flag", [1, 1], I32)
        ident_q = sb("ident_q", [S, PAIRS, S])
        mx = sb("mx", [TR, TH, PAIRS])
        m_fold = sb("m_fold", [TR, PAIRS])
        m_rest = sb("m_rest", [TR, PAIRS])
        m_part = sb("m_part", [TR, PAIRS, 3], BF16)
        x_sb = sb("x_sb", [TR, T, D])
        xn = sb("xn", [TR, T, D])
        xt = sb("xt", [P, NTOK])
        stats = sb("stats", [TR, T, 6])
        mv = sb("mv", [TR, T, 2])
        rstd = sb("rstd", [TR, T])
        minus_half = sb("minus_half", [TR, T])
        rec = sb("rec", [TR, T, 4, 4])
        ident = sb("ident", [P, P])
        ident_b = sb("ident_b", [P, P], BF16)
        tie = sb("tie", [TR, E])
        tg = sb("tg", [P, 4])
        one = sb("one", [P, TK])
        ones_b = sb("ones_b", [3, MK], BF16)
        w_q = [sb(f"w_q{i}", [P, D]) for i in range(2)]
        w_k = [sb(f"w_k{i}", [P, D]) for i in range(2)]
        w_v = [sb(f"w_v{i}", [P, D]) for i in range(2)]
        w_o = sb("w_o", [P, D])
        w_r = [sb(f"w_r{i}", [P, E]) for i in range(2)]
        b_q = sb("b_q", [P, 1])
        b_k = sb("b_k", [P, 2])
        b_v = sb("b_v", [TR, D])
        b_r = sb("b_r", [TR, E])
        gam = sb("gam", [TR, D])
        bet = sb("bet", [TR, D])
        lg = sb("lg", [TR, 8, T, E])
        ls = sb("ls", [TR, 8, T])
        g_t = sb("g_t", [E, NTOK])
        b1_sb = sb("b1_sb", [P, 2, FC])
        fb2 = [sb(f"fb2{i}", [E, D]) for i in range(2)]

        ff = shared[:, :]
        w1_sb = ff[:, 0:1024].rearrange("p (b f) -> p b f", b=2)
        w2_sb = ff[:, 1024:2048].rearrange("p (b c d) -> p b c d", b=2, c=FC)
        gate_b = ff[:, 2048:2048 + 2 * NTOK].rearrange("p (b n) -> p b n", b=2)
        h_sb = ff[:, 4096:4096 + 4 * HALF].rearrange("p (b n) -> p b n", b=4)
        hg_sb = ff[:, 6144:6144 + 4 * HALF].rearrange("p (b n) -> p b n", b=4)
        resid = ff[0:TR, 10752:10752 + T * D].rearrange("r (t d) -> r t d", t=T)
        y_t = ff[:, 8192:8192 + NTOK]
        m_row = sb("m_row", [MJ * (B + 1), MK])
        m_left = sb("m_left", [MJ * (B + 1), MK])
        mr_part = [sb(f"mr_part{i}", [MJ * (B + 1), MK], BF16)[:, :] for i in range(3)]

        bank = [es.enter_context(nc.psum_tensor(f"bank{i}", [P, 512], F32)) for i in range(4)]
        wide = [es.enter_context(nc.psum_tensor(f"wide{i}", [P, 2, 512], F32)) for i in range(2)]
        acc, aux = bank[2], bank[3]
        post = bank

        state = {}

        w_in, w_late = sem("w_in"), sem("w_late")
        mr_in, mr_split, mask_out = sem("mr_in"), sem("mr_split"), sem("mask_out")
        x_in, const, zeroed, tg_in, tg_done = (sem(n) for n in ("x_in", "const", "zeroed", "tg_in", "tg_done"))
        W_IN = 16 * 5
        late = ((b_v, bv0.broadcast_to([TR, D])), (w_q[1], wq1), (w_k[1], wk1), (w_v[1], wv1), (w_o, wo1),
                (w_r[0], wr0), (w_r[1], wr1), (fb2[0], fb2_0), (fb2[1], fb2_1),
                (b_r, br0.broadcast_to([TR, E])), (gam, gamma.broadcast_to([TR, D])),
                (bet, beta.broadcast_to([TR, D])), (tie, tie_in.broadcast_to([TR, E])))
        W_LATE = 16 * len(late)

        with nc.Block() as block:
            @block.sync
            def _(sp):
                sp.dma_start(x_sb[:, :, :], x.rearrange("(t r) d -> r t d", r=TR)).then_inc(x_in, 16)
                sp.dma_start(ident[:, :], ident_in).then_inc(x_in, 16)
                sp.dma_start(m_row[0:MJ * B, :], mask0[:, 0, :].rearrange("b (j k) -> b j k", j=MJ))\
                    .then_inc(mr_in, 16)
                sp.dma_start(m_row[MJ * B:MJ * (B + 1), :], mask1[0:1, :].rearrange("b (j k) -> b j k", j=MJ))\
                    .then_inc(mr_in, 16)
            @block.scalar
            def _(act):
                for dst, src in ((w_k[0], wk0), (b_k, bk0), (w_q[0], wq0), (b_q, bq0), (w_v[0], wv0)):
                    act.dma_start(dst[:, :], src).then_inc(w_in, 16)
                act.dma_start(tg[:, :], gates_in.broadcast_to([P, 4])).then_inc(tg_in, 16)
            @block.vector
            def _(dve):
                nc.vector.memset(q_cur[SHIFT_ROW:ROWS, :, :, :], 1.0).then_inc(const, 1)
                nc.vector.memset(ones_b[:, :], 1.0).then_inc(const, 1)
                nc.vector.memset(v_sb[:, :, :, :, 0:1], 1.0).then_inc(const, 1)
                nc.vector.memset(v_sb[:, :, :, :, 33:34], 1.0).then_inc(const, 1)
                nc.vector.memset(one[:, :], 1.0).then_inc(const, 1)
                dve.wait_ge(x_in, 32)
                nc.vector.tensor_copy(ident_b[:, :], ident[:, :]).then_inc(const, 1)
                nc.vector.tensor_copy(ident_q[:, :, :], ident[0:S, None, 0:S].broadcast_to([S, PAIRS, S]))\
                    .then_inc(const, 1)
            @block.gpsimd
            def _(pool):
                nc.gpsimd.memset(minus_half[:, :], -0.5).then_inc(const, 1)
        CONST = 8

        def norm(tag, block, src, dst, first, affine=False):
            st, ag, rs, nm, tp, ev, af = (sem(f"{tag}_{n}") for n in ("stat", "aggr", "rstd", "norm", "tp", "ev", "aff"))
            return st, ag, rs, nm, tp, ev, af

        def norm_vector(dve, q, src, dst, affine):
            st, ag, rs, nm, tp, ev, af = q
            for t in range(T):
                nc.vector.bn_stats(stats[:, t, :], src[:, t, :]).then_inc(st, 1)
            for t in range(T):
                dve.wait_ge(st, t + 1)
                nc.vector.bn_aggr(mv[:, t, :], stats[:, t, :]).then_inc(ag, 1)
            dve.wait_ge(rs, 2)
            for t in range(T):
                nc.vector.tensor_scalar(dst[:, t, :], src[:, t, :], mv[:, t, 0:1], rstd[:, t:t + 1],
                                        ALU.subtract, ALU.mult).then_inc(nm, 1)
            if affine:
                dve.wait_ge(nm, T)
                nc.vector.tensor_tensor(dst[:, :, :], dst[:, :, :], gam[:, None, :].broadcast_to([TR, T, D]),
                                        ALU.mult).then_inc(af, 1)
                dve.wait_ge(af, 1)
                nc.vector.tensor_tensor(dst[:, :, :], dst[:, :, :], bet[:, None, :].broadcast_to([TR, T, D]),
                                        ALU.add).then_inc(af, 1)

        def norm_pool(pool, q):
            st, ag, rs, nm, tp, ev, af = q
            pool.wait_ge(ag, T)
            nc.gpsimd.tensor_scalar(rstd[:, :], mv[:, :, 1], EPS, None, ALU.add).then_inc(rs, 1)
            pool.wait_ge(rs, 1)
            nc.gpsimd.tensor_tensor(rstd[:, :], rstd[:, :], minus_half[:, :], ALU.pow).then_inc(rs, 1)

        def transpose_tensor(pe, q, src, affine):
            st, ag, rs, nm, tp, ev, af = q
            if affine:
                pe.wait_ge(af, 2)
            for t in range(T):
                if not affine:
                    pe.wait_ge(nm, t + 1)
                dst = wide[0][:, t // 4, TR * (t % 4):TR * (t % 4) + TR]
                nc.tensor.transpose(dst, src[:, t, :], ident[0:TR, 0:TR]).then_inc(tp, 1)

        def transpose_copy(act, q):
            st, ag, rs, nm, tp, ev, af = q
            for i in range(2):
                act.wait_ge(tp, 4 * i + 4)
                nc.scalar.copy(xt[:, HALF * i:HALF * i + HALF], wide[0][:, i, 0:HALF]).then_inc(ev, 1)

        def attention(L):
            s = {n: sem(f"a{L}_{n}") for n in (
                "qp", "qs", "qr", "qm", "ql", "qd", "qd0", "kp", "khi", "kres", "kmid", "klo",
                "ctx0", "ctx1", "st0", "st1", "st2", "dz", "mk", "mk0", "mk1", "ci", "cs", "cr", "ca", "cf", "fl", "vp", "vc", "qz", "qc", "p1", "mxd", "fold", "shi", "srs", "smid", "slo",
                "ones", "mt", "mrow", "sc", "ex", "pv", "uc", "ut", "rc", "o", "xo", "ot", "otc", "wo", "xd")}
            q = norm(f"n{L}", None, x_sb, xn, True)
            scale_q = -1.0 / A ** 0.5 if L == 0 else 1.0
            scale_e = 1.0 if L == 0 else 1.0 / D ** 0.5

            NST = TERMS + (1 if L == 0 else 0)

            def wait_mask(pe, b, r, par):
                pe.wait_ge(s[f"mk{par}"], 16 * r + 16 if L == 0 else 16)

            def k_proj(pe, b, r, par, th, free):
                if th == 0:
                    pe.wait_ge(s[f"ctx{par}"], 16 * r + 16)
                if free is not None:
                    pe.wait_ge(*free)
                nc.tensor.matmul(aux[:, 0:TK], w_k[L][:, :], ctx_sb[:, par, TK * th:TK * th + TK],
                                 start=True, stop=True).then_inc(s["kp"], 1)

            def v_proj(pe, b, par, f, free, chunks=range(4)):
                if chunks[0] == 0:
                    pe.wait_ge(*free)
                for c in chunks:
                    k0 = CK * (4 * f + c)
                    i = nc.tensor.matmul(aux[0:CK, P * c:P * c + P], ctx_sb[:, par, k0:k0 + CK], w_v[L][:, :],
                                         start=True, stop=True)
                if chunks[-1] == 3:
                    i.then_inc(s["vp"], 1)

            def max_scores(pe, b, r, par, n, masked):
                th, p = n // PAIRS, n % PAIRS
                if n == 0:
                    pe.wait_ge(s["qz"], b + 1)
                    pe.wait_ge(s["qc"], b + 1)
                if p == 0:
                    pe.wait_ge(s[f"st{th}"], 16 * NST * (b + 1))
                if not (isinstance(b, int) and b == 0 and n < 2):
                    pe.wait_ge(s["mxd"], 24 * b + n - 1)
                cols = slice(TK * th, TK * th + TK)
                rows = MASK_ROW if masked else ROWS
                i = nc.tensor.matmul(bank[n % 2][0:TR, 0:TK], q_cur[0:rows, par, p, :],
                                     k_stack[0:rows, par, p, cols], start=True, stop=not masked)
                if masked:
                    if n == 0:
                        wait_mask(pe, b, r, par)
                    i = nc.tensor.matmul(bank[n % 2][0:TR, 0:TK],
                                         ident_q[:, 0:2, :].rearrange("k h q -> k (h q)"),
                                         mask_sb[:, par, cols], start=False, stop=True)
                i.then_inc(s["p1"], 1)

            def max_rows(pe, b, free):
                pe.wait_ge(s["slo"], b + 1)
                pe.wait_ge(*free)
                rows = aux[SHIFT_ROW:SHIFT_ROW + 3, 0:448].bitcast(BF16)
                for p in range(PAIRS):
                    i = nc.tensor.transpose(rows[:, TR * p:TR * p + TR], m_part[:, p, :], ident_b[0:TR, 0:TR])
                i.then_inc(s["mt"], 1)

            def scores(pe, b, r, par, c, half, masked):
                if c == 0 and half == 0:
                    pe.wait_ge(s["mrow"], b + 1)
                if half == 0 and not (isinstance(b, int) and b == 0 and c < 2):
                    pe.wait_ge(s["ex"], CH * b + c - 1)
                if masked and c == 0 and half == 0:
                    wait_mask(pe, b, r, par)
                rows = MASK_ROW if masked else ROWS
                for n in range(4):
                    p = 4 * half + n
                    i = nc.tensor.matmul(wide[c % 2][0:CK, half, TR * n:TR * n + TR],
                                         k_stack[0:rows, par, p, CK * c:CK * c + CK], q_cur[0:rows, par, p, :],
                                         start=(n == 0), stop=(n == 3 and not masked), skip_group_check=True)
                if masked:
                    i = nc.tensor.matmul(wide[c % 2][0:CK, half, 0:4 * TR], mask_sb[:, par, CK * c:CK * c + CK],
                                         ident_q[:, :, :].rearrange("k h q -> k (h q)"),
                                         start=False, stop=True, skip_group_check=True)
                if half:
                    i.then_inc(s["sc"], 1)

            def weigh(pe, b, par, c, part):
                if part == 0:
                    pe.wait_ge(s["ex"], CH * b + c + 1)
                    if c == 0:
                        pe.wait_ge(s["vc"], 3 * b + 3)
                        if not (isinstance(b, int) and b == 0):
                            pe.wait_ge(s["uc"], b)
                    for j in range(4):
                        nc.tensor.matmul(acc[32 * j:32 * j + 32, 0:3 * S], v_sb[0:CK, par, c, j, 0:32],
                                         e_sb[0:CK, c % 3, 4 * S * j:4 * S * j + 3 * S],
                                         start=(c == 0), stop=(c == CH - 1), skip_group_check=True)
                else:
                    for j in range(4):
                        i = nc.tensor.matmul(acc[32 * j:32 * j + 32, 3 * S:4 * S], v_sb[0:CK, par, c, j, 2:34],
                                             e_sb[0:CK, c % 3, 4 * S * j + 3 * S:4 * S * j + 4 * S],
                                             start=False, stop=(c == CH - 1), skip_group_check=True)
                    i.then_inc(s["pv"], 1)

            SPREAD = (2, 3, 3, 2, 3, 3, 3, 2, 3, 0, 0, 0)
            COMPARE_AT = (2, 3, 5)
            K_AT, V_AT = (0, 7, 9), ((2, 3), (4, 5), (6, 6))

            def pe_batch(pe, b, r, par, first, nxt, nxt2, masked):
                r1 = r + par
                for c in range(CH):
                    n0 = sum(SPREAD[:c])
                    todo = list(range(n0, n0 + SPREAD[c])) if nxt else []

                    def spread():
                        if todo:
                            max_scores(pe, b + 1, r1, 1 - par, todo.pop(0), masked)

                    scores(pe, b, r, par, c, 0, masked)
                    spread()
                    scores(pe, b, r, par, c, 1, masked)
                    for f in range(3) if nxt else ():
                        free = (((s["kres"], 3 * b + 7) if nxt2 else (s["mrow"], b + 1)),
                                (s["vc"], 3 * b + 4), (s["vc"], 3 * b + 5))[f]
                        if c == V_AT[f][0]:
                            v_proj(pe, b + 1, 1 - par, f, free, range(2))
                        if c == V_AT[f][1]:
                            v_proj(pe, b + 1, 1 - par, f, free, range(2, 4))
                    if nxt2 and c in K_AT:
                        th = K_AT.index(c)
                        k_proj(pe, b + 2, r + 1, par, th, (
                            (s["mrow"], b + 1), (s["vc"], 3 * b + 6), (s["kres"], 3 * b + 8))[th])
                    spread()
                    wb, wp, wc = (b, par, c - 1) if c > 0 else (b - 1, 1 - par, CH - 1)
                    if nxt and c == CH - 1:
                        if L == 0 and par == 1 and not (isinstance(r, int) and r == B // 2 - 2):
                            pe.wait_ge(s["fl"], r + 2)
                        max_rows(pe, b + 1, (s["kres"], 3 * b + 9) if nxt2 else (s["vc"], 3 * b + 6))
                    if not (first and c == 0):
                        weigh(pe, wb, wp, wc, 0)
                    spread()
                    if not (first and c == 0):
                        weigh(pe, wb, wp, wc, 1)

            def over_rounds(e, emit, peeled=1):
                last = B // 2 - peeled
                for b in range(2):
                    emit(e, b, 0, b, b == 0, True, True, True)
                with e.Fori(1, last) as i:
                    for par in range(2):
                        emit(e, 2 * i + par, i, par, False, True, True, True)
                for b in range(2 * last, B):
                    emit(e, b, b // 2, b % 2, False, b < B - 1, b < B - 2, b < B - 3)

            def by_mask(pe, emit, count=None):
                if count is not None:
                    pe.wait_ge(s["fl"], count)
                seen = pe.value_load(flag[0:1, 0:1], min_val=0, max_val=1)
                with pe.If(seen > 0):
                    emit(True)
                with pe.Else():
                    emit(False)

            def pe_rounds(pe):
                def emit(masked, r, b, first=False, last=False):
                    for par in range(2):
                        pe_batch(pe, b + par, r, par, first and par == 0, not (last and par == 1), not last, masked)

                def start(masked):
                    for n in range(24):
                        max_scores(pe, 0, 0, 0, n, masked)
                    max_rows(pe, 0, (s["kres"], 6))
                    emit(masked, 0, 0, first=True)

                by_mask(pe, start, 1)
                with pe.Fori(1, B // 2 - 1) as i:
                    by_mask(pe, lambda masked: emit(masked, i, 2 * i))
                by_mask(pe, lambda masked: emit(masked, B // 2 - 1, B - 2, last=True))

            def act_k(act, b, th):
                act.wait_ge(s["kp"], 3 * b + th + 1)
                if not (isinstance(b, int) and b == 0):
                    act.wait_ge(s[f"st{th}"], 16 * NST * b)
                nc.scalar.activation(k_part[0][:, TK * th:TK * th + TK], aux[:, 0:TK], ACT.Identity,
                                     bias=b_k[:, L:L + 1]).then_inc(s["khi"], 1)

            def act_v(act, b, par, f):
                act.wait_ge(s["vp"], 3 * b + f + 1)
                if f == 0 and not (isinstance(b, int) and b < 2):
                    act.wait_ge(s["pv"], CH * (b - 1))
                nc.scalar.copy(v_sb[0:CK, par, 4 * f:4 * f + 4, :, 1:33],
                               aux[0:CK, :].rearrange("p (c j d) -> p c j d", c=4, j=4)).then_inc(s["vc"], 1)

            def act_u(act, b):
                act.wait_ge(s["pv"], CH * b + CH)
                nc.scalar.copy(u_all[:, :, b, :], acc[:, 0:4 * S].rearrange("p (s q) -> p s q", s=4))\
                    .then_inc(s["uc"], 1)

            def act_batch(act, b, r, par, first, nxt, nxt2, nxt3):
                for c in range(CH):
                    act.wait_ge(s["sc"], CH * b + c + 1)
                    if not (isinstance(b, int) and b == 0 and c < 3):
                        act.wait_ge(s["pv"], CH * b + c - 2)
                    nc.scalar.activation(e_sb[0:CK, c % 3, :].rearrange("p (h n) -> p h n", h=2),
                                         wide[c % 2][0:CK, :, 0:448], ACT.Exp, scale=scale_e).then_inc(s["ex"], 1)
                    if c == 0 and not first:
                        act_u(act, b - 1)
                    for f in range(3) if nxt else ():
                        if c == V_AT[f][1]:
                            act_v(act, b + 1, 1 - par, f)
                    if nxt2 and c in K_AT:
                        act_k(act, b + 2, K_AT.index(c))

            def dve_k(dve, b, th):
                cols = slice(TK * th, TK * th + TK)
                dve.wait_ge(s["khi"], 3 * b + th + 1)
                if not (isinstance(b, int) and b == 0):
                    dve.wait_ge(s["klo"], 3 * b + th - 2)
                nc.vector.scalar_tensor_tensor(k_rest[:, th, :], aux[:, 0:TK], b_k[:, L:L + 1], k_part[0][:, cols],
                                               ALU.add, ALU.subtract).then_inc(s["kres"], 1)

            def dve_q(dve, b, par):
                if not (isinstance(b, int) and b < 2):
                    dve.wait_ge(s["sc"], CH * (b - 1))
                nc.vector.tensor_copy(q_cur[0:SHIFT_ROW, par, :, :], q_all[:, :, b, :]).then_inc(s["qc"], 1)

            def dve_max(dve, b, n):
                dve.wait_ge(s["p1"], 24 * b + n + 1)
                nc.vector.tensor_reduce(out=mx[:, n // PAIRS, n % PAIRS:n % PAIRS + 1], in_=bank[n % 2][0:TR, 0:TK],
                                        axis=AX, op=ALU.max).then_inc(s["mxd"], 1)

            def dve_shift(dve, b):
                dve.wait_ge(s["mxd"], 24 * b + 24)
                nc.vector.tensor_reduce(out=m_fold[:, :], in_=mx[:, :, :].rearrange("q t p -> q p t"),
                                        axis=AX, op=ALU.max).then_inc(s["fold"], 1)
                dve.wait_ge(s["fold"], b + 1)
                nc.vector.tensor_scalar(m_part[:, :, 0], m_fold[:, :], -1.0, None, ALU.mult).then_inc(s["shi"], 1)
                dve.wait_ge(s["shi"], b + 1)
                nc.vector.scalar_tensor_tensor(m_rest[:, :], m_fold[:, :], -1.0, m_part[:, :, 0],
                                               ALU.mult, ALU.subtract).then_inc(s["srs"], 1)
                dve.wait_ge(s["srs"], b + 1)
                nc.vector.tensor_copy(m_part[:, :, 1], m_rest[:, :]).then_inc(s["smid"], 1)
                dve.wait_ge(s["smid"], b + 1)
                nc.vector.tensor_tensor(m_part[:, :, 2], m_rest[:, :], m_part[:, :, 1], ALU.subtract)\
                    .then_inc(s["slo"], 1)

            def dve_shift_rows(dve, b, par):
                dve.wait_ge(s["mt"], b + 1)
                nc.vector.tensor_copy(q_cur[SHIFT_ROW:SHIFT_ROW + 3, par, :, :].rearrange("r p n -> r (p n)"),
                                      aux[SHIFT_ROW:SHIFT_ROW + 3, 0:448].bitcast(BF16)).then_inc(s["mrow"], 1)

            def dve_compare(dve, r, th):
                dve.wait_ge(s["cs"], r + 1)
                if not (isinstance(r, int) and r == 0):
                    dve.wait_ge(s["ca"], r)
                nc.vector.tensor_reduce(out=differ[:, th:th + 1], in_=mask_cmp[:, TK * th:TK * th + TK], axis=AX,
                                        op=ALU.max, apply_absolute_value=True).then_inc(s["cr"], 1)

            def dve_differ(dve, r):
                dve.wait_ge(s["cr"], 3 * r + 3)
                nc.vector.tensor_reduce(out=differ[:, 3:4], in_=differ[:, 0:4], axis=AX, op=ALU.max)\
                    .then_inc(s["ca"], 1)

            def dve_flag(dve, r):
                dve.wait_ge(s["cf"], r + 2)
                nc.vector.tensor_scalar(flag[:, :], differ[0:1, 4:5], 0.0, None, ALU.is_gt).then_inc(s["fl"], 1)

            def dve_batch(dve, b, r, par, first, nxt, nxt2, nxt3):
                if nxt:
                    dve_q(dve, b + 1, 1 - par)
                compare = L == 0 and par == 1 and not (isinstance(r, int) and r + 2 >= B // 2)
                for c in range(CH):
                    n0 = sum(SPREAD[:c])
                    for n in range(n0, n0 + SPREAD[c]):
                        if nxt:
                            dve_max(dve, b + 1, n)
                        if nxt2 and n == n0 and c - 1 in K_AT:
                            dve_k(dve, b + 2, K_AT.index(c - 1))
                    if nxt and c == CH - 2:
                        dve_shift(dve, b + 1)
                    if nxt2 and SPREAD[c] == 0 and c - 1 in K_AT:
                        dve_k(dve, b + 2, K_AT.index(c - 1))
                    if compare and c in COMPARE_AT:
                        dve_compare(dve, r + 2, COMPARE_AT.index(c))
                    if compare and c == COMPARE_AT[2] + 1:
                        dve_differ(dve, r + 2)
                    if compare and c == 9:
                        dve_flag(dve, r)
                    if L == 0 and isinstance(b, int) and b == B - 3 and c == 9:
                        dve_flag(dve, r - 1)
                if nxt:
                    dve_shift_rows(dve, b + 1, 1 - par)

            def load_ctx(sp, b, par):
                if not (isinstance(b, int) and b < 2):
                    sp.wait_ge(s["vp"], 3 * (b - 1))
                sp.dma_start(ctx_sb[:, par, :], ctx_t[b]).then_inc(s[f"ctx{par}"], 16)

            def load_mask(sp, b, par):
                if not (isinstance(b, int) and b < 2):
                    sp.wait_ge(s["sc"], CH * (b - 1))
                sp.dma_start(mask_sb[:, par, :], mask0[b] if L == 0 else mask1).then_inc(s[f"mk{par}"], 16)

            def load_compare(sp, r):
                if L == 0:
                    if not (isinstance(r, int) and r == 0):
                        sp.wait_ge(s["cr"], 3 * r)
                    sp.dma_start(mask_cmp[:, :], mask0.rearrange("(r h) q k -> r (h q) k", h=2)[r])\
                        .then_inc(s["ci"], 16)
                    for h in range(2):
                        sp.dma_start(mask_row[S * h:S * h + S, :], mask0[2 * r + h, 0:1, :].broadcast_to([S, S2]))\
                            .then_inc(s["ci"], 16)
                else:
                    for h in range(2):
                        sp.dma_start(mask_cmp[S * h:S * h + S, :], mask1).then_inc(s["ci"], 16)
                    sp.dma_start(mask_row[:, :], mask1[0:1, :].broadcast_to([2 * S, S2])).then_inc(s["ci"], 16)

            def stack(sp, b, par, th):
                sp.wait_ge(s["klo"], 3 * b + th + 1)
                cols = slice(TK * th, TK * th + TK)
                for t in range(TERMS):
                    sp.dma_start(k_stack[16 * t:16 * t + 16, par, :, cols],
                                 k_part[K_PART[t]][:, cols]).then_inc(s[f"st{th}"], 16)
                if L == 0:
                    sp.dma_start(k_stack[MASK_ROW:ROWS, par, :, cols],
                                 mask_scratch[b][:, None, cols].broadcast_to([3, PAIRS, TK])).then_inc(s[f"st{th}"], 16)

            def sp_batch(sp, b, r, par, first, nxt, nxt2, nxt3):
                if L == 0 and nxt:
                    load_mask(sp, b + 1, 1 - par)
                if nxt3:
                    load_ctx(sp, b + 3, 1 - par)
                if L == 0 and par == 0 and not (isinstance(r, int) and r + 2 >= B // 2):
                    load_compare(sp, r + 2)
                if nxt2:
                    stack(sp, b + 2, par, 0)
                if nxt2:
                    stack(sp, b + 2, par, 1)
                if nxt2:
                    stack(sp, b + 2, par, 2)

            with nc.Block() as block:
                @block.sync
                def _(sp):
                    load_ctx(sp, 0, 0)
                    if L == 0:
                        sp.wait_ge(const, CONST)
                    for par in range(2):
                        sp.dma_start(k_stack[SHIFT_ROW:MASK_ROW, par, :, :].rearrange("r p (j k) -> r (p j) k", j=MJ),
                                     ones_b[:, None, :].broadcast_to([3, PAIRS * MJ, MK])).then_inc(s["ones"], 16)
                    if L == 0:
                        sp.wait_ge(mr_split, 4)
                        for i in range(3):
                            sp.dma_start(mask_scratch[:, i, :].rearrange("b (j k) -> b j k", j=MJ), mr_part[i])\
                                .then_inc(mask_out, 16)
                    load_ctx(sp, 1, 1)
                    load_compare(sp, 0)
                    load_mask(sp, 0, 0)
                    if L == 1:
                        load_mask(sp, 1, 1)
                        for par in range(2):
                            sp.dma_start(k_stack[MASK_ROW:ROWS, par, :, :],
                                         mask_scratch[B][:, None, :].broadcast_to([3, PAIRS, S2]))\
                                .then_inc(s["mk"], 16)
                    else:
                        load_compare(sp, 1)
                        sp.wait_ge(mask_out, 48)
                    stack(sp, 0, 0, 0)
                    sp.wait_ge(s["ql"], 1)
                    if L == 0:
                        sp.wait_ge(zeroed, 1)
                    for t in range(TERMS):
                        for h2 in range(2):
                            r = 16 * t + A * h2
                            sp.dma_start(
                                q_all[r:r + A, :, :, S * h2:S * h2 + S].rearrange("a p b q -> a (p b) q"),
                                q_part[Q_PART[t]][64 * h2:64 * h2 + 64, :].rearrange("n (b q) -> n b q", b=B),
                            ).then_inc(s["qd"], 16)
                    for b in range(2):
                        for th in range(TH):
                            if b or th:
                                stack(sp, b, b, th)
                    if L == 0:
                        for dst, src in late:
                            sp.dma_start(dst[:, :], src).then_inc(w_late, 16)
                    load_ctx(sp, 2, 0)
                    over_rounds(sp, sp_batch, 2)
                    for par in range(2):
                        sp.wait_ge(s[f"mk{par}"], 16 * (B // 2 if L == 0 else 1))

                @block.gpsimd
                def _(pool):
                    if L == 0:
                        pool.wait_ge(const, CONST)
                        nc.gpsimd.memset(q_all[:, :, :, :].rearrange("r p b n -> r (p b n)").bitcast(F32), 0.0)\
                            .then_inc(zeroed, 1)
                        pool.wait_ge(zeroed, 1)
                    norm_pool(pool, q)

                    def no_shift(b, par):
                        if not (isinstance(b, int) and b < 2):
                            pool.wait_ge(s["klo"], 3 * b + 2)
                            pool.wait_ge(s["sc"], CH * (b - 1))
                        elif b == 1:
                            pool.wait_ge(s["qz"], 1)
                        zero = one[SHIFT_ROW:MASK_ROW, 0:PAIRS * S].rearrange("r (p n) -> r p n", p=PAIRS)
                        nc.gpsimd.tensor_tensor(q_cur[SHIFT_ROW:MASK_ROW, par, :, :].bitcast(F32), zero, zero,
                                                ALU.subtract).then_inc(s["qz"], 1)

                    def lo(b, th):
                        cols = slice(TK * th, TK * th + TK)
                        if not (isinstance(b, int) and b < 2):
                            pool.wait_ge(s["sc"], CH * (b - 2) + 4 * th + 4)
                        pool.wait_ge(s["kres"], 3 * b + th + 1)
                        if not (isinstance(b, int) and b == 0):
                            pool.wait_ge(s[f"st{th}"], 16 * NST * b)
                        nc.gpsimd.tensor_tensor(k_part[1][:, cols], k_rest[:, th, :], one[:, :], ALU.mult)\
                            .then_inc(s["kmid"], 1)
                        pool.wait_ge(s["kmid"], 3 * b + th + 1)
                        nc.gpsimd.tensor_tensor(k_part[2][:, cols], k_rest[:, th, :], k_part[1][:, cols],
                                                ALU.subtract).then_inc(s["klo"], 1)

                    def against_row(r):
                        pool.wait_ge(s["ci"], 48 * r + 48)
                        nc.gpsimd.tensor_tensor(mask_cmp[:, :], mask_cmp[:, :], mask_row[:, :], ALU.subtract)\
                            .then_inc(s["cs"], 1)

                    def over_partitions():
                        nc.gpsimd.partition_all_reduce(differ[:, 4:5], differ[:, 3:4], 2 * S, RMAX)\
                            .then_inc(s["cf"], 1)

                    def pool_batch(pool, b, r, par, first, nxt, nxt2, nxt3):
                        compare = L == 0 and not (isinstance(r, int) and r + 2 >= B // 2)
                        for th in range(TH):
                            if compare and par == 1 and th == 0:
                                pool.wait_ge(s["ca"], r + 3)
                            if nxt2:
                                if th == 2:
                                    no_shift(b + 2, par)
                                    pool.wait_ge(s["qz"], b + 3)
                                lo(b + 2, th)
                            if compare and par == 1 and th == 0:
                                over_partitions()
                        if compare and par == 0:
                            against_row(r + 2)

                    pool.wait_ge(q[2], 2)
                    for b in range(2):
                        no_shift(b, b)
                    pool.wait_ge(s["qz"], 2)
                    for th in range(TH):
                        lo(0, th)
                    against_row(0)
                    if L == 0:
                        against_row(1)
                    pool.wait_ge(s["ca"], 2 if L == 0 else 1)
                    over_partitions()
                    for th in range(TH):
                        lo(1, th)
                    over_rounds(pool, pool_batch, 2)

                @block.scalar
                def _(act):
                    if L == 0:
                        act.wait_ge(w_in, W_IN)
                        act.wait_ge(const, CONST)
                        act.wait_ge(tg_in, 16)
                        nc.scalar.activation(tg[:, :], tg[:, :], ACT.Tanh).then_inc(tg_done, 1)
                    act_k(act, 0, 0)
                    transpose_copy(act, q)
                    act_k(act, 0, 1)
                    for i in range(2):
                        act.wait_ge(s["qp"], i + 1)
                        if L == 0:
                            act.wait_ge(s["qs"], 1)
                            nc.scalar.activation(q_f[:, HALF * i:HALF * i + HALF], wide[1][:, i, 0:HALF],
                                                 ACT.Identity, bias=b_q[:, 0:1], scale=scale_q).then_inc(s["qs"], 1)
                        else:
                            nc.scalar.copy(q_f[:, HALF * i:HALF * i + HALF], wide[1][:, i, 0:HALF])\
                                .then_inc(s["qs"], 1)
                    act_k(act, 0, 2)
                    for f in range(3):
                        act_v(act, 0, 0, f)
                    for th in range(TH):
                        act_k(act, 1, th)
                    over_rounds(act, act_batch)
                    act_u(act, B - 1)
                    if L == 1:
                        for i in range(2):
                            act.wait_ge(s["ot"], 4 * i + 4)
                            nc.scalar.copy(xt[:, HALF * i:HALF * i + HALF], wide[1][:, i, 0:HALF])\
                                .then_inc(s["otc"], 1)

                @block.vector
                def _(dve):
                    if L == 0:
                        dve.wait_ge(w_in, W_IN)
                        dve.wait_ge(const, CONST)
                        nc.vector.tensor_scalar(b_q[:, :], b_q[:, :], scale_q, None, ALU.mult).then_inc(s["qs"], 1)
                    nc.vector.memset(differ[:, :], 0.0).then_inc(s["dz"], 1)
                    if L == 0:
                        dve.wait_ge(mr_in, 32)
                        nc.vector.tensor_copy(mr_part[0], m_row[:, :]).then_inc(mr_split, 1)
                        dve.wait_ge(mr_split, 1)
                        nc.vector.tensor_tensor(m_left[:, :], m_row[:, :], mr_part[0], ALU.subtract).then_inc(mr_split, 1)
                        dve.wait_ge(mr_split, 2)
                        nc.vector.tensor_copy(mr_part[1], m_left[:, :]).then_inc(mr_split, 1)
                        dve.wait_ge(mr_split, 3)
                        nc.vector.tensor_tensor(mr_part[2], m_left[:, :], mr_part[1], ALU.subtract).then_inc(mr_split, 1)
                    norm_vector(dve, q, x_sb, xn, False)
                    dve_k(dve, 0, 0)
                    dve_k(dve, 0, 1)
                    dve.wait_ge(s["qs"], 3 if L == 0 else 2)
                    nc.vector.tensor_copy(q_part[0][:, :], q_f[:, :]).then_inc(s["qr"], 1)
                    dve.wait_ge(s["qr"], 1)
                    nc.vector.tensor_tensor(q_rest[:, :], q_f[:, :], q_part[0][:, :], ALU.subtract)\
                        .then_inc(s["qr"], 1)
                    dve.wait_ge(s["qr"], 2)
                    nc.vector.tensor_copy(q_part[1][:, :], q_rest[:, :]).then_inc(s["qm"], 1)
                    dve.wait_ge(s["qm"], 1)
                    nc.vector.tensor_tensor(q_part[2][:, :], q_rest[:, :], q_part[1][:, :], ALU.subtract)\
                        .then_inc(s["ql"], 1)
                    dve_k(dve, 0, 2)
                    dve.wait_ge(s["dz"], 1)
                    for r in range(2 if L == 0 else 1):
                        for th in range(TH):
                            dve_compare(dve, r, th)
                        dve_differ(dve, r)
                    dve_flag(dve, -1)
                    for th in range(TH):
                        dve_k(dve, 1, th)
                    dve.wait_ge(s["qd"], 16 * 12)
                    dve_q(dve, 0, 0)
                    for n in range(24):
                        dve_max(dve, 0, n)
                    dve_shift(dve, 0)
                    dve_shift_rows(dve, 0, 0)
                    over_rounds(dve, dve_batch, 2)
                    for g in range(2):
                        dve.wait_ge(s["ut"], 16 * g + 16)
                        for t4 in range(4):
                            t = 4 * g + t4
                            src = post[t4][0:TR, :].rearrange("r (s j n) -> r s j n", s=4, j=4)
                            nc.vector.reciprocal(rec[:, t, 0:3, :], src[:, 0:3, :, 0]).then_inc(s["rc"], 1)
                            nc.vector.reciprocal(rec[:, t, 3, :], src[:, 3, :, 31]).then_inc(s["rc"], 1)
                        for t4 in range(4):
                            t = 4 * g + t4
                            src = post[t4][0:TR, :].rearrange("r (s j n) -> r s j n", s=4, j=4)
                            dve.wait_ge(s["rc"], 2 * t + 2)
                            for k in range(4):
                                r0 = 1 + A * k if k < 3 else 23
                                o = xn[:, t, :].rearrange("r (j k a) -> r j k a", j=4, k=4)[:, :, k, :]
                                nc.vector.tensor_tensor(o, src[:, k, :, r0:r0 + A],
                                                        rec[:, t, k, :, None].broadcast_to([TR, 4, A]), ALU.mult)\
                                    .then_inc(s["o"], 1)
                    if L == 0:
                        dve.wait_ge(s["o"], 32)
                        dve.wait_ge(w_late, W_LATE)
                        dve.wait_ge(tg_done, 1)
                        nc.vector.tensor_tensor(xn[:, :, :], xn[:, :, :], b_v[:, None, :].broadcast_to([TR, T, D]),
                                                ALU.add).then_inc(s["xo"], 1)
                        dve.wait_ge(s["xo"], 1)
                        nc.vector.scalar_tensor_tensor(
                            x_sb[:, :, :].rearrange("r t d -> r (t d)"), xn[:, :, :].rearrange("r t d -> r (t d)"),
                            tg[0:TR, 0:1], x_sb[:, :, :].rearrange("r t d -> r (t d)"), ALU.mult, ALU.add)\
                            .then_inc(s["xd"], 1)
                        dve.wait_ge(s["xd"], 1)
                    else:
                        for i in range(2):
                            dve.wait_ge(s["wo"], 4 * i + 4)
                            v = x_sb[:, 4 * i:4 * i + 4, :].rearrange("r t d -> r (t d)")
                            nc.vector.scalar_tensor_tensor(v, wide[0][0:TR, i, :], tg[0:TR, 1:2], v,
                                                           ALU.mult, ALU.add).then_inc(s["xd"], 1)
                        dve.wait_ge(s["xd"], 2)

                @block.tensor
                def _(pe):
                    if L == 0:
                        pe.wait_ge(w_in, W_IN)
                        pe.wait_ge(const, CONST)
                    k_proj(pe, 0, 0, 0, 0, None)
                    transpose_tensor(pe, q, xn, False)
                    k_proj(pe, 0, 0, 0, 1, (s["kres"], 1))
                    for i in range(2):
                        pe.wait_ge(q[5], i + 1)
                        nc.tensor.matmul(wide[1][:, i, 0:HALF], w_q[L][:, :], xt[:, HALF * i:HALF * i + HALF],
                                         start=True, stop=True).then_inc(s["qp"], 1)
                    k_proj(pe, 0, 0, 0, 2, (s["kres"], 2))
                    for f in range(3):
                        v_proj(pe, 0, 0, f, (s["kres"], 3) if f == 0 else (s["vc"], f))
                    for th in range(TH):
                        k_proj(pe, 1, 0, 1, th, (s["kres"], 3 + th) if th else (s["vc"], 3))
                    pe.wait_ge(s["ones"], 32)
                    if L == 1:
                        pe.wait_ge(s["mk"], 32)
                    pe_rounds(pe)
                    for part in range(2):
                        weigh(pe, B - 1, 1, CH - 1, part)
                    pe.wait_ge(s["ex"], CH * B)
                    pe.wait_ge(s["uc"], B)
                    for t in range(T):
                        if t >= 4:
                            pe.wait_ge(s["o"], 4 * (t - 4) + 4)
                        for k in range(4):
                            nc.tensor.transpose(post[t % 4][0:TR, P * k:P * k + P],
                                                u_all[:, k, 2 * t:2 * t + 2, :].rearrange("p b q -> p (b q)"),
                                                ident[:, :]).then_inc(s["ut"], 1)
                    if L == 1:
                        for t in range(T):
                            pe.wait_ge(s["o"], 4 * t + 4)
                            nc.tensor.transpose(wide[1][:, t // 4, TR * (t % 4):TR * (t % 4) + TR], xn[:, t, :],
                                                ident[0:TR, 0:TR]).then_inc(s["ot"], 1)
                        for t in range(T):
                            pe.wait_ge(s["otc"], t // 4 + 1)
                            nc.tensor.matmul(wide[0][0:TR, t // 4, P * (t % 4):P * (t % 4) + P],
                                             xt[:, TR * t:TR * t + TR], w_o[:, :], start=True, stop=True)\
                                .then_inc(s["wo"], 1)


        def experts(L):
            s = {n: sem(f"f{L}_{n}") for n in (
                "ch", "lg", "ex", "g", "gt", "gtc", "gs", "w10", "w11", "w20", "w21", "gb0", "gb1", "hp", "gelu", "hg", "yp",
                "yc", "yt", "xd", "out")}
            fw1, fb1, fw2 = (fw1_0, fb1_0, fw2_0) if L == 0 else (fw1_1, fb1_1, fw2_1)
            q0 = norm(f"m{L}", None, None, None, False)
            q1 = norm("mm", None, None, None, True) if L == 1 else q0
            U = 2 * FC
            LAG = 2
            chain = [0]

            def over_experts(e, emit):
                for n in range(2):
                    emit(e, n, 0, n, n == 0, False)
                with e.Fori(1, E // 2 - 1) as i:
                    for par in range(2):
                        emit(e, 2 * i + par, i, par, False, False)
                for n in range(E - 2, E):
                    emit(e, n, n // 2, n % 2, False, n == E - 1)

            def early(n, k):
                return isinstance(n, int) and n < k

            def load(sp, e, par):
                if not early(e, 2):
                    sp.wait_ge(s["hp"], U * (e - 1))
                sp.dma_start(w1_sb[:, par, :], fw1[e]).then_inc(s[f"w1{par}"], 16)
                if not early(e, 2):
                    sp.wait_ge(s["gelu"], U * (e - 1))
                sp.dma_start(b1_sb[:, par, :], fb1[e]).then_inc(s[f"w1{par}"], 16)
                if not early(e, 2):
                    sp.wait_ge(s["yp"], U * (e - 1))
                sp.dma_start(w2_sb[:, par, :, :], fw2[e]).then_inc(s[f"w2{par}"], 16)

            def load_gates(sp, e, par):
                if not early(e, 2):
                    sp.wait_ge(s["hg"], U * (e - 1))
                sp.dma_start(gate_b[:, par, :], gate_scratch[L, e][None, :].broadcast_to([P, NTOK]))\
                    .then_inc(s[f"gb{par}"], 16)

            def hidden(pe, e, r, par, u):
                n = U * e + u
                if u == 0:
                    pe.wait_ge(s[f"w1{par}"], 32 * r + 32)
                if not early(n, 4):
                    pe.wait_ge(s["gelu"], n - 3)
                fc, half = u // 2, u % 2
                nc.tensor.matmul(bank[u % 4][:, 0:HALF], w1_sb[:, par, P * fc:P * fc + P],
                                 xt[:, HALF * half:HALF * half + HALF], start=True, stop=True).then_inc(s["hp"], 1)

            def back(pe, e, r, par, u, last):
                n = U * e + u
                if u == 0:
                    pe.wait_ge(s[f"w2{par}"], 16 * r + 16)
                pe.wait_ge(s["hg"], n + 1)
                fc, half = u // 2, u % 2
                nc.tensor.matmul(wide[1][:, half, 0:HALF], w2_sb[:, par, fc, :], hg_sb[:, u % 4, :],
                                 start=False, stop=last and fc == FC - 1, skip_group_check=True)\
                    .then_inc(s["yp"], 1)

            def pe_expert(pe, e, r, par, first, last):
                for u in range(U):
                    if u + LAG < U:
                        hidden(pe, e, r, par, u + LAG)
                    elif not last:
                        hidden(pe, e + 1, r + par, 1 - par, u + LAG - U)
                    back(pe, e, r, par, u, last)

            def act_expert(act, e, r, par, first, last):
                for u in range(U):
                    n = U * e + u
                    act.wait_ge(s["hp"], n + 1)
                    if not early(n, 4):
                        act.wait_ge(s["hg"], n - 3)
                    nc.scalar.activation(h_sb[:, u % 4, :], bank[u % 4][:, 0:HALF],
                                         ACT.Gelu if L == 0 else ACT.Gelu_apprx_tanh,
                                         bias=b1_sb[:, par, u // 2:u // 2 + 1]).then_inc(s["gelu"], 1)

            def dve_expert(dve, e, r, par, first, last):
                dve.wait_ge(s[f"gb{par}"], 16 * r + 16)
                for u in range(U):
                    n = U * e + u
                    dve.wait_ge(s["gelu"], n + 1)
                    if not early(n, 4):
                        dve.wait_ge(s["yp"], n - 3)
                    half = u % 2
                    nc.vector.tensor_tensor(hg_sb[:, u % 4, :], h_sb[:, u % 4, :],
                                            gate_b[:, par, HALF * half:HALF * half + HALF], ALU.mult)\
                        .then_inc(s["hg"], 1)

            def sp_expert(sp, e, r, par, first, last):
                load(sp, e, par)
                load_gates(sp, e, par)

            def over_tokens(v):
                return v[:, :, None].broadcast_to([TR, T, E])

            with nc.Block() as block:
                @block.sync
                def _(sp):
                    sp.wait_ge(s["gtc"], 2)
                    sp.dma_start(gate_scratch[L], g_t[:, :]).then_inc(s["gs"], 16)
                    sp.wait_ge(s["gs"], 16)
                    over_experts(sp, sp_expert)
                    if L == 1:
                        for i in range(2):
                            sp.wait_ge(s["xd"], i + 1)
                            sp.dma_start(out[HALF * i:HALF * i + HALF, :].rearrange("(t r) d -> r t d", r=TR),
                                         x_sb[:, 4 * i:4 * i + 4, :]).then_inc(s["out"], 16)
                        sp.wait_ge(s["out"], 32)

                @block.gpsimd
                def _(pool):
                    norm_pool(pool, q0)
                    if L == 1:
                        pool.wait_ge(q0[2], 2)
                        pool.wait_ge(q0[3], T)
                        norm_pool(pool, q1)

                @block.tensor
                def _(pe):
                    transpose_tensor(pe, q1, xn, L == 1)
                    for t in range(T):
                        pe.wait_ge(q1[5], t // 4 + 1)
                        i = nc.tensor.matmul(aux[0:TR, E * t:E * t + E], xt[:, TR * t:TR * t + TR], w_r[L][:, :],
                                             start=True, stop=True)
                    i.then_inc(s["lg"], 1)
                    pe.wait_ge(s["g"], 1)
                    for t in range(T):
                        nc.tensor.transpose(wide[0][0:E, t // 4, TR * (t % 4):TR * (t % 4) + TR],
                                            lg[:, 7, t, :], ident[0:TR, 0:TR]).then_inc(s["gt"], 1)
                    pe.wait_ge(s["gtc"], 2)
                    for i in range(2):
                        nc.tensor.matmul(wide[1][:, i, 0:HALF], fb2[L][:, :], g_t[:, HALF * i:HALF * i + HALF],
                                         start=True, stop=False, skip_group_check=True)
                    for u in range(LAG):
                        hidden(pe, 0, 0, 0, u)
                    over_experts(pe, pe_expert)
                    for t in range(T):
                        pe.wait_ge(s["yc"], t // 4 + 1)
                        nc.tensor.transpose(wide[0][0:TR, t // 4, P * (t % 4):P * (t % 4) + P],
                                            y_t[:, TR * t:TR * t + TR], ident[:, :]).then_inc(s["yt"], 1)

                @block.scalar
                def _(act):
                    transpose_copy(act, q1)
                    act.wait_ge(s["ch"], 3)
                    nc.scalar.activation(lg[:, 2, :, :], lg[:, 1, :, :], ACT.Exp).then_inc(s["ex"], 1)
                    for i in range(2):
                        act.wait_ge(s["gt"], 4 * i + 4)
                        nc.scalar.copy(g_t[:, HALF * i:HALF * i + HALF], wide[0][0:E, i, 0:HALF])\
                            .then_inc(s["gtc"], 1)
                    over_experts(act, act_expert)
                    act.wait_ge(s["yp"], U * E)
                    for i in range(2):
                        nc.scalar.copy(y_t[:, HALF * i:HALF * i + HALF], wide[1][:, i, 0:HALF])\
                            .then_inc(s["yc"], 1)

                @block.vector
                def _(dve):
                    def link(ins):
                        chain[0] += 1
                        ins.then_inc(s["ch"], 1)
                        dve.wait_ge(s["ch"], chain[0])

                    def first_of(eq, best, tie_of, to):
                        link(nc.vector.tensor_tensor(lg[:, eq, :, :], lg[:, eq, :, :],
                                                     tie[:, None, :].broadcast_to([TR, T, E]), ALU.mult))
                        link(nc.vector.tensor_reduce(out=ls[:, best, :], in_=lg[:, eq, :, :], axis=AX, op=ALU.max))
                        link(nc.vector.tensor_tensor(lg[:, to, :, :], lg[:, eq, :, :], over_tokens(ls[:, best, :]),
                                                     ALU.is_equal))

                    if L == 0:
                        norm_vector(dve, q0, x_sb, xn, False)
                    else:
                        norm_vector(dve, q0, x_sb, resid, False)
                        dve.wait_ge(q0[3], T)
                        norm_vector(dve, q1, resid, xn, True)
                    dve.wait_ge(s["lg"], 1)
                    logits = aux[0:TR, 0:T * E].rearrange("r (t e) -> r t e", t=T)
                    if L == 0:
                        link(nc.vector.tensor_tensor(lg[:, 0, :, :], logits,
                                                     b_r[:, None, :].broadcast_to([TR, T, E]), ALU.add))
                    else:
                        link(nc.vector.tensor_copy(lg[:, 0, :, :], logits))
                    link(nc.vector.tensor_reduce(out=ls[:, 0, :], in_=lg[:, 0, :, :], axis=AX, op=ALU.max))
                    link(nc.vector.tensor_tensor(lg[:, 1, :, :], lg[:, 0, :, :], over_tokens(ls[:, 0, :]),
                                                 ALU.subtract))
                    dve.wait_ge(s["ex"], 1)
                    link(nc.vector.tensor_reduce(out=ls[:, 1, :], in_=lg[:, 2, :, :], axis=AX, op=ALU.add))
                    link(nc.vector.reciprocal(ls[:, 2, :], ls[:, 1, :]))
                    if L == 0:
                        link(nc.vector.tensor_tensor(lg[:, 3, :, :], lg[:, 0, :, :], over_tokens(ls[:, 0, :]),
                                                     ALU.is_equal))
                        first_of(3, 3, tie, 4)
                        nc.vector.tensor_tensor(lg[:, 7, :, :], lg[:, 4, :, :], over_tokens(ls[:, 2, :]),
                                                ALU.mult).then_inc(s["g"], 1)
                    else:
                        link(nc.vector.tensor_tensor(lg[:, 3, :, :], lg[:, 2, :, :], over_tokens(ls[:, 2, :]),
                                                     ALU.mult))
                        link(nc.vector.tensor_reduce(out=ls[:, 3, :], in_=lg[:, 3, :, :], axis=AX, op=ALU.max))
                        link(nc.vector.tensor_tensor(lg[:, 4, :, :], lg[:, 3, :, :], over_tokens(ls[:, 3, :]),
                                                     ALU.is_equal))
                        first_of(4, 4, tie, 5)
                        link(nc.vector.tensor_scalar(lg[:, 6, :, :], lg[:, 5, :, :], -4.0, None, ALU.mult))
                        link(nc.vector.tensor_tensor(lg[:, 3, :, :], lg[:, 3, :, :], lg[:, 6, :, :], ALU.add))
                        link(nc.vector.tensor_reduce(out=ls[:, 5, :], in_=lg[:, 3, :, :], axis=AX, op=ALU.max))
                        link(nc.vector.tensor_tensor(lg[:, 4, :, :], lg[:, 3, :, :], over_tokens(ls[:, 5, :]),
                                                     ALU.is_equal))
                        first_of(4, 4, tie, 6)
                        link(nc.vector.tensor_tensor(ls[:, 6, :], ls[:, 3, :], ls[:, 5, :], ALU.add))
                        link(nc.vector.tensor_scalar(ls[:, 6, :], ls[:, 6, :], 1e-9, None, ALU.add))
                        link(nc.vector.reciprocal(ls[:, 7, :], ls[:, 6, :]))
                        link(nc.vector.tensor_tensor(ls[:, 3, :], ls[:, 3, :], ls[:, 7, :], ALU.mult))
                        link(nc.vector.tensor_tensor(ls[:, 5, :], ls[:, 5, :], ls[:, 7, :], ALU.mult))
                        link(nc.vector.tensor_tensor(lg[:, 5, :, :], lg[:, 5, :, :], over_tokens(ls[:, 3, :]),
                                                     ALU.mult))
                        link(nc.vector.tensor_tensor(lg[:, 6, :, :], lg[:, 6, :, :], over_tokens(ls[:, 5, :]),
                                                     ALU.mult))
                        nc.vector.tensor_tensor(lg[:, 7, :, :], lg[:, 5, :, :], lg[:, 6, :, :], ALU.add)\
                            .then_inc(s["g"], 1)
                    over_experts(dve, dve_expert)
                    for i in range(2):
                        dve.wait_ge(s["yt"], 4 * i + 4)
                        y = wide[0][0:TR, i, :]
                        v = x_sb[:, 4 * i:4 * i + 4, :].rearrange("r t d -> r (t d)")
                        if L == 1:
                            r = resid[:, 4 * i:4 * i + 4, :].rearrange("r t d -> r (t d)")
                            link(nc.vector.tensor_tensor(r, y, r, ALU.add))
                            y = r
                        nc.vector.scalar_tensor_tensor(v, y, tg[0:TR, 2 + L:3 + L], v, ALU.mult, ALU.add)\
                            .then_inc(s["xd"], 1)
                    dve.wait_ge(s["xd"], 2)

        attention(0)
        experts(0)
        nc.all_engine_barrier()
        nc.clear_and_free_semaphores(made)
        nc.all_engine_barrier()
        attention(1)
        experts(1)


def kernel(x, ctx_1024, mask_BxSxS2_ff0, mask_SxS2_fk0, g_xattn, g_ffn, L0_xattn_Wq, L0_xattn_bq, L0_xattn_Wk,
           L0_xattn_bk, L0_xattn_Wv, L0_xattn_bv, L0_ffn_W1, L0_ffn_b1, L0_ffn_W2, L0_ffn_b2, L0_ffn_Wr, L0_ffn_br,
           L1_xattn_Wq, L1_xattn_Wkv, L1_xattn_Wout, L1_ffn_gamma, L1_ffn_beta, L1_ffn_Wg, L1_ffn_W1, L1_ffn_b1,
           L1_ffn_W2, L1_ffn_b2):
    import numpy as np
    import concourse.bacc as bacc
    from concourse.bass_utils import run_bass_kernel_spmd

    def by_pair(w):
        return np.asarray(w).reshape(PAIRS, 2, A, -1).transpose(1, 2, 0, 3).reshape(D, -1)

    def turned(w):
        return np.ascontiguousarray(np.asarray(w).T)

    def row(v):
        return np.asarray(v).reshape(1, -1)

    def chunks(v):
        return np.asarray(v).reshape(E, FC, P).transpose(0, 2, 1)

    def chunked_rows(w):
        return np.asarray(w).reshape(E, FC, P, D).transpose(0, 2, 1, 3)

    wkv = np.asarray(L1_xattn_Wkv)
    arrays = {
        "x": np.asarray(x).reshape(NTOK, D),
        "ctx_t": np.asarray(ctx_1024).transpose(0, 2, 1),
        "mask0": mask_BxSxS2_ff0, "mask1": mask_SxS2_fk0,
        "gates_in": row(np.concatenate([np.asarray(g_xattn), np.asarray(g_ffn)])),
        "ident_in": np.eye(P, dtype=np.float32),
        "tie_in": row(np.arange(E, 0, -1, dtype=np.float32)),
        "wq0": turned(by_pair(L0_xattn_Wq)), "bq0": by_pair(L0_xattn_bq),
        "wk0": turned(by_pair(L0_xattn_Wk)),
        "bk0": np.concatenate([by_pair(L0_xattn_bk), np.zeros((D, 1), np.float32)], axis=1),
        "wv0": turned(L0_xattn_Wv), "bv0": row(L0_xattn_bv),
        "wq1": turned(by_pair(L1_xattn_Wq)), "wk1": turned(by_pair(wkv[:D])), "wv1": turned(wkv[D:]),
        "wo1": turned(L1_xattn_Wout),
        "fw1_0": L0_ffn_W1, "fb1_0": chunks(L0_ffn_b1), "fw2_0": chunked_rows(L0_ffn_W2), "fb2_0": L0_ffn_b2,
        "wr0": L0_ffn_Wr, "br0": row(L0_ffn_br),
        "gamma": row(L1_ffn_gamma), "beta": row(L1_ffn_beta),
        "fw1_1": L1_ffn_W1, "fb1_1": chunks(L1_ffn_b1), "fw2_1": chunked_rows(L1_ffn_W2), "fb2_1": L1_ffn_b2,
        "wr1": turned(L1_ffn_Wg),
    }
    nc = bacc.Bacc("TRN2", target_bir_lowering=False, num_devices=1)
    feeds, args = {}, {}
    for name, a in arrays.items():
        a = np.ascontiguousarray(a)
        feeds[f"in_{name}"] = a
        args[name] = nc.dram_tensor(f"in_{name}", a.shape, mybir.dt.from_np(a.dtype), kind="ExternalInput").ap()
    args["out"] = nc.dram_tensor("out_x", (NTOK, D), F32, kind="ExternalOutput").ap()
    build(nc, **args)
    got = run_bass_kernel_spmd(nc, [feeds], core_ids=[0])
    return got.results[0]["out_x"].reshape(B, S, D)
```

```python
from contextlib import ExitStack

import concourse.bass as bass
from concourse import mybir

ALU = mybir.AluOpType
ACT = mybir.ActivationFunctionType
AX = mybir.AxisListType.X
RMAX = bass.bass_isa.ReduceOp.max
F32 = mybir.dt.float32
BF16 = mybir.dt.bfloat16
I32 = mybir.dt.int32

P = 128
B, S, D = 16, 56, 128
S2 = 1500
H, A = 16, 8
PAIRS = H // 2
CH, CK = 12, 125
TH, TK = 3, 500
HQ = H * S
MJ, MK = 6, 250
T, TR = 8, 112
NTOK = B * S
HALF = NTOK // 2
E, F = 8, 512
FC = F // P
EPS = 1e-5
MASK_BIG = 1e3
TERMS = 6
K_PART = (0, 0, 0, 1, 1, 2)
Q_PART = (0, 1, 2, 0, 1, 0)
SHIFT_ROW = TERMS * 2 * A
MASK_ROW = SHIFT_ROW + 3
ROWS = MASK_ROW + 3


def build(nc, x, ctx_t, mask0, mask1, gates_in, ident_in, tie_in,
          wq0, bq0, wk0, bk0, wv0, bv0, wq1, wk1, wv1, wo1,
          fw1_0, fb1_0, fw2_0, fb2_0, wr0, br0,
          gamma, beta, fw1_1, fb1_1, fw2_1, fb2_1, wr1, out):
    es = ExitStack()
    with es:
        def sb(name, shape, dt=F32):
            return es.enter_context(nc.sbuf_tensor(name, shape, dt))

        made = []

        def sem(name):
            made.append(nc.alloc_semaphore(name=name))
            return made[-1]

        mask_scratch = nc.dram_tensor("mask_scratch", (B + 1, 3, S2), BF16, kind="Internal").ap()
        gate_scratch = nc.dram_tensor("gate_scratch", (2, E, NTOK), F32, kind="Internal").ap()

        shared = sb("shared", [P, 2 * PAIRS * S2 // 2])
        k_stack = shared[:, :].bitcast(BF16).rearrange("p (b h k) -> p b h k", b=2, h=PAIRS)
        k_part = [sb(n, [P, S2], BF16) for n in ("k_hi", "k_mid", "k_lo")]
        k_rest = sb("k_rest", [P, TH, TK])
        ctx_sb = sb("ctx_sb", [P, 2, S2])
        v_sb = sb("v_sb", [P, 2, CH, 4, 34])
        e_sb = sb("e_sb", [P, 3, HQ])
        q_all = sb("q_all", [SHIFT_ROW, PAIRS, B, 2 * S], BF16)
        q_cur = sb("q_cur", [ROWS, 2, PAIRS, 2 * S], BF16)
        q_max = sb("q_max", [ROWS, PAIRS, 2 * S], BF16)
        q_part = [sb(n, [P, NTOK], BF16) for n in ("q_hi", "q_mid", "q_lo")]
        u_all = sb("u_all", [P, 4, B, S])
        q_f = u_all[:, 0, :, :].rearrange("p b q -> p (b q)")
        q_rest = u_all[:, 1, :, :].rearrange("p b q -> p (b q)")
        mask_sb = sb("mask_sb", [S, 2, S2])
        mask_cmp = sb("mask_cmp", [2 * S, S2])
        mask_row = sb("mask_row", [2 * S, S2])
        mask_first = ctx_sb[0:B, 1, :]
        top = sb("top", [B, 2])
        differ = sb("differ", [2 * S, 5])
        flag = sb("flag", [1, 1], I32)
        ident_q = sb("ident_q", [S, PAIRS, S])
        mx = sb("mx", [TR, TH, PAIRS])
        m_fold = sb("m_fold", [TR, PAIRS])
        m_rest = sb("m_rest", [TR, PAIRS])
        m_part = sb("m_part", [TR, PAIRS, 3], BF16)
        x_sb = sb("x_sb", [TR, T, D])
        xn = sb("xn", [TR, T, D])
        xt = sb("xt", [P, NTOK])
        stats = sb("stats", [TR, T, 6])
        mv = sb("mv", [TR, T, 2])
        rstd = sb("rstd", [TR, T])
        minus_half = sb("minus_half", [TR, T])
        rec = sb("rec", [TR, T, 4, 4])
        ident = sb("ident", [P, P])
        ident_b = sb("ident_b", [P, P], BF16)
        tie = sb("tie", [TR, E])
        tg = sb("tg", [P, 4])
        one = sb("one", [P, TK])
        ones_b = sb("ones_b", [3, MK], BF16)
        w_q = [sb(f"w_q{i}", [P, D]) for i in range(2)]
        w_k = [sb(f"w_k{i}", [P, D]) for i in range(2)]
        w_v = [sb(f"w_v{i}", [P, D]) for i in range(2)]
        w_o = sb("w_o", [P, D])
        w_r = [sb(f"w_r{i}", [P, E]) for i in range(2)]
        b_q = sb("b_q", [P, 1])
        b_k = sb("b_k", [P, 2])
        b_v = sb("b_v", [TR, D])
        b_r = sb("b_r", [TR, E])
        gam = sb("gam", [TR, D])
        bet = sb("bet", [TR, D])
        lg = sb("lg", [TR, 8, T, E])
        ls = sb("ls", [TR, 8, T])
        g_t = sb("g_t", [E, NTOK])
        b1_sb = sb("b1_sb", [P, 2, FC])
        fb2 = [sb(f"fb2{i}", [E, D]) for i in range(2)]

        ff = shared[:, :]
        w1_sb = ff[:, 0:1024].rearrange("p (b f) -> p b f", b=2)
        w2_sb = ff[:, 1024:2048].rearrange("p (b c d) -> p b c d", b=2, c=FC)
        gate_b = ff[:, 2048:2048 + 2 * NTOK].rearrange("p (b n) -> p b n", b=2)
        h_sb = ff[:, 4096:4096 + 4 * HALF].rearrange("p (b n) -> p b n", b=4)
        hg_sb = ff[:, 6144:6144 + 4 * HALF].rearrange("p (b n) -> p b n", b=4)
        resid = ff[0:TR, 10752:10752 + T * D].rearrange("r (t d) -> r t d", t=T)
        y_t = ff[:, 8192:8192 + NTOK]
        m_row = sb("m_row", [MJ * (B + 1), MK])
        m_left = sb("m_left", [MJ * (B + 1), MK])
        mr_part = [sb(f"mr_part{i}", [MJ * (B + 1), MK], BF16)[:, :] for i in range(3)]

        bank = [es.enter_context(nc.psum_tensor(f"bank{i}", [P, 512], F32)) for i in range(4)]
        wide = [es.enter_context(nc.psum_tensor(f"wide{i}", [P, 2, 512], F32)) for i in range(2)]
        acc, aux = bank[2], bank[3]

        w_in, w_late = sem("w_in"), sem("w_late")
        mr_in, mr_split, mask_out = sem("mr_in"), sem("mr_split"), sem("mask_out")
        x_in, const, zeroed, tg_in, tg_done = (sem(n) for n in ("x_in", "const", "zeroed", "tg_in", "tg_done"))
        no_shift, half_set = sem("no_shift"), sem("half_set")
        W_IN = 16 * 5
        late = ((b_v, bv0.broadcast_to([TR, D])), (w_q[1], wq1), (w_k[1], wk1), (w_v[1], wv1), (w_o, wo1),
                (w_r[0], wr0), (w_r[1], wr1), (fb2[0], fb2_0), (fb2[1], fb2_1),
                (b_r, br0.broadcast_to([TR, E])), (gam, gamma.broadcast_to([TR, D])),
                (bet, beta.broadcast_to([TR, D])), (tie, tie_in.broadcast_to([TR, E])))
        W_LATE = 16 * len(late)

        with nc.Block() as block:
            @block.sync
            def _(sp):
                sp.dma_start(x_sb[:, :, :], x.rearrange("(t r) d -> r t d", r=TR)).then_inc(x_in, 16)
                sp.dma_start(ident[:, :], ident_in).then_inc(x_in, 16)
                sp.dma_start(m_row[0:MJ * B, :], mask0[:, 0, :].rearrange("b (j k) -> b j k", j=MJ))\
                    .then_inc(mr_in, 16)
                sp.dma_start(m_row[MJ * B:MJ * (B + 1), :], mask1[0:1, :].rearrange("b (j k) -> b j k", j=MJ))\
                    .then_inc(mr_in, 16)
            @block.scalar
            def _(act):
                for dst, src in ((w_k[0], wk0), (b_k, bk0), (w_q[0], wq0), (b_q, bq0), (w_v[0], wv0)):
                    act.dma_start(dst[:, :], src).then_inc(w_in, 16)
                act.dma_start(tg[:, :], gates_in.broadcast_to([P, 4])).then_inc(tg_in, 16)
            @block.vector
            def _(dve):
                nc.vector.memset(q_cur[SHIFT_ROW:ROWS, :, :, :], 1.0).then_inc(const, 1)
                nc.vector.memset(q_max[SHIFT_ROW:ROWS, :, :], 1.0).then_inc(const, 1)
                nc.vector.memset(ones_b[:, :], 1.0).then_inc(const, 1)
                nc.vector.memset(v_sb[:, :, :, :, 0:1], 1.0).then_inc(const, 1)
                nc.vector.memset(v_sb[:, :, :, :, 33:34], 1.0).then_inc(const, 1)
                nc.vector.memset(one[:, :], 1.0).then_inc(const, 1)
                dve.wait_ge(x_in, 32)
                nc.vector.tensor_copy(ident_b[:, :], ident[:, :]).then_inc(const, 1)
                nc.vector.tensor_copy(ident_q[:, :, :], ident[0:S, None, 0:S].broadcast_to([S, PAIRS, S]))\
                    .then_inc(const, 1)
                dve.wait_ge(const, 2)
                nc.vector.memset(q_max[SHIFT_ROW:MASK_ROW, :, :], 0.0).then_inc(no_shift, 1)
            @block.gpsimd
            def _(pool):
                nc.gpsimd.memset(minus_half[:, :], -0.5).then_inc(half_set, 1)
                nc.gpsimd.memset(q_all[:, :, :, :].rearrange("r p b n -> r (p b n)").bitcast(F32), 0.0)\
                    .then_inc(zeroed, 1)
        CONST = 8

        def norm_sems(tag):
            return {n: sem(f"{tag}_{n}") for n in (
                "stats_ready", "moments_ready", "rstd_ready", "normed", "turned", "turned_copied", "affine_done")}

        def norm_vector(dve, q, src, dst, affine):
            for t in range(T):
                nc.vector.bn_stats(stats[:, t, :], src[:, t, :]).then_inc(q["stats_ready"], 1)
            for t in range(T):
                dve.wait_ge(q["stats_ready"], t + 1)
                nc.vector.bn_aggr(mv[:, t, :], stats[:, t, :]).then_inc(q["moments_ready"], 1)
            dve.wait_ge(q["rstd_ready"], 2)
            for t in range(T):
                nc.vector.tensor_scalar(dst[:, t, :], src[:, t, :], mv[:, t, 0:1], rstd[:, t:t + 1],
                                        ALU.subtract, ALU.mult).then_inc(q["normed"], 1)
            if affine:
                dve.wait_ge(q["normed"], T)
                nc.vector.tensor_tensor(dst[:, :, :], dst[:, :, :], gam[:, None, :].broadcast_to([TR, T, D]),
                                        ALU.mult).then_inc(q["affine_done"], 1)
                dve.wait_ge(q["affine_done"], 1)
                nc.vector.tensor_tensor(dst[:, :, :], dst[:, :, :], bet[:, None, :].broadcast_to([TR, T, D]),
                                        ALU.add).then_inc(q["affine_done"], 1)

        def norm_pool(pool, q):
            pool.wait_ge(q["moments_ready"], T)
            nc.gpsimd.tensor_scalar(rstd[:, :], mv[:, :, 1], EPS, None, ALU.add).then_inc(q["rstd_ready"], 1)
            pool.wait_ge(q["rstd_ready"], 1)
            nc.gpsimd.tensor_tensor(rstd[:, :], rstd[:, :], minus_half[:, :], ALU.pow).then_inc(q["rstd_ready"], 1)

        def transpose_tensor(pe, q, src, affine):
            if affine:
                pe.wait_ge(q["affine_done"], 2)
            for t in range(T):
                if not affine:
                    pe.wait_ge(q["normed"], t + 1)
                dst = wide[0][:, t // 4, TR * (t % 4):TR * (t % 4) + TR]
                nc.tensor.transpose(dst, src[:, t, :], ident[0:TR, 0:TR]).then_inc(q["turned"], 1)

        def transpose_copy(act, q):
            for i in range(2):
                act.wait_ge(q["turned"], 4 * i + 4)
                nc.scalar.copy(xt[:, HALF * i:HALF * i + HALF], wide[0][:, i, 0:HALF]).then_inc(q["turned_copied"], 1)

        def attention(L):
            s = {n: sem(f"a{L}_{n}") for n in (
                "ctx_in0", "ctx_in1", "k_made", "k_hi_ready", "k_rest_ready", "k_mid_ready",
                "k_lo_ready", "stacked0", "stacked1", "stacked2", "ones_in", "mask_rows_in",
                "v_made", "v_copied", "q_made", "q_scaled", "q_hi_rest_ready", "q_mid_ready",
                "q_lo_ready", "q_stacked", "q_max_set", "q_cur_set", "first_rows_in",
                "large_checked", "compare_in", "compare_less_row", "compare_reduced",
                "differ_ready", "differ_anywhere", "flag_set", "mask_in00", "mask_in01",
                "mask_in02", "mask_in10", "mask_in11", "mask_in12", "max_scores_ready",
                "max_taken", "max_folded", "shift_hi_ready", "shift_rest_ready", "shift_mid_ready",
                "shift_lo_ready", "shift_turned", "shift_rows_set", "scores_ready", "exp_ready",
                "chunk_weighed", "outputs_copied", "outputs_turned", "sums_inverted",
                "outputs_divided", "bias_added", "outputs_to_columns", "columns_copied",
                "outputs_projected", "x_updated")}
            q = norm_sems(f"n{L}")
            scale_q = -1.0 / A ** 0.5 if L == 0 else 1.0
            scale_e = 1.0 if L == 0 else 1.0 / D ** 0.5

            spare = (e_sb[0:2 * S, :, :].rearrange("p c n -> p (c n)")[:, 0:S2],
                     u_all[0:2 * S, 2:4, :, :].rearrange("p s b q -> p (s b q)")[:, 0:S2])
            NST = TERMS + (1 if L == 0 else 0)

            def wait_mask(pe, r, par, th):
                pe.wait_ge(s[f"mask_in{par}{th}"], 16 * r + 16 if L == 0 else 16)

            def k_proj(pe, b, r, par, th, free):
                if th == 0:
                    pe.wait_ge(s[f"ctx_in{par}"], 16 * r + 16)
                if free is not None:
                    pe.wait_ge(*free)
                nc.tensor.matmul(aux[:, 0:TK], w_k[L][:, :], ctx_sb[:, par, TK * th:TK * th + TK],
                                 start=True, stop=True).then_inc(s["k_made"], 1)

            def v_proj(pe, b, par, f, free, chunks=range(4)):
                if chunks[0] == 0:
                    pe.wait_ge(*free)
                for c in chunks:
                    k0 = CK * (4 * f + c)
                    i = nc.tensor.matmul(aux[0:CK, P * c:P * c + P], ctx_sb[:, par, k0:k0 + CK], w_v[L][:, :],
                                         start=True, stop=True)
                if chunks[-1] == 3:
                    i.then_inc(s["v_made"], 1)

            def max_scores(pe, b, r, par, n, masked):
                th, p = n // PAIRS, n % PAIRS
                if n == 0:
                    pe.wait_ge(s["q_max_set"], b + 1)
                if p == 0:
                    pe.wait_ge(s[f"stacked{th}"], 16 * NST * (b + 1))
                if not (isinstance(b, int) and b == 0 and n < 2):
                    pe.wait_ge(s["max_taken"], 24 * b + n - 1)
                cols = slice(TK * th, TK * th + TK)
                rows = MASK_ROW if masked else ROWS
                i = nc.tensor.matmul(bank[n % 2][0:TR, 0:TK], q_max[0:rows, p, :],
                                     k_stack[0:rows, par, p, cols], start=True, stop=not masked)
                if masked:
                    if p == 0 or n == N_AHEAD:
                        wait_mask(pe, r, par, th)
                    i = nc.tensor.matmul(bank[n % 2][0:TR, 0:TK],
                                         ident_q[:, 0:2, :].rearrange("k h q -> k (h q)"),
                                         mask_sb[:, par, cols], start=False, stop=True)
                i.then_inc(s["max_scores_ready"], 1)

            def max_rows(pe, b, free):
                pe.wait_ge(s["shift_lo_ready"], b + 1)
                pe.wait_ge(*free)
                rows = aux[SHIFT_ROW:SHIFT_ROW + 3, 0:4 * TR].bitcast(BF16)
                for p in range(PAIRS):
                    i = nc.tensor.transpose(rows[:, TR * p:TR * p + TR], m_part[:, p, :], ident_b[0:TR, 0:TR])
                i.then_inc(s["shift_turned"], 1)

            def scores(pe, b, r, par, c, half, masked):
                if c == 0 and half == 0:
                    pe.wait_ge(s["q_cur_set"], b + 1)
                    pe.wait_ge(s["shift_rows_set"], b + 1)
                if half == 0 and not (isinstance(b, int) and b == 0 and c < 2):
                    pe.wait_ge(s["exp_ready"], CH * b + c - 1)
                if masked and c % 4 == 0 and half == 0:
                    wait_mask(pe, r, par, c // 4)
                rows = MASK_ROW if masked else ROWS
                for n in range(4):
                    p = 4 * half + n
                    i = nc.tensor.matmul(wide[c % 2][0:CK, half, TR * n:TR * n + TR],
                                         k_stack[0:rows, par, p, CK * c:CK * c + CK], q_cur[0:rows, par, p, :],
                                         start=(n == 0), stop=(n == 3 and not masked), skip_group_check=True)
                if masked:
                    i = nc.tensor.matmul(wide[c % 2][0:CK, half, 0:4 * TR], mask_sb[:, par, CK * c:CK * c + CK],
                                         ident_q[:, :, :].rearrange("k h q -> k (h q)"),
                                         start=False, stop=True, skip_group_check=True)
                if half:
                    i.then_inc(s["scores_ready"], 1)

            def weigh(pe, b, par, c, part):
                if part == 0:
                    pe.wait_ge(s["exp_ready"], CH * b + c + 1)
                    if c == 0:
                        pe.wait_ge(s["v_copied"], 3 * b + 3)
                        if not (isinstance(b, int) and b == 0):
                            pe.wait_ge(s["outputs_copied"], b)
                    for j in range(4):
                        nc.tensor.matmul(acc[32 * j:32 * j + 32, 0:3 * S], v_sb[0:CK, par, c, j, 0:32],
                                         e_sb[0:CK, c % 3, 4 * S * j:4 * S * j + 3 * S],
                                         start=(c == 0), stop=(c == CH - 1), skip_group_check=True)
                else:
                    for j in range(4):
                        i = nc.tensor.matmul(acc[32 * j:32 * j + 32, 3 * S:4 * S], v_sb[0:CK, par, c, j, 2:34],
                                             e_sb[0:CK, c % 3, 4 * S * j + 3 * S:4 * S * j + 4 * S],
                                             start=False, stop=(c == CH - 1), skip_group_check=True)
                    i.then_inc(s["chunk_weighed"], 1)

            SPREAD = (2, 2, 3, 3, 2, 3, 3, 2, 2, 0, 0, 0)
            AHEAD = (0, 0, 0, 0, 0, 0, 0, 0, 0, 0, 0, 2)
            N_AHEAD = sum(AHEAD)
            LAST = max(c for c in range(CH) if SPREAD[c])
            K_AT, V_AT = (0, 6, 8), ((2, 2), (3, 4), (5, 5))
            K_FIRST, V_FIRST = (0, 3, 6), (9, 12, 15)
            TURN_AT = 2
            COMPARE_AT = (2, 3, 5)

            def max_steps(b, r, par, c, nxt, nxt2):
                n0, a0 = N_AHEAD + sum(SPREAD[:c]), sum(AHEAD[:c])
                return ([(b + 1, r + par, 1 - par, n) for n in range(n0, n0 + SPREAD[c]) if nxt]
                        + [(b + 2, r + 1, par, n) for n in range(a0, a0 + AHEAD[c]) if nxt2])

            def turn_outputs(pe, t):
                pe.wait_ge(s["outputs_copied"], 2 * t + 2)
                if t >= 2:
                    pe.wait_ge(s["outputs_divided"], 4 * (t - 2) + 4)
                for k in range(4):
                    i = nc.tensor.transpose(bank[t % 2][0:TR, P * k:P * k + P],
                                            u_all[:, k, 2 * t:2 * t + 2, :].rearrange("p b q -> p (b q)"), ident[:, :])
                i.then_inc(s["outputs_turned"], 1)

            def pe_batch(pe, b, r, par, first, nxt, nxt2, masked):
                for c in range(CH):
                    steps = max_steps(b, r, par, c, nxt, nxt2)

                    def ahead(k):
                        if k < len(steps):
                            max_scores(pe, *steps[k], masked)

                    scores(pe, b, r, par, c, 0, masked)
                    if nxt and c == CH - 1:
                        if L == 0 and par == 1 and not (isinstance(r, int) and r == B // 2 - 2):
                            pe.wait_ge(s["flag_set"], r + 2)
                        max_rows(pe, b + 1, (s["k_rest_ready"], 3 * b + 9) if nxt2 else (s["v_copied"], 3 * b + 6))
                    ahead(0)
                    scores(pe, b, r, par, c, 1, masked)
                    for f in range(3) if nxt else ():
                        free = (((s["k_rest_ready"], 3 * b + 7) if nxt2 else (s["shift_rows_set"], b + 1)),
                                (s["v_copied"], 3 * b + 4), (s["v_copied"], 3 * b + 5))[f]
                        if c == V_AT[f][0]:
                            v_proj(pe, b + 1, 1 - par, f, free, range(2))
                        if c == V_AT[f][1]:
                            v_proj(pe, b + 1, 1 - par, f, free, range(2, 4))
                    if nxt2 and c in K_AT:
                        th = K_AT.index(c)
                        k_proj(pe, b + 2, r + 1, par, th, (
                            (s["shift_rows_set"], b + 1), (s["v_copied"], 3 * b + 6),
                            (s["k_rest_ready"], 3 * b + 8))[th])
                    ahead(1)
                    wb, wp, wc = (b, par, c - 1) if c > 0 else (b - 1, 1 - par, CH - 1)
                    if not (first and c == 0):
                        weigh(pe, wb, wp, wc, 0)
                    ahead(2)
                    if not (first and c == 0):
                        weigh(pe, wb, wp, wc, 1)
                    if not nxt and c >= TURN_AT and c - TURN_AT < T - 1:
                        turn_outputs(pe, c - TURN_AT)

            def over_rounds(e, emit, peeled=1):
                last = B // 2 - peeled
                for b in range(2):
                    emit(e, b, 0, b, b == 0, True, True, True)
                with e.Fori(1, last) as i:
                    for par in range(2):
                        emit(e, 2 * i + par, i, par, False, True, True, True)
                for b in range(2 * last, B):
                    emit(e, b, b // 2, b % 2, False, b < B - 1, b < B - 2, b < B - 3)

            def by_mask(pe, emit, count=None):
                if count is not None:
                    pe.wait_ge(s["flag_set"], count)
                seen = pe.value_load(flag[0:1, 0:1], min_val=0, max_val=1)
                with pe.If(seen > 0):
                    emit(True)
                with pe.Else():
                    emit(False)

            def pe_rounds(pe):
                def emit(masked, r, b, first=False, last=False):
                    for par in range(2):
                        pe_batch(pe, b + par, r, par, first and par == 0, not (last and par == 1), not last, masked)

                def start(masked):
                    for n in range(24):
                        max_scores(pe, 0, 0, 0, n, masked)
                        if n in K_FIRST:
                            th = K_FIRST.index(n)
                            k_proj(pe, 1, 0, 1, th, (s["k_rest_ready"], 3 + th))
                        if n in V_FIRST:
                            f = V_FIRST.index(n)
                            v_proj(pe, 0, 0, f, (s["v_copied"], f) if f else (s["k_rest_ready"], 6))
                    max_rows(pe, 0, (s["v_copied"], 3))
                    for n in range(N_AHEAD):
                        max_scores(pe, 1, 0, 1, n, masked)
                    emit(masked, 0, 0, first=True)

                def middle(masked, i):
                    emit(masked, i, 2 * i)

                def end(masked):
                    emit(masked, B // 2 - 1, B - 2, last=True)

                if L == 0:
                    by_mask(pe, start, 1)
                    with pe.Fori(1, B // 2 - 1) as i:
                        by_mask(pe, lambda masked: middle(masked, i))
                    by_mask(pe, end)
                else:
                    def whole(masked):
                        start(masked)
                        with pe.Fori(1, B // 2 - 1) as i:
                            middle(masked, i)
                        end(masked)

                    by_mask(pe, whole, 1)

            def act_k(act, b, th):
                act.wait_ge(s["k_made"], 3 * b + th + 1)
                if not (isinstance(b, int) and b == 0):
                    act.wait_ge(s[f"stacked{th}"], 16 * NST * b)
                nc.scalar.activation(k_part[0][:, TK * th:TK * th + TK], aux[:, 0:TK], ACT.Identity,
                                     bias=b_k[:, L:L + 1]).then_inc(s["k_hi_ready"], 1)

            def act_v(act, b, par, f):
                act.wait_ge(s["v_made"], 3 * b + f + 1)
                if f == 0 and not (isinstance(b, int) and b < 2):
                    act.wait_ge(s["chunk_weighed"], CH * (b - 1))
                nc.scalar.copy(v_sb[0:CK, par, 4 * f:4 * f + 4, :, 1:33],
                               aux[0:CK, :].rearrange("p (c j d) -> p c j d", c=4, j=4)).then_inc(s["v_copied"], 1)

            def act_u(act, b):
                act.wait_ge(s["chunk_weighed"], CH * b + CH)
                nc.scalar.copy(u_all[:, :, b, :], acc[:, 0:4 * S].rearrange("p (s q) -> p s q", s=4))\
                    .then_inc(s["outputs_copied"], 1)

            def act_batch(act, b, r, par, first, nxt, nxt2, nxt3):
                for c in range(CH):
                    act.wait_ge(s["scores_ready"], CH * b + c + 1)
                    if not (isinstance(b, int) and b == 0 and c < 3):
                        act.wait_ge(s["chunk_weighed"], CH * b + c - 2)
                    nc.scalar.activation(e_sb[0:CK, c % 3, :].rearrange("p (h n) -> p h n", h=2),
                                         wide[c % 2][0:CK, :, 0:4 * TR], ACT.Exp, scale=scale_e)\
                        .then_inc(s["exp_ready"], 1)
                    if c == 0 and not first:
                        act_u(act, b - 1)
                    for f in range(3) if nxt else ():
                        if c == V_AT[f][1]:
                            act_v(act, b + 1, 1 - par, f)
                    if nxt2 and c in K_AT:
                        act_k(act, b + 2, K_AT.index(c))

            def dve_k(dve, b, th):
                cols = slice(TK * th, TK * th + TK)
                dve.wait_ge(s["k_hi_ready"], 3 * b + th + 1)
                if not (isinstance(b, int) and b == 0):
                    dve.wait_ge(s["k_lo_ready"], 3 * b + th - 2)
                nc.vector.scalar_tensor_tensor(k_rest[:, th, :], aux[:, 0:TK], b_k[:, L:L + 1], k_part[0][:, cols],
                                               ALU.add, ALU.subtract).then_inc(s["k_rest_ready"], 1)

            def dve_q_max(dve, b):
                nc.vector.tensor_copy(q_max[0:SHIFT_ROW, :, :], q_all[:, :, b, :]).then_inc(s["q_max_set"], 1)

            def dve_q(dve, b, par):
                nc.vector.tensor_copy(q_cur[0:SHIFT_ROW, par, :, :], q_all[:, :, b, :]).then_inc(s["q_cur_set"], 1)

            def dve_max(dve, b, n):
                dve.wait_ge(s["max_scores_ready"], 24 * b + n + 1)
                nc.vector.tensor_reduce(out=mx[:, n // PAIRS, n % PAIRS:n % PAIRS + 1], in_=bank[n % 2][0:TR, 0:TK],
                                        axis=AX, op=ALU.max).then_inc(s["max_taken"], 1)

            def dve_shift(dve, b):
                dve.wait_ge(s["max_taken"], 24 * b + 24)
                nc.vector.tensor_reduce(out=m_fold[:, :], in_=mx[:, :, :].rearrange("q t p -> q p t"),
                                        axis=AX, op=ALU.max).then_inc(s["max_folded"], 1)
                dve.wait_ge(s["max_folded"], b + 1)
                nc.vector.tensor_scalar(m_part[:, :, 0], m_fold[:, :], -1.0, None, ALU.mult)\
                    .then_inc(s["shift_hi_ready"], 1)
                dve.wait_ge(s["shift_hi_ready"], b + 1)
                nc.vector.scalar_tensor_tensor(m_rest[:, :], m_fold[:, :], -1.0, m_part[:, :, 0],
                                               ALU.mult, ALU.subtract).then_inc(s["shift_rest_ready"], 1)
                dve.wait_ge(s["shift_rest_ready"], b + 1)
                nc.vector.tensor_copy(m_part[:, :, 1], m_rest[:, :]).then_inc(s["shift_mid_ready"], 1)
                dve.wait_ge(s["shift_mid_ready"], b + 1)
                nc.vector.tensor_tensor(m_part[:, :, 2], m_rest[:, :], m_part[:, :, 1], ALU.subtract)\
                    .then_inc(s["shift_lo_ready"], 1)

            def dve_shift_rows(dve, b, par):
                dve.wait_ge(s["shift_turned"], b + 1)
                nc.vector.tensor_copy(q_cur[SHIFT_ROW:SHIFT_ROW + 3, par, :, :].rearrange("r p n -> r (p n)"),
                                      aux[SHIFT_ROW:SHIFT_ROW + 3, 0:4 * TR].bitcast(BF16))\
                                          .then_inc(s["shift_rows_set"], 1)

            def dve_compare(dve, r, th, cmp=mask_cmp[:, :]):
                dve.wait_ge(s["compare_less_row"], r + 1)
                if not (isinstance(r, int) and r == 0):
                    dve.wait_ge(s["differ_ready"], r)
                nc.vector.tensor_reduce(out=differ[:, th:th + 1], in_=cmp[:, TK * th:TK * th + TK], axis=AX,
                                        op=ALU.max, apply_absolute_value=True).then_inc(s["compare_reduced"], 1)

            def dve_differ(dve, r):
                dve.wait_ge(s["compare_reduced"], 3 * r + 3)
                nc.vector.tensor_reduce(out=differ[:, 3:4], in_=differ[:, 0:4], axis=AX, op=ALU.max)\
                    .then_inc(s["differ_ready"], 1)

            def dve_flag(dve, r):
                dve.wait_ge(s["differ_anywhere"], r + 2)
                nc.vector.tensor_scalar(flag[:, :], differ[0:1, 4:5], 0.0, None, ALU.is_gt).then_inc(s["flag_set"], 1)

            def dve_outputs(dve, t):
                src = bank[t % 2][0:TR, :].rearrange("r (s j n) -> r s j n", s=4, j=4)
                dve.wait_ge(s["outputs_turned"], t + 1)
                nc.vector.reciprocal(rec[:, t, 0:3, :], src[:, 0:3, :, 0]).then_inc(s["sums_inverted"], 1)
                nc.vector.reciprocal(rec[:, t, 3, :], src[:, 3, :, 31]).then_inc(s["sums_inverted"], 1)
                dve.wait_ge(s["sums_inverted"], 2 * t + 2)
                for k in range(4):
                    r0 = 1 + A * k if k < 3 else 23
                    o = xn[:, t, :].rearrange("r (j k a) -> r j k a", j=4, k=4)[:, :, k, :]
                    nc.vector.tensor_tensor(o, src[:, k, :, r0:r0 + A],
                                            rec[:, t, k, :, None].broadcast_to([TR, 4, A]), ALU.mult)\
                        .then_inc(s["outputs_divided"], 1)

            def dve_batch(dve, b, r, par, first, nxt, nxt2, nxt3):
                compare = L == 0 and par == 1 and not (isinstance(r, int) and r + 2 >= B // 2)
                for c in range(CH):
                    if nxt and c == CH - 1:
                        if compare:
                            dve_flag(dve, r)
                        if L == 0 and isinstance(b, int) and b == B - 3:
                            dve_flag(dve, r - 1)
                        dve_shift_rows(dve, b + 1, 1 - par)
                    k_due = nxt2 and c - 1 in K_AT
                    for step in max_steps(b, r, par, c, nxt, nxt2):
                        dve_max(dve, step[0], step[3])
                        if k_due:
                            k_due = False
                            dve_k(dve, b + 2, K_AT.index(c - 1))
                    if nxt and c == 1:
                        dve_q(dve, b + 1, 1 - par)
                    if nxt and c == LAST:
                        dve_shift(dve, b + 1)
                        if nxt2:
                            dve_q_max(dve, b + 2)
                    if k_due:
                        dve_k(dve, b + 2, K_AT.index(c - 1))
                    if compare and c in COMPARE_AT:
                        dve_compare(dve, r + 2, COMPARE_AT.index(c))
                    if compare and c == COMPARE_AT[2] + 1:
                        dve_differ(dve, r + 2)

            def load_ctx(sp, b, par):
                if not (isinstance(b, int) and b < 2):
                    sp.wait_ge(s["v_made"], 3 * (b - 1))
                sp.dma_start(ctx_sb[:, par, :], ctx_t[b]).then_inc(s[f"ctx_in{par}"], 16)

            def load_mask(sp, b, par, th):
                cols = slice(TK * th, TK * th + TK)
                sp.dma_start(mask_sb[:, par, cols], mask0[b][:, cols] if L == 0 else mask1[:, cols])\
                    .then_inc(s[f"mask_in{par}{th}"], 16)

            def load_compare(sp, r, cmp=mask_cmp[:, :], row=mask_row[:, :]):
                if L == 0:
                    if not (isinstance(r, int) and r < 2):
                        sp.wait_ge(s["compare_reduced"], 3 * r)
                    sp.dma_start(cmp, mask0.rearrange("(r h) q k -> r (h q) k", h=2)[r]).then_inc(s["compare_in"], 16)
                    for h in range(2):
                        sp.dma_start(row[S * h:S * h + S, :], mask0[2 * r + h, 0:1, :].broadcast_to([S, S2]))\
                            .then_inc(s["compare_in"], 16)
                else:
                    for h in range(2):
                        sp.dma_start(cmp[S * h:S * h + S, :], mask1).then_inc(s["compare_in"], 16)
                    sp.dma_start(row, mask1[0:1, :].broadcast_to([2 * S, S2])).then_inc(s["compare_in"], 16)

            def stack(sp, b, par, th):
                sp.wait_ge(s["k_lo_ready"], 3 * b + th + 1)
                cols = slice(TK * th, TK * th + TK)
                for t in range(TERMS):
                    sp.dma_start(k_stack[16 * t:16 * t + 16, par, :, cols],
                                 k_part[K_PART[t]][:, cols]).then_inc(s[f"stacked{th}"], 16)
                if L == 0:
                    sp.dma_start(k_stack[MASK_ROW:ROWS, par, :, cols],
                                 mask_scratch[b][:, None, cols].broadcast_to([3, PAIRS, TK]))\
                                     .then_inc(s[f"stacked{th}"], 16)

            def sp_batch(sp, b, r, par, first, nxt, nxt2, nxt3):
                for th in range(TH):
                    if nxt2:
                        stack(sp, b + 2, par, th)
                        if L == 0:
                            load_mask(sp, b + 2, par, th)
                    if nxt3 and th == 0:
                        load_ctx(sp, b + 3, 1 - par)
                    if th == 0 and L == 0 and par == 0 and not (isinstance(r, int) and r + 2 >= B // 2):
                        load_compare(sp, r + 2)

            with nc.Block() as block:
                @block.sync
                def _(sp):
                    load_ctx(sp, 0, 0)
                    if L == 0:
                        sp.wait_ge(const, CONST)
                    for par in range(2):
                        sp.dma_start(k_stack[SHIFT_ROW:MASK_ROW, par, :, :].rearrange("r p (j k) -> r (p j) k", j=MJ),
                                     ones_b[:, None, :].broadcast_to([3, PAIRS * MJ, MK])).then_inc(s["ones_in"], 16)
                    if L == 0:
                        sp.wait_ge(mr_split, 4)
                        for i in range(3):
                            sp.dma_start(mask_scratch[:, i, :].rearrange("b (j k) -> b j k", j=MJ), mr_part[i])\
                                .then_inc(mask_out, 16)
                    n = B if L == 0 else 1
                    sp.dma_start(mask_first[0:n, :], mask0[:, 0, :] if L == 0 else mask1[0:1, :])\
                        .then_inc(s["first_rows_in"], 16)
                    load_compare(sp, 0)
                    if L == 0:
                        load_compare(sp, 1, *spare)
                    if L == 1:
                        for par in range(2):
                            sp.dma_start(k_stack[MASK_ROW:ROWS, par, :, :],
                                         mask_scratch[B][:, None, :].broadcast_to([3, PAIRS, S2]))\
                                .then_inc(s["mask_rows_in"], 16)
                    else:
                        sp.wait_ge(mask_out, 48)
                    stack(sp, 0, 0, 0)
                    sp.wait_ge(s["large_checked"], 2)
                    load_ctx(sp, 1, 1)
                    sp.wait_ge(s["q_lo_ready"], 1)
                    if L == 0:
                        sp.wait_ge(zeroed, 1)
                    for t in range(TERMS):
                        for h2 in range(2):
                            r = 16 * t + A * h2
                            sp.dma_start(
                                q_all[r:r + A, :, :, S * h2:S * h2 + S].rearrange("a p b q -> a (p b) q"),
                                q_part[Q_PART[t]][64 * h2:64 * h2 + 64, :].rearrange("n (b q) -> n b q", b=B),
                            ).then_inc(s["q_stacked"], 16)
                    stack(sp, 0, 0, 1)
                    stack(sp, 0, 0, 2)
                    for b in range(2):
                        for th in range(TH):
                            load_mask(sp, b, b, th)
                    for th in range(TH):
                        stack(sp, 1, 1, th)
                    load_ctx(sp, 2, 0)
                    if L == 0:
                        for dst, src in late:
                            sp.dma_start(dst[:, :], src).then_inc(w_late, 16)
                    over_rounds(sp, sp_batch, 2)
                    for par in range(2):
                        for th in range(TH):
                            sp.wait_ge(s[f"mask_in{par}{th}"], 16 * (B // 2 if L == 0 else 1))

                @block.gpsimd
                def _(pool):
                    if L == 0:
                        pool.wait_ge(half_set, 1)
                    norm_pool(pool, q)

                    def lo(b, th):
                        cols = slice(TK * th, TK * th + TK)
                        if not (isinstance(b, int) and b < 2):
                            pool.wait_ge(s["scores_ready"], CH * (b - 2) + 4 * th + 4)
                        pool.wait_ge(s["k_rest_ready"], 3 * b + th + 1)
                        if not (isinstance(b, int) and b == 0):
                            pool.wait_ge(s[f"stacked{th}"], 16 * NST * b)
                        nc.gpsimd.tensor_tensor(k_part[1][:, cols], k_rest[:, th, :], one[:, :], ALU.mult)\
                            .then_inc(s["k_mid_ready"], 1)
                        pool.wait_ge(s["k_mid_ready"], 3 * b + th + 1)
                        nc.gpsimd.tensor_tensor(k_part[2][:, cols], k_rest[:, th, :], k_part[1][:, cols],
                                                ALU.subtract).then_inc(s["k_lo_ready"], 1)

                    def against_row(r):
                        pool.wait_ge(s["compare_in"], 48 * r + 48)
                        nc.gpsimd.tensor_tensor(mask_cmp[:, :], mask_cmp[:, :], mask_row[:, :], ALU.subtract)\
                            .then_inc(s["compare_less_row"], 1)

                    def over_partitions():
                        nc.gpsimd.partition_all_reduce(differ[:, 4:5], differ[:, 3:4], 2 * S, RMAX)\
                            .then_inc(s["differ_anywhere"], 1)

                    def pool_batch(pool, b, r, par, first, nxt, nxt2, nxt3):
                        compare = L == 0 and not (isinstance(r, int) and r + 2 >= B // 2)
                        for th in range(TH):
                            if compare and par == 1 and th == 1:
                                pool.wait_ge(s["differ_ready"], r + 3)
                            if nxt2:
                                lo(b + 2, th)
                            if compare and par == 1 and th == 1:
                                over_partitions()
                        if compare and par == 0:
                            against_row(r + 2)

                    pool.wait_ge(q["rstd_ready"], 2)
                    for th in range(TH):
                        lo(0, th)
                    pool.wait_ge(s["differ_ready"], 2 if L == 0 else 1)
                    over_partitions()
                    for th in range(TH):
                        lo(1, th)
                    over_rounds(pool, pool_batch, 2)

                @block.scalar
                def _(act):
                    if L == 0:
                        act.wait_ge(w_in, W_IN)
                        act.wait_ge(const, CONST)
                        act.wait_ge(tg_in, 16)
                        nc.scalar.activation(tg[:, :], tg[:, :], ACT.Tanh).then_inc(tg_done, 1)
                    act_k(act, 0, 0)
                    transpose_copy(act, q)
                    act_k(act, 0, 1)
                    for i in range(2):
                        act.wait_ge(s["q_made"], i + 1)
                        if L == 0:
                            act.wait_ge(s["q_scaled"], 1)
                            nc.scalar.activation(q_f[:, HALF * i:HALF * i + HALF], wide[1][:, i, 0:HALF],
                                                 ACT.Identity, bias=b_q[:, 0:1], scale=scale_q)\
                                                     .then_inc(s["q_scaled"], 1)
                        else:
                            nc.scalar.copy(q_f[:, HALF * i:HALF * i + HALF], wide[1][:, i, 0:HALF])\
                                .then_inc(s["q_scaled"], 1)
                    act_k(act, 0, 2)
                    for th in range(TH):
                        act_k(act, 1, th)
                    for f in range(3):
                        act_v(act, 0, 0, f)
                    over_rounds(act, act_batch)
                    act_u(act, B - 1)
                    if L == 1:
                        for i in range(2):
                            act.wait_ge(s["outputs_to_columns"], 4 * i + 4)
                            nc.scalar.copy(xt[:, HALF * i:HALF * i + HALF], wide[1][:, i, 0:HALF])\
                                .then_inc(s["columns_copied"], 1)

                @block.vector
                def _(dve):
                    if L == 0:
                        dve.wait_ge(w_in, W_IN)
                        dve.wait_ge(const, CONST)
                        nc.vector.tensor_scalar(b_q[:, :], b_q[:, :], scale_q, None, ALU.mult)\
                            .then_inc(s["q_scaled"], 1)
                    nc.vector.memset(differ[:, :], 0.0).then_inc(s["large_checked"], 1)
                    if L == 0:
                        dve.wait_ge(mr_in, 32)
                        nc.vector.tensor_copy(mr_part[0], m_row[:, :]).then_inc(mr_split, 1)
                        dve.wait_ge(mr_split, 1)
                        nc.vector.tensor_tensor(m_left[:, :], m_row[:, :], mr_part[0], ALU.subtract)\
                            .then_inc(mr_split, 1)
                        dve.wait_ge(mr_split, 2)
                        nc.vector.tensor_copy(mr_part[1], m_left[:, :]).then_inc(mr_split, 1)
                        dve.wait_ge(mr_split, 3)
                        nc.vector.tensor_tensor(mr_part[2], m_left[:, :], mr_part[1], ALU.subtract)\
                            .then_inc(mr_split, 1)
                    norm_vector(dve, q, x_sb, xn, False)
                    dve_k(dve, 0, 0)
                    n = B if L == 0 else 1
                    dve.wait_ge(s["first_rows_in"], 16)
                    nc.vector.tensor_reduce(out=top[0:n, 0:1], in_=mask_first[0:n, :], axis=AX, op=ALU.max)\
                        .then_inc(s["large_checked"], 1)
                    dve.wait_ge(s["large_checked"], 2)
                    nc.vector.tensor_tensor(top[0:n, 1:2], top[0:n, 0:1], top[0:n, 0:1], ALU.mult)\
                        .then_inc(s["large_checked"], 1)
                    dve.wait_ge(s["large_checked"], 3)
                    nc.vector.tensor_scalar(differ[0:n, 3:4], top[0:n, 1:2], MASK_BIG ** 2, 0.0, ALU.subtract, ALU.max)\
                        .then_inc(s["large_checked"], 1)
                    dve_k(dve, 0, 1)
                    dve.wait_ge(s["q_scaled"], 3 if L == 0 else 2)
                    nc.vector.tensor_copy(q_part[0][:, :], q_f[:, :]).then_inc(s["q_hi_rest_ready"], 1)
                    dve.wait_ge(s["q_hi_rest_ready"], 1)
                    nc.vector.tensor_tensor(q_rest[:, :], q_f[:, :], q_part[0][:, :], ALU.subtract)\
                        .then_inc(s["q_hi_rest_ready"], 1)
                    dve.wait_ge(s["q_hi_rest_ready"], 2)
                    nc.vector.tensor_copy(q_part[1][:, :], q_rest[:, :]).then_inc(s["q_mid_ready"], 1)
                    dve.wait_ge(s["q_mid_ready"], 1)
                    nc.vector.tensor_tensor(q_part[2][:, :], q_rest[:, :], q_part[1][:, :], ALU.subtract)\
                        .then_inc(s["q_lo_ready"], 1)
                    dve_k(dve, 0, 2)
                    dve.wait_ge(s["large_checked"], 4)
                    for r in range(2 if L == 0 else 1):
                        cmp, row = (mask_cmp[:, :], mask_row[:, :]) if r == 0 else spare
                        dve.wait_ge(s["compare_in"], 96 if L == 0 else 48)
                        nc.vector.tensor_tensor(cmp, cmp, row, ALU.subtract).then_inc(s["compare_less_row"], 1)
                        for th in range(TH):
                            dve_compare(dve, r, th, cmp)
                        dve_differ(dve, r)
                    dve_flag(dve, -1)
                    dve.wait_ge(s["q_stacked"], 16 * 12)
                    dve_q_max(dve, 0)
                    dve_q(dve, 0, 0)
                    for n in range(24):
                        dve_max(dve, 0, n)
                        if n - 1 in K_FIRST:
                            dve_k(dve, 1, K_FIRST.index(n - 1))
                    dve_shift(dve, 0)
                    dve_q_max(dve, 1)
                    dve_shift_rows(dve, 0, 0)
                    for n in range(N_AHEAD):
                        dve_max(dve, 1, n)
                    over_rounds(dve, dve_batch, 2)
                    for t in range(T):
                        dve_outputs(dve, t)
                    if L == 0:
                        dve.wait_ge(s["outputs_divided"], 32)
                        dve.wait_ge(w_late, W_LATE)
                        dve.wait_ge(tg_done, 1)
                        nc.vector.tensor_tensor(xn[:, :, :], xn[:, :, :], b_v[:, None, :].broadcast_to([TR, T, D]),
                                                ALU.add).then_inc(s["bias_added"], 1)
                        dve.wait_ge(s["bias_added"], 1)
                        nc.vector.scalar_tensor_tensor(
                            x_sb[:, :, :].rearrange("r t d -> r (t d)"), xn[:, :, :].rearrange("r t d -> r (t d)"),
                            tg[0:TR, 0:1], x_sb[:, :, :].rearrange("r t d -> r (t d)"), ALU.mult, ALU.add)\
                            .then_inc(s["x_updated"], 1)
                        dve.wait_ge(s["x_updated"], 1)
                    else:
                        for i in range(2):
                            dve.wait_ge(s["outputs_projected"], 4 * i + 4)
                            v = x_sb[:, 4 * i:4 * i + 4, :].rearrange("r t d -> r (t d)")
                            nc.vector.scalar_tensor_tensor(v, wide[0][0:TR, i, :], tg[0:TR, 1:2], v,
                                                           ALU.mult, ALU.add).then_inc(s["x_updated"], 1)
                        dve.wait_ge(s["x_updated"], 2)

                @block.tensor
                def _(pe):
                    if L == 0:
                        pe.wait_ge(no_shift, 1)
                        pe.wait_ge(w_in, W_IN)
                        pe.wait_ge(const, CONST)
                    k_proj(pe, 0, 0, 0, 0, None)
                    transpose_tensor(pe, q, xn, False)
                    k_proj(pe, 0, 0, 0, 1, (s["k_rest_ready"], 1))
                    for i in range(2):
                        pe.wait_ge(q["turned_copied"], i + 1)
                        nc.tensor.matmul(wide[1][:, i, 0:HALF], w_q[L][:, :], xt[:, HALF * i:HALF * i + HALF],
                                         start=True, stop=True).then_inc(s["q_made"], 1)
                    k_proj(pe, 0, 0, 0, 2, (s["k_rest_ready"], 2))
                    pe.wait_ge(s["ones_in"], 32)
                    if L == 1:
                        pe.wait_ge(s["mask_rows_in"], 32)
                    pe_rounds(pe)
                    for part in range(2):
                        weigh(pe, B - 1, 1, CH - 1, part)
                    turn_outputs(pe, T - 1)
                    if L == 1:
                        for t in range(T):
                            pe.wait_ge(s["outputs_divided"], 4 * t + 4)
                            nc.tensor.transpose(wide[1][:, t // 4, TR * (t % 4):TR * (t % 4) + TR], xn[:, t, :],
                                                ident[0:TR, 0:TR]).then_inc(s["outputs_to_columns"], 1)
                        for t in range(T):
                            pe.wait_ge(s["columns_copied"], t // 4 + 1)
                            nc.tensor.matmul(wide[0][0:TR, t // 4, P * (t % 4):P * (t % 4) + P],
                                             xt[:, TR * t:TR * t + TR], w_o[:, :], start=True, stop=True)\
                                .then_inc(s["outputs_projected"], 1)


        def experts(L):
            s = {n: sem(f"f{L}_{n}") for n in (
                "router_step", "logits_ready", "exp_ready", "gates_ready", "gates_turned",
                "gates_copied", "gates_stored", "hidden_ready", "gelu_ready", "gated_ready",
                "y_added", "y_copied", "y_turned", "x_updated", "out_stored", "w1_in0", "w1_in1",
                "w2_in0", "w2_in1", "gate_in0", "gate_in1")}
            fw1, fb1, fw2 = (fw1_0, fb1_0, fw2_0) if L == 0 else (fw1_1, fb1_1, fw2_1)
            q0 = norm_sems(f"m{L}")
            q1 = norm_sems("mm") if L == 1 else q0
            U = 2 * FC
            LAG = 4
            chain = [0]

            def over_experts(e, emit):
                for n in range(2):
                    emit(e, n, 0, n, n == 0, False)
                with e.Fori(1, E // 2 - 1) as i:
                    for par in range(2):
                        emit(e, 2 * i + par, i, par, False, False)
                for n in range(E - 2, E):
                    emit(e, n, n // 2, n % 2, False, n == E - 1)

            def early(n, k):
                return isinstance(n, int) and n < k

            def load(sp, e, par):
                if not early(e, 2):
                    sp.wait_ge(s["hidden_ready"], U * (e - 1))
                sp.dma_start(w1_sb[:, par, :], fw1[e]).then_inc(s[f"w1_in{par}"], 16)
                if not early(e, 2):
                    sp.wait_ge(s["gelu_ready"], U * (e - 1))
                sp.dma_start(b1_sb[:, par, :], fb1[e]).then_inc(s[f"w1_in{par}"], 16)
                if not early(e, 2):
                    sp.wait_ge(s["y_added"], U * (e - 1))
                sp.dma_start(w2_sb[:, par, :, :], fw2[e]).then_inc(s[f"w2_in{par}"], 16)

            def load_gates(sp, e, par):
                if not early(e, 2):
                    sp.wait_ge(s["gated_ready"], U * (e - 1))
                sp.dma_start(gate_b[:, par, :], gate_scratch[L, e][None, :].broadcast_to([P, NTOK]))\
                    .then_inc(s[f"gate_in{par}"], 16)

            def hidden(pe, e, r, par, u):
                n = U * e + u
                if u == 0:
                    pe.wait_ge(s[f"w1_in{par}"], 32 * r + 32)
                if not early(n, 4):
                    pe.wait_ge(s["gelu_ready"], n - 3)
                fc, half = u // 2, u % 2
                nc.tensor.matmul(bank[u % 4][:, 0:HALF], w1_sb[:, par, P * fc:P * fc + P],
                                 xt[:, HALF * half:HALF * half + HALF], start=True, stop=True)\
                                     .then_inc(s["hidden_ready"], 1)

            def back(pe, e, r, par, u, last):
                n = U * e + u
                if u == 0:
                    pe.wait_ge(s[f"w2_in{par}"], 16 * r + 16)
                pe.wait_ge(s["gated_ready"], n + 1)
                fc, half = u // 2, u % 2
                nc.tensor.matmul(wide[1][:, half, 0:HALF], w2_sb[:, par, fc, :], hg_sb[:, u % 4, :],
                                 start=False, stop=last and fc == FC - 1, skip_group_check=True)\
                    .then_inc(s["y_added"], 1)

            def pe_expert(pe, e, r, par, first, last):
                for u in range(U):
                    if u + LAG < U:
                        hidden(pe, e, r, par, u + LAG)
                    elif not last:
                        hidden(pe, e + 1, r + par, 1 - par, u + LAG - U)
                    back(pe, e, r, par, u, last)

            def act_expert(act, e, r, par, first, last):
                for u in range(U):
                    n = U * e + u
                    act.wait_ge(s["hidden_ready"], n + 1)
                    if not early(n, 4):
                        act.wait_ge(s["gated_ready"], n - 3)
                    nc.scalar.activation(h_sb[:, u % 4, :], bank[u % 4][:, 0:HALF],
                                         ACT.Gelu if L == 0 else ACT.Gelu_apprx_tanh,
                                         bias=b1_sb[:, par, u // 2:u // 2 + 1]).then_inc(s["gelu_ready"], 1)

            def dve_expert(dve, e, r, par, first, last):
                dve.wait_ge(s[f"gate_in{par}"], 16 * r + 16)
                for u in range(U):
                    n = U * e + u
                    dve.wait_ge(s["gelu_ready"], n + 1)
                    if not early(n, 4):
                        dve.wait_ge(s["y_added"], n - 3)
                    half = u % 2
                    nc.vector.tensor_tensor(hg_sb[:, u % 4, :], h_sb[:, u % 4, :],
                                            gate_b[:, par, HALF * half:HALF * half + HALF], ALU.mult)\
                        .then_inc(s["gated_ready"], 1)

            def sp_expert(sp, e, r, par, first, last):
                if not early(e, 2):
                    load(sp, e, par)
                load_gates(sp, e, par)

            def over_tokens(v):
                return v[:, :, None].broadcast_to([TR, T, E])

            with nc.Block() as block:
                @block.sync
                def _(sp):
                    for n in range(2):
                        load(sp, n, n)
                    sp.wait_ge(s["gates_copied"], 2)
                    sp.dma_start(gate_scratch[L], g_t[:, :]).then_inc(s["gates_stored"], 16)
                    sp.wait_ge(s["gates_stored"], 16)
                    over_experts(sp, sp_expert)
                    if L == 1:
                        for i in range(2):
                            sp.wait_ge(s["x_updated"], i + 1)
                            sp.dma_start(out[HALF * i:HALF * i + HALF, :].rearrange("(t r) d -> r t d", r=TR),
                                         x_sb[:, 4 * i:4 * i + 4, :]).then_inc(s["out_stored"], 16)
                        sp.wait_ge(s["out_stored"], 32)

                @block.gpsimd
                def _(pool):
                    norm_pool(pool, q0)
                    if L == 1:
                        pool.wait_ge(q0["rstd_ready"], 2)
                        pool.wait_ge(q0["normed"], T)
                        norm_pool(pool, q1)

                @block.tensor
                def _(pe):
                    transpose_tensor(pe, q1, xn, L == 1)
                    for t in range(T):
                        pe.wait_ge(q1["turned_copied"], t // 4 + 1)
                        i = nc.tensor.matmul(wide[1][0:TR, 0, E * t:E * t + E], xt[:, TR * t:TR * t + TR], w_r[L][:, :],
                                             start=True, stop=True)
                    i.then_inc(s["logits_ready"], 1)
                    for u in range(2):
                        hidden(pe, 0, 0, 0, u)
                    pe.wait_ge(s["gates_ready"], 1)
                    for t in range(T):
                        nc.tensor.transpose(wide[0][0:E, t // 4, TR * (t % 4):TR * (t % 4) + TR],
                                            lg[:, 7, t, :], ident[0:TR, 0:TR]).then_inc(s["gates_turned"], 1)
                    for u in range(2, LAG):
                        hidden(pe, 0, 0, 0, u)
                    pe.wait_ge(s["gates_copied"], 2)
                    for i in range(2):
                        nc.tensor.matmul(wide[1][:, i, 0:HALF], fb2[L][:, :], g_t[:, HALF * i:HALF * i + HALF],
                                         start=True, stop=False, skip_group_check=True)
                    over_experts(pe, pe_expert)
                    for t in range(T):
                        pe.wait_ge(s["y_copied"], t // 4 + 1)
                        nc.tensor.transpose(wide[0][0:TR, t // 4, P * (t % 4):P * (t % 4) + P],
                                            y_t[:, TR * t:TR * t + TR], ident[:, :]).then_inc(s["y_turned"], 1)

                @block.scalar
                def _(act):
                    transpose_copy(act, q1)
                    act.wait_ge(s["router_step"], 3)
                    nc.scalar.activation(lg[:, 2, :, :], lg[:, 1, :, :], ACT.Exp).then_inc(s["exp_ready"], 1)
                    for i in range(2):
                        act.wait_ge(s["gates_turned"], 4 * i + 4)
                        nc.scalar.copy(g_t[:, HALF * i:HALF * i + HALF], wide[0][0:E, i, 0:HALF])\
                            .then_inc(s["gates_copied"], 1)
                    over_experts(act, act_expert)
                    act.wait_ge(s["y_added"], U * E)
                    for i in range(2):
                        nc.scalar.copy(y_t[:, HALF * i:HALF * i + HALF], wide[1][:, i, 0:HALF])\
                            .then_inc(s["y_copied"], 1)

                @block.vector
                def _(dve):
                    def link(ins):
                        chain[0] += 1
                        ins.then_inc(s["router_step"], 1)
                        dve.wait_ge(s["router_step"], chain[0])

                    def first_of(eq, best, tie_of, to):
                        link(nc.vector.tensor_tensor(lg[:, eq, :, :], lg[:, eq, :, :],
                                                     tie[:, None, :].broadcast_to([TR, T, E]), ALU.mult))
                        link(nc.vector.tensor_reduce(out=ls[:, best, :], in_=lg[:, eq, :, :], axis=AX, op=ALU.max))
                        link(nc.vector.tensor_tensor(lg[:, to, :, :], lg[:, eq, :, :], over_tokens(ls[:, best, :]),
                                                     ALU.is_equal))

                    if L == 0:
                        norm_vector(dve, q0, x_sb, xn, False)
                    else:
                        norm_vector(dve, q0, x_sb, resid, False)
                        dve.wait_ge(q0["normed"], T)
                        norm_vector(dve, q1, resid, xn, True)
                    dve.wait_ge(s["logits_ready"], 1)
                    logits = wide[1][0:TR, 0, 0:T * E].rearrange("r (t e) -> r t e", t=T)
                    if L == 0:
                        link(nc.vector.tensor_tensor(lg[:, 0, :, :], logits,
                                                     b_r[:, None, :].broadcast_to([TR, T, E]), ALU.add))
                    else:
                        link(nc.vector.tensor_copy(lg[:, 0, :, :], logits))
                    link(nc.vector.tensor_reduce(out=ls[:, 0, :], in_=lg[:, 0, :, :], axis=AX, op=ALU.max))
                    link(nc.vector.tensor_tensor(lg[:, 1, :, :], lg[:, 0, :, :], over_tokens(ls[:, 0, :]),
                                                 ALU.subtract))
                    dve.wait_ge(s["exp_ready"], 1)
                    link(nc.vector.tensor_reduce(out=ls[:, 1, :], in_=lg[:, 2, :, :], axis=AX, op=ALU.add))
                    link(nc.vector.reciprocal(ls[:, 2, :], ls[:, 1, :]))
                    if L == 0:
                        link(nc.vector.tensor_tensor(lg[:, 3, :, :], lg[:, 0, :, :], over_tokens(ls[:, 0, :]),
                                                     ALU.is_equal))
                        first_of(3, 3, tie, 4)
                        nc.vector.tensor_tensor(lg[:, 7, :, :], lg[:, 4, :, :], over_tokens(ls[:, 2, :]),
                                                ALU.mult).then_inc(s["gates_ready"], 1)
                    else:
                        link(nc.vector.tensor_tensor(lg[:, 3, :, :], lg[:, 2, :, :], over_tokens(ls[:, 2, :]),
                                                     ALU.mult))
                        link(nc.vector.tensor_reduce(out=ls[:, 3, :], in_=lg[:, 3, :, :], axis=AX, op=ALU.max))
                        link(nc.vector.tensor_tensor(lg[:, 4, :, :], lg[:, 3, :, :], over_tokens(ls[:, 3, :]),
                                                     ALU.is_equal))
                        first_of(4, 4, tie, 5)
                        link(nc.vector.tensor_scalar(lg[:, 6, :, :], lg[:, 5, :, :], -4.0, None, ALU.mult))
                        link(nc.vector.tensor_tensor(lg[:, 3, :, :], lg[:, 3, :, :], lg[:, 6, :, :], ALU.add))
                        link(nc.vector.tensor_reduce(out=ls[:, 5, :], in_=lg[:, 3, :, :], axis=AX, op=ALU.max))
                        link(nc.vector.tensor_tensor(lg[:, 4, :, :], lg[:, 3, :, :], over_tokens(ls[:, 5, :]),
                                                     ALU.is_equal))
                        first_of(4, 4, tie, 6)
                        link(nc.vector.tensor_tensor(ls[:, 6, :], ls[:, 3, :], ls[:, 5, :], ALU.add))
                        link(nc.vector.tensor_scalar(ls[:, 6, :], ls[:, 6, :], 1e-9, None, ALU.add))
                        link(nc.vector.reciprocal(ls[:, 7, :], ls[:, 6, :]))
                        link(nc.vector.tensor_tensor(ls[:, 3, :], ls[:, 3, :], ls[:, 7, :], ALU.mult))
                        link(nc.vector.tensor_tensor(ls[:, 5, :], ls[:, 5, :], ls[:, 7, :], ALU.mult))
                        link(nc.vector.tensor_tensor(lg[:, 5, :, :], lg[:, 5, :, :], over_tokens(ls[:, 3, :]),
                                                     ALU.mult))
                        link(nc.vector.tensor_tensor(lg[:, 6, :, :], lg[:, 6, :, :], over_tokens(ls[:, 5, :]),
                                                     ALU.mult))
                        nc.vector.tensor_tensor(lg[:, 7, :, :], lg[:, 5, :, :], lg[:, 6, :, :], ALU.add)\
                            .then_inc(s["gates_ready"], 1)
                    over_experts(dve, dve_expert)
                    for i in range(2):
                        dve.wait_ge(s["y_turned"], 4 * i + 4)
                        y = wide[0][0:TR, i, :]
                        v = x_sb[:, 4 * i:4 * i + 4, :].rearrange("r t d -> r (t d)")
                        if L == 1:
                            r = resid[:, 4 * i:4 * i + 4, :].rearrange("r t d -> r (t d)")
                            link(nc.vector.tensor_tensor(r, y, r, ALU.add))
                            y = r
                        nc.vector.scalar_tensor_tensor(v, y, tg[0:TR, 2 + L:3 + L], v, ALU.mult, ALU.add)\
                            .then_inc(s["x_updated"], 1)
                    dve.wait_ge(s["x_updated"], 2)

        attention(0)
        experts(0)
        nc.all_engine_barrier()
        nc.clear_and_free_semaphores(made)
        nc.all_engine_barrier()
        attention(1)
        experts(1)


def kernel(x, ctx_1024, mask_BxSxS2_ff0, mask_SxS2_fk0, g_xattn, g_ffn, L0_xattn_Wq, L0_xattn_bq, L0_xattn_Wk,
           L0_xattn_bk, L0_xattn_Wv, L0_xattn_bv, L0_ffn_W1, L0_ffn_b1, L0_ffn_W2, L0_ffn_b2, L0_ffn_Wr, L0_ffn_br,
           L1_xattn_Wq, L1_xattn_Wkv, L1_xattn_Wout, L1_ffn_gamma, L1_ffn_beta, L1_ffn_Wg, L1_ffn_W1, L1_ffn_b1,
           L1_ffn_W2, L1_ffn_b2):
    import numpy as np
    import concourse.bacc as bacc
    from concourse.bass_utils import run_bass_kernel_spmd

    def by_pair(w):
        return np.asarray(w).reshape(PAIRS, 2, A, -1).transpose(1, 2, 0, 3).reshape(D, -1)

    def turned(w):
        return np.ascontiguousarray(np.asarray(w).T)

    def row(v):
        return np.asarray(v).reshape(1, -1)

    def chunks(v):
        return np.asarray(v).reshape(E, FC, P).transpose(0, 2, 1)

    def chunked_rows(w):
        return np.asarray(w).reshape(E, FC, P, D).transpose(0, 2, 1, 3)

    wkv = np.asarray(L1_xattn_Wkv)
    arrays = {
        "x": np.asarray(x).reshape(NTOK, D),
        "ctx_t": np.asarray(ctx_1024).transpose(0, 2, 1),
        "mask0": mask_BxSxS2_ff0, "mask1": mask_SxS2_fk0,
        "gates_in": row(np.concatenate([np.asarray(g_xattn), np.asarray(g_ffn)])),
        "ident_in": np.eye(P, dtype=np.float32),
        "tie_in": row(np.arange(E, 0, -1, dtype=np.float32)),
        "wq0": turned(by_pair(L0_xattn_Wq)), "bq0": by_pair(L0_xattn_bq),
        "wk0": turned(by_pair(L0_xattn_Wk)),
        "bk0": np.concatenate([by_pair(L0_xattn_bk), np.zeros((D, 1), np.float32)], axis=1),
        "wv0": turned(L0_xattn_Wv), "bv0": row(L0_xattn_bv),
        "wq1": turned(by_pair(L1_xattn_Wq)), "wk1": turned(by_pair(wkv[:D])), "wv1": turned(wkv[D:]),
        "wo1": turned(L1_xattn_Wout),
        "fw1_0": L0_ffn_W1, "fb1_0": chunks(L0_ffn_b1), "fw2_0": chunked_rows(L0_ffn_W2), "fb2_0": L0_ffn_b2,
        "wr0": L0_ffn_Wr, "br0": row(L0_ffn_br),
        "gamma": row(L1_ffn_gamma), "beta": row(L1_ffn_beta),
        "fw1_1": L1_ffn_W1, "fb1_1": chunks(L1_ffn_b1), "fw2_1": chunked_rows(L1_ffn_W2), "fb2_1": L1_ffn_b2,
        "wr1": turned(L1_ffn_Wg),
    }
    nc = bacc.Bacc("TRN2", target_bir_lowering=False, num_devices=1)
    feeds, args = {}, {}
    for name, a in arrays.items():
        a = np.ascontiguousarray(a)
        feeds[f"in_{name}"] = a
        args[name] = nc.dram_tensor(f"in_{name}", a.shape, mybir.dt.from_np(a.dtype), kind="ExternalInput").ap()
    args["out"] = nc.dram_tensor("out_x", (NTOK, D), F32, kind="ExternalOutput").ap()
    build(nc, **args)
    got = run_bass_kernel_spmd(nc, [feeds], core_ids=[0])
    return got.results[0]["out_x"].reshape(B, S, D)
```
